# Optimizing a Trainium2 kernel written in Bass

```python
import numpy as np
import jax
import jax.numpy as jnp

def _softmax(x, axis=-1):
    return jax.nn.softmax(x, axis=axis)

def _gelu(x):
    return jax.nn.gelu(x, approximate=True)

def _silu(x):
    return jax.nn.silu(x)

def _sigmoid(x):
    return jax.nn.sigmoid(x)

def _layernorm(x, axis=-1, eps=1e-05):
    m = jnp.mean(x, axis=axis, keepdims=True)
    v = jnp.var(x, axis=axis, keepdims=True)
    return (x - m) / jnp.sqrt(v + eps)

def _scatter_add(tgt, idx, src, axis=0):
    return tgt.at[idx].add(src)

def _segment_sum(src, seg, n):
    return jax.ops.segment_sum(src, seg, n)
kernel_name = 'mk_xattn_ffn_d1_seqx_r2_e643cb'

def setup_inputs(seed: int=0):
    np.random.seed(seed)
    _w = jnp.asarray

    def _rec_inputs():
        import jax
        import jax.numpy as jnp
        _rk = jax.random.key(seed)
        x = -1.394e-06 + 0.9999 * jax.random.normal(jax.random.fold_in(_rk, 1), (16, 512, 512), jnp.float32)
        _lenS = 512 - jax.random.randint(jax.random.fold_in(_rk, 7), (16,), 0, max(1, 512 // 4) + 1, jnp.int32)
        _lenS2 = 77 - jax.random.randint(jax.random.fold_in(_rk, 8), (16,), 0, max(1, 77 // 4) + 1, jnp.int32)
        _ctx_1024P = jax.random.normal(jax.random.fold_in(_rk, 11), (16, 16, 512), jnp.float32)
        _ctx_1024c = jax.random.dirichlet(jax.random.fold_in(_rk, 511), 0.3 * jnp.ones((16,), jnp.float32), (16, 77))
        _ctx_1024t = jnp.einsum('bsk,bkd->bsd', _ctx_1024c, _ctx_1024P)
        _ctx_1024t = _ctx_1024t * jax.lax.rsqrt(jnp.mean(jnp.square(_ctx_1024t)) + 1e-12) * 0.953939
        ctx_1024 = 7.22013e-05 + 1.00017 * (_ctx_1024t + 0.3 * jax.random.normal(jax.random.fold_in(_rk, 611), (16, 77, 512), jnp.float32))
        return (x, ctx_1024)
    x, ctx_1024 = _rec_inputs()

    def _L0_xattn_setup():
        import jax, jax.numpy as jnp
        import numpy as np
        L_IN, L_OUT = (1024, 512)
        D_IN, D_OUT, D_POS = (512, 512, 128)
        B = 4
        EPS = 1e-05

        def _layernorm(x, g, b):
            m = jnp.mean(x, axis=-1, keepdims=True)
            v = jnp.mean(jnp.square(x - m), axis=-1, keepdims=True)
            return (x - m) * jax.lax.rsqrt(v + EPS) * g + b

        def _ffn(x, g, be, W1, b1, W2, b2):
            y = _layernorm(x, g, be)
            y = jax.nn.silu(y @ W1 + b1)
            y = y @ W2 + b2
            return y + x
        key = jax.random.key(seed)
        ks = jax.random.split(key, 24)
        s = lambda k, shp, sc=0.02: jax.random.normal(k, shp, dtype=jnp.float32) * sc
        d = {'z': jax.random.normal(ks[0], (B, L_IN, D_IN), dtype=jnp.float32), 'x': jax.random.normal(ks[1], (B, L_OUT, D_OUT), dtype=jnp.float32), 'pe': jax.random.normal(ks[2], (L_IN, D_POS), dtype=jnp.float32), 'W_in': s(ks[3], (D_IN, D_OUT)), 'b_in': jnp.zeros((D_OUT,), jnp.float32), 'g_ln': jnp.ones((D_OUT,), jnp.float32), 'beta_ln': jnp.zeros((D_OUT,), jnp.float32), 'Wp1': s(ks[4], (D_POS, D_POS + D_OUT)), 'bp1': jnp.zeros((D_POS + D_OUT,), jnp.float32), 'Wp2': s(ks[5], (D_POS + D_OUT, D_OUT)), 'bp2': jnp.zeros((D_OUT,), jnp.float32), 'a': jax.random.normal(ks[6], (1,), dtype=jnp.float32), 'g1': jnp.ones((D_OUT,), jnp.float32), 'be1': jnp.zeros((D_OUT,), jnp.float32), 'W1a': s(ks[7], (D_OUT, 2 * D_OUT)), 'b1a': jnp.zeros((2 * D_OUT,), jnp.float32), 'W1b': s(ks[8], (2 * D_OUT, D_OUT)), 'b1b': jnp.zeros((D_OUT,), jnp.float32), 'g2': jnp.ones((D_OUT,), jnp.float32), 'be2': jnp.zeros((D_OUT,), jnp.float32), 'W2a': s(ks[9], (D_OUT, 2 * D_OUT)), 'b2a': jnp.zeros((2 * D_OUT,), jnp.float32), 'W2b': s(ks[10], (2 * D_OUT, D_OUT)), 'b2b': jnp.zeros((D_OUT,), jnp.float32)}
        return d
    _L0_xattn_all = _L0_xattn_setup()
    _L0_xattn_in = {k: v for k, v in _L0_xattn_all.items() if k in ('pe', 'W_in', 'b_in', 'g_ln', 'beta_ln', 'Wp1', 'bp1', 'Wp2', 'bp2', 'a', 'g1', 'be1', 'W1a', 'b1a', 'W1b', 'b1b', 'g2', 'be2', 'W2a', 'b2a', 'W2b', 'b2b')}
    del _L0_xattn_all

    def _L0_ffn_setup():
        import jax, jax.numpy as jnp
        import numpy as np
        CAPACITY_FACTOR = 0.5
        key = jax.random.key(seed)
        ks = jax.random.split(key, 5)
        B, S, D, F = (4, 2048, 512, 2048)
        scale_in = 1.0 / np.sqrt(D)
        scale_ff = 1.0 / np.sqrt(F)
        return {'hidden_states': jax.random.normal(ks[0], (B, S, D), dtype=jnp.float32), 'w_router': jax.random.normal(ks[1], (D,), dtype=jnp.float32) * scale_in, 'W1': jax.random.normal(ks[2], (D, F), dtype=jnp.float32) * scale_in, 'b1': jnp.zeros((F,), dtype=jnp.float32), 'W2': jax.random.normal(ks[3], (F, D), dtype=jnp.float32) * scale_ff, 'b2': jnp.zeros((D,), dtype=jnp.float32)}
    _L0_ffn_all = _L0_ffn_setup()
    _L0_ffn_in = {k: v for k, v in _L0_ffn_all.items() if k in ('w_router', 'W1', 'b1', 'W2', 'b2')}
    del _L0_ffn_all
    return {'x': x, 'ctx_1024': ctx_1024, 'L0_xattn_pe': _L0_xattn_in['pe'], 'L0_xattn_W_in': _L0_xattn_in['W_in'], 'L0_xattn_b_in': _L0_xattn_in['b_in'], 'L0_xattn_g_ln': _L0_xattn_in['g_ln'], 'L0_xattn_beta_ln': _L0_xattn_in['beta_ln'], 'L0_xattn_Wp1': _L0_xattn_in['Wp1'], 'L0_xattn_bp1': _L0_xattn_in['bp1'], 'L0_xattn_Wp2': _L0_xattn_in['Wp2'], 'L0_xattn_bp2': _L0_xattn_in['bp2'], 'L0_xattn_a': _L0_xattn_in['a'], 'L0_xattn_g1': _L0_xattn_in['g1'], 'L0_xattn_be1': _L0_xattn_in['be1'], 'L0_xattn_W1a': _L0_xattn_in['W1a'], 'L0_xattn_b1a': _L0_xattn_in['b1a'], 'L0_xattn_W1b': _L0_xattn_in['W1b'], 'L0_xattn_b1b': _L0_xattn_in['b1b'], 'L0_xattn_g2': _L0_xattn_in['g2'], 'L0_xattn_be2': _L0_xattn_in['be2'], 'L0_xattn_W2a': _L0_xattn_in['W2a'], 'L0_xattn_b2a': _L0_xattn_in['b2a'], 'L0_xattn_W2b': _L0_xattn_in['W2b'], 'L0_xattn_b2b': _L0_xattn_in['b2b'], 'L0_ffn_w_router': _L0_ffn_in['w_router'], 'L0_ffn_W1': _L0_ffn_in['W1'], 'L0_ffn_b1': _L0_ffn_in['b1'], 'L0_ffn_W2': _L0_ffn_in['W2'], 'L0_ffn_b2': _L0_ffn_in['b2']}

def reference(x, ctx_1024, L0_xattn_pe, L0_xattn_W_in, L0_xattn_b_in, L0_xattn_g_ln, L0_xattn_beta_ln, L0_xattn_Wp1, L0_xattn_bp1, L0_xattn_Wp2, L0_xattn_bp2, L0_xattn_a, L0_xattn_g1, L0_xattn_be1, L0_xattn_W1a, L0_xattn_b1a, L0_xattn_W1b, L0_xattn_b1b, L0_xattn_g2, L0_xattn_be2, L0_xattn_W2a, L0_xattn_b2a, L0_xattn_W2b, L0_xattn_b2b, L0_ffn_w_router, L0_ffn_W1, L0_ffn_b1, L0_ffn_W2, L0_ffn_b2):
    import jax
    import jax.numpy as jnp

    def _L0_xattn_ref(z, x, pe, W_in, b_in, g_ln, beta_ln, Wp1, bp1, Wp2, bp2, a, g1, be1, W1a, b1a, W1b, b1b, g2, be2, W2a, b2a, W2b, b2b):
        import jax, jax.numpy as jnp
        import numpy as np
        L_IN, L_OUT = (1024, 512)
        D_IN, D_OUT, D_POS = (512, 512, 128)
        B = 4
        EPS = 1e-05

        def _layernorm(x, g, b):
            m = jnp.mean(x, axis=-1, keepdims=True)
            v = jnp.mean(jnp.square(x - m), axis=-1, keepdims=True)
            return (x - m) * jax.lax.rsqrt(v + EPS) * g + b

        def _ffn(x, g, be, W1, b1, W2, b2):
            y = _layernorm(x, g, be)
            y = jax.nn.silu(y @ W1 + b1)
            y = y @ W2 + b2
            return y + x
        L = L_IN
        z = z @ W_in + b_in
        zn = _layernorm(z, g_ln, beta_ln)
        fz = jnp.fft.rfft(zn, n=2 * L, axis=1)
        h = jax.nn.silu(pe @ Wp1 + bp1) @ Wp2 + bp2
        window = jnp.exp(-jnp.arange(L, dtype=jnp.float32) * jnp.exp(a[0]))
        wfh = jnp.fft.rfft(window[:, None] * h, n=2 * L, axis=0)
        cwhz = jnp.fft.irfft(wfh[None] * fz, n=2 * L, axis=1)[:, :L]
        idx = jnp.arange(L_OUT) * L // L_OUT
        dcwhz = cwhz[:, idx]
        xr = _ffn(x, g1, be1, W1a, b1a, W1b, b1b)
        y = xr * dcwhz
        y = _ffn(y, g2, be2, W2a, b2a, W2b, b2b)
        return y

    def _L0_ffn_ref(hidden_states, w_router, W1, b1, W2, b2):
        import jax, jax.numpy as jnp
        import numpy as np
        CAPACITY_FACTOR = 0.5
        'Mixture-of-Depths block: route top-k tokens through an FFN inner block,\n            scatter back with sigmoid router weights; bypassed tokens pass through.'
        B, S, D = hidden_states.shape
        k = int(S * CAPACITY_FACTOR)
        scores = jnp.einsum('bsd,d->bs', hidden_states, w_router)
        top_scores, top_idx = jax.lax.top_k(scores, k)
        weights = jax.nn.sigmoid(top_scores)
        selected = jnp.take_along_axis(hidden_states, top_idx[:, :, None], axis=1)
        h = jax.nn.gelu(jnp.einsum('bkd,df->bkf', selected, W1) + b1)
        processed = jnp.einsum('bkf,fd->bkd', h, W2) + b2
        update = weights[:, :, None] * processed

        def scatter_one(xb, ib, ub):
            return xb.at[ib].add(ub)
        output = jax.vmap(scatter_one)(hidden_states, top_idx, update)
        return output
    x = x + _L0_xattn_ref(ctx_1024, _layernorm(x, axis=-1), L0_xattn_pe, L0_xattn_W_in, L0_xattn_b_in, L0_xattn_g_ln, L0_xattn_beta_ln, L0_xattn_Wp1, L0_xattn_bp1, L0_xattn_Wp2, L0_xattn_bp2, L0_xattn_a, L0_xattn_g1, L0_xattn_be1, L0_xattn_W1a, L0_xattn_b1a, L0_xattn_W1b, L0_xattn_b1b, L0_xattn_g2, L0_xattn_be2, L0_xattn_W2a, L0_xattn_b2a, L0_xattn_W2b, L0_xattn_b2b)
    x = x + _L0_ffn_ref(_layernorm(x, axis=-1), L0_ffn_w_router, L0_ffn_W1, L0_ffn_b1, L0_ffn_W2, L0_ffn_b2)
    return x

_drawn_inputs = setup_inputs


def setup_inputs(seed=0):
    import zlib

    import numpy as np

    out = dict(_drawn_inputs(seed))
    spreads = {'L0_xattn_b_in': (0.0, 0.585),
     'L0_xattn_g_ln': (1.0, 0.6),
     'L0_xattn_beta_ln': (0.0, 0.8),
     'L0_xattn_bp1': (0.0, 0.609),
     'L0_xattn_bp2': (0.0, 0.1),
     'L0_xattn_g1': (1.0, 0.6),
     'L0_xattn_be1': (0.0, 0.8),
     'L0_xattn_b1a': (0.0, 0.8),
     'L0_xattn_b1b': (0.0, 0.8),
     'L0_xattn_g2': (1.0, 0.6),
     'L0_xattn_be2': (0.0, 0.565),
     'L0_xattn_b2a': (0.0, 0.269),
     'L0_xattn_b2b': (0.0, 0.1),
     'L0_ffn_b1': (0.0, 0.511),
     'L0_ffn_b2': (0.0, 0.357)}
    factors = {'L0_xattn_W1a': 5.912, 'L0_xattn_W1b': 5.598}
    for name, (base, spread) in spreads.items():
        noise = np.random.default_rng([zlib.crc32(name.encode()), seed]).standard_normal(out[name].shape)
        drawn = base * np.exp(spread * noise) if base else spread * noise
        out[name] = jnp.asarray(drawn.astype(out[name].dtype))
    for name, factor in factors.items():
        out[name] = (out[name] * factor).astype(out[name].dtype)
    return out
```

```python
from contextlib import ExitStack

import concourse.bass as bass
from concourse import mybir

ALU = mybir.AluOpType
ACT = mybir.ActivationFunctionType
F32 = mybir.dt.float32
F32R = mybir.dt.float32r
I32 = mybir.dt.int32
U32 = mybir.dt.uint32

P = 128
EPS = 1e-5
D = 512
KC = D // P
NB, S = 16, 512
NT = S // P
F = 1024
NF = F // P
FM = 2048
NFM = FM // P
CTX = 77
ZROWS = NB * CTX
ZT = -(-ZROWS // P)
L = 1024
DP = 128
H = DP + D
KH = H // P
TOP = S // 2
HALO = (CTX - 1) // 2
EDGES = [0, 86, 172, 256, 342, 428]
NP = len(EDGES)
PIECES = [(0, 1), (1, 2), (3, 4), (4, 5)]
PAD = 2 * HALO + 2
GROWS = 2 * (EDGES[-1] + P) + PAD
DH = D // 2


class LayerNorm:

    def __init__(self, nc, sb, sem, name, const):
        self.nc, self.const = nc, const
        self.stats = sb(name + "_stats", [P, NT, 6])
        self.mv = sb(name + "_mv", [P, NT, 2])
        self.veps = sb(name + "_veps", [P, NT])
        self.rstd = sb(name + "_rstd", [P, NT])
        self.s_stats = sem(name + "_stats_done")
        self.s_seen = sem(name + "_stats_seen")
        self.s_mv = sem(name + "_mean_var_done")
        self.s_veps = sem(name + "_veps_done")
        self.s_rstd = sem(name + "_rstd_done")

    def dve(self, dve, x, n, used=None):
        for t in range(NT):
            self.nc.vector.bn_stats(self.stats[:, t, :], x[:, t, :]).then_inc(self.s_stats, 1)
        dve.wait_ge(self.s_stats, NT * n + NT)
        dve.sem_inc(self.s_seen, 1)
        for t in range(NT):
            self.nc.vector.bn_aggr(self.mv[:, t, :], self.stats[:, t, :]).then_inc(self.s_mv, 1)

    def pool(self, pool, n):
        pool.wait_ge(self.s_mv, NT * n + NT)
        self.nc.gpsimd.tensor_tensor(self.veps[:, :], self.mv[:, :, 1], self.const[:, 1, :],
                                     ALU.add).then_inc(self.s_veps, 1)
        pool.wait_ge(self.s_veps, n + 1)
        self.nc.gpsimd.tensor_tensor(self.rstd[:, :], self.veps[:, :], self.const[:, 0, :],
                                     ALU.pow).then_inc(self.s_rstd, 1)

    def apply(self, out, x, t):
        return self.nc.vector.tensor_scalar(out, x, self.mv[:, t, 0:1], self.rstd[:, t:t + 1],
                                            ALU.subtract, ALU.mult)


def bcast(vec, n=P):
    return vec.rearrange("(a n) -> a n", a=1).broadcast_to([n, vec.shape[0]])


def split_weights(nc, name, jobs, bias=None):
    with ExitStack() as ctx:
        ctx.enter_context(nc.cleanup_on_exit())
        def sb(n, shape, dt=F32):
            return ctx.enter_context(nc.sbuf_tensor(f"{name}_{n}", shape, dt))

        def sem(n):
            return nc.alloc_semaphore(name=f"{name}_{n}")

        chunks = [(j, k) for j, job in enumerate(jobs) for k in range(job[1].shape[1])]
        R = 4
        width = max(job[1].shape[2] for job in jobs)
        ring = sb("ring", [P, R, width])
        cols = sb("cols", [P, 3, 16])
        s_in = [sem(f"chunk_loaded{r}") for r in range(R)]
        s_cols = sem("cols_loaded")
        s_hi = sem("hi_done")
        s_lo = sem("lo_done")
        s_bias = sem("bias_product")
        s_out = sem("bias_done")
        scaled = [j for j, job in enumerate(jobs) if job[3] is not None]
        KB = jobs[0][1].shape[1]
        NBI = jobs[0][1].shape[2] // P
        if bias is not None:
            ps = ctx.enter_context(nc.psum_tensor(f"{name}_ps", [P, 512], F32))
        block = ctx.enter_context(nc.Block())
        ncols = 16 * (len(scaled) + (2 if bias is not None else 0))

        @block.sync
        def _(sp):
            if scaled:
                sp.dma_start(cols[:, 0, 0:KB], jobs[scaled[0]][3])\
                  .then_inc(s_cols, 16)
            if bias is not None:
                sp.dma_start(cols[:, 1, 0:KB], bias[0]).then_inc(s_cols, 16)
                sp.dma_start(cols[:, 2, 0:NBI], bias[1]).then_inc(s_cols, 16)
            for n, (j, k) in enumerate(chunks):
                w, hi = jobs[j][0], jobs[j][1]
                if n >= R:
                    sp.wait_ge(s_lo, n - R + 1)
                    if bias is not None and n - R < KB:
                        sp.wait_ge(s_bias, 1)
                sp.dma_start(ring[:, n % R, 0:hi.shape[2]], w[k * P:(k + 1) * P, :]).then_inc(s_in[n % R], 16)

        @block.scalar
        def _(act):
            if ncols:
                act.wait_ge(s_cols, ncols)
            for n, (j, k) in enumerate(chunks):
                _, hi, lo, scale = jobs[j]
                act.wait_ge(s_in[n % R], 16 * (n // R + 1))
                src = ring[:, n % R, 0:hi.shape[2]]
                if scale is None:
                    nc.scalar.activation(hi[:, k, :], src, ACT.Copy).then_inc(s_hi, 1)
                else:
                    nc.scalar.activation(hi[:, k, :], src, ACT.Copy, scale=cols[:, 0, k:k + 1]).then_inc(s_hi, 1)

        @block.vector
        def _(dve):
            if ncols:
                dve.wait_ge(s_cols, ncols)
            for n, (j, k) in enumerate(chunks):
                _, hi, lo, scale = jobs[j]
                dve.wait_ge(s_in[n % R], 16 * (n // R + 1))
                dve.wait_ge(s_hi, n + 1)
                src = ring[:, n % R, 0:hi.shape[2]]
                h = hi[:, k, :].bitcast(F32)
                if scale is None:
                    nc.vector.tensor_tensor(lo[:, k, :], src, h, ALU.subtract).then_inc(s_lo, 1)
                else:
                    nc.vector.scalar_tensor_tensor(lo[:, k, :], src, cols[:, 0, k:k + 1], h,
                                                   ALU.mult, ALU.subtract).then_inc(s_lo, 1)
                if bias is not None and n == KB - 1:
                    dve.wait_ge(s_bias, 1)
                    nc.vector.tensor_tensor(bias[2][:, :], ps[:, 0:NBI], cols[:, 2, 0:NBI],
                                            ALU.add).then_inc(s_out, 1)

        @block.tensor
        def _(pe):
            if bias is not None:
                pe.wait_ge(s_cols, ncols)
                for k in range(KB):
                    pe.wait_ge(s_in[k % R], 16)
                for f in range(NBI):
                    for k in range(KB):
                        last = pe.matmul(ps[:, f:f + 1], ring[:, k, f * P:(f + 1) * P], cols[:, 1, k:k + 1],
                                         start=(k == 0), stop=(k == KB - 1))
                last.then_inc(s_bias, 1)


def passes(a_hi, a_lo, b_hi, b_lo):
    return ((a_hi, b_hi), (a_lo, b_hi), (a_hi, b_lo))


def product(pe, out, terms):
    pairs = [p for t in terms for p in passes(*t)]
    for n, (a, b) in enumerate(pairs):
        last = pe.matmul(out, a, b, start=(n == 0), stop=(n == len(pairs) - 1))
    return last


def filters(nc, T, G1, G2, gpad):
    with ExitStack() as ctx:
        ctx.enter_context(nc.cleanup_on_exit())
        def sb(n, shape, dt=F32):
            return ctx.enter_context(nc.sbuf_tensor(f"flt_{n}", shape, dt))

        def sem(n):
            return nc.alloc_semaphore(name=f"flt_{n}")

        wp1 = [sb(f"wp1{h}", [P, 1, H], F32R) for h in "hl"]
        wp2 = [sb(f"wp2{h}", [P, KH, D], F32R) for h in "hl"]
        pet = [sb(f"pet{h}", [P, 1, L], F32R) for h in "hl"]
        dft = [sb(f"dft{h}", [P, 1, P], F32R) for h in "hl"]
        split_weights(nc, "fw", [(T["Wp1"], *wp1, None), (T["Wp2"], *wp2, None), (T["peT"], *pet, None),
                                 (T["dft_g"], *dft, None)])
        hp = [sb(f"hp{h}", [P, KH, L], F32R) for h in "hl"]
        bp1 = sb("bp1", [P, KH])
        bp2 = sb("bp2", [P, D])
        negl = sb("negl", [P, L // P])
        a_col = sb("a", [P, 1])
        ea = sb("ea", [P, 1])
        arg = sb("arg", [P, L // P])
        win = sb("win", [P, L // P])
        tmp = sb("tmp", [P, 2, D])
        wh = sb("wh", [P, 2, D])
        zero = sb("zero", [P, D])
        gin = sb("gin", [P, 2, D])
        gh = sb("gh", [P, 2, D], F32R)
        gl = sb("gl", [P, 2, D], F32R)
        ps = [ctx.enter_context(nc.psum_tensor(f"flt_ps{n}", [P, D], F32)) for n in range(2)]
        s_in = sem("vectors_loaded")
        s_ea, s_arg, s_win = sem("exp_a_done"), sem("arg_done"), sem("window_done")
        s_hid, s_silu, s_hhi, s_hlo = sem("hidden_done"), sem("silu_done"), sem("hidden_hi_done"), sem("hidden_lo_done")
        s_row, s_bias, s_wh = sem("filter_done"), sem("filter_bias_added"), sem("windowed_done")
        s_st = [sem(f"windowed_stored{n}") for n in range(2)]
        s_zero, s_pad = sem("zero_done"), sem("pads_stored")
        s_gin = [sem(f"piece_loaded{n}") for n in range(2)]
        s_ghi, s_glo, s_spec, s_g1, s_g2 = (sem("piece_hi_done"), sem("piece_lo_done"), sem("spectrum_done"),
                                            sem("g1_done"), sem("g2_done"))
        block = ctx.enter_context(nc.Block())
        HID = [(f, m) for f in range(KH) for m in range(L // 512)]
        LT = L // P
        PC = [(ph, p) for p in range(NP) for ph in range(2)]

        @block.sync
        def _(sp):
            sp.dma_start(bp1[:, :], T["bp1"]).then_inc(s_in, 16)
            sp.dma_start(bp2[:, :], bcast(T["bp2"])).then_inc(s_in, 16)
            sp.dma_start(negl[:, :], T["negl"]).then_inc(s_in, 16)
            sp.dma_start(a_col[:, :], bcast(T["a"])).then_inc(s_in, 16)
            sp.wait_ge(s_zero, 1)
            sp.dma_start(gpad[0:PAD, :], zero[0:PAD, :]).then_inc(s_pad, 16)
            tail = GROWS - PAD - L
            sp.dma_start(gpad[PAD + L:GROWS, :], zero[0:tail, :]).then_inc(s_pad, 16)
            for m in range(LT):
                sp.wait_ge(s_wh, m + 1)
                sp.dma_start(gpad[PAD + m * P:PAD + (m + 1) * P, :], wh[:, m % 2, :]).then_inc(s_st[m % 2], 16)
            sp.wait_ge(s_pad, 32)
            for n in range(2):
                sp.wait_ge(s_st[n], 16 * (LT // 2))
            for n, (ph, p) in enumerate(PC):
                if n >= 2:
                    sp.wait_ge(s_glo, n - 1)
                r = 2 * EDGES[p] + 2 - ph
                sp.dma_start(gin[:, n % 2, :], gpad[r:r + 2 * P - 1:2, :]).then_inc(s_gin[n % 2], 16)
            sp.wait_ge(s_g1, 2 * NP)
            sp.dma_start(G2[0:64, :, :, :], G1[64:P, :, :, :]).then_inc(s_g2, 16)
            sp.dma_start(G2[64:P, :, :, :], G1[0:64, :, :, :]).then_inc(s_g2, 16)
            sp.wait_ge(s_g2, 32)

        @block.scalar
        def _(act):
            act.wait_ge(s_in, 64)
            nc.scalar.activation(ea[:, :], a_col[:, :], ACT.Exp).then_inc(s_ea, 1)
            act.wait_ge(s_arg, 1)
            nc.scalar.activation(win[:, :], arg[:, :], ACT.Exp).then_inc(s_win, 1)
            for n, (f, m) in enumerate(HID):
                act.wait_ge(s_hid, n + 1)
                nc.scalar.activation(ps[n % 2][:, :], ps[n % 2][:, :], ACT.Silu,
                                     bias=bp1[:, f:f + 1]).then_inc(s_silu, 1)
                act.wait_ge(s_silu, n + 1)
                nc.scalar.activation(hp[0][:, f, m * 512:(m + 1) * 512], ps[n % 2][:, :], ACT.Copy)\
                  .then_inc(s_hhi, 1)
            act.wait_ge(s_win, 1)
            for m in range(LT):
                act.wait_ge(s_bias, m + 1)
                if m >= 2:
                    act.wait_ge(s_st[m % 2], 16 * (m // 2))
                nc.scalar.activation(wh[:, m % 2, :], tmp[:, m % 2, :], ACT.Copy, scale=win[:, m:m + 1])\
                  .then_inc(s_wh, 1)
            for n in range(2 * NP):
                act.wait_ge(s_gin[n % 2], 16 * (n // 2 + 1))
                if n >= 2:
                    act.wait_ge(s_spec, n - 1)
                nc.scalar.activation(gh[:, n % 2, :], gin[:, n % 2, :], ACT.Copy).then_inc(s_ghi, 1)

        def g1_copy(dve, n):
            ph, p = PC[n]
            dve.wait_ge(s_spec, n + 1)
            nc.vector.tensor_copy(G1[:, ph, p, :], ps[n % 2][:, :]).then_inc(s_g1, 1)

        @block.vector
        def _(dve):
            nc.vector.memset(zero[:, :], 0.0).then_inc(s_zero, 1)
            dve.wait_ge(s_in, 64)
            dve.wait_ge(s_ea, 1)
            nc.vector.tensor_scalar(arg[:, :], negl[:, :], ea[:, 0:1], None, ALU.mult).then_inc(s_arg, 1)
            for n, (f, m) in enumerate(HID):
                dve.wait_ge(s_hhi, n + 1)
                nc.vector.tensor_tensor(hp[1][:, f, m * 512:(m + 1) * 512], ps[n % 2][:, :],
                                        hp[0][:, f, m * 512:(m + 1) * 512].bitcast(F32),
                                        ALU.subtract).then_inc(s_hlo, 1)
            for m in range(LT):
                dve.wait_ge(s_row, m + 1)
                if m >= 2:
                    dve.wait_ge(s_wh, m - 1)
                nc.vector.tensor_tensor(tmp[:, m % 2, :], ps[m % 2][:, :], bp2[:, :], ALU.add)\
                  .then_inc(s_bias, 1)
            for n, (ph, p) in enumerate(PC):
                dve.wait_ge(s_ghi, n + 1)
                if n >= 2:
                    dve.wait_ge(s_spec, n - 1)
                nc.vector.tensor_tensor(gl[:, n % 2, :], gin[:, n % 2, :], gh[:, n % 2, :].bitcast(F32),
                                        ALU.subtract).then_inc(s_glo, 1)
                if n >= 1:
                    g1_copy(dve, n - 1)
            g1_copy(dve, 2 * NP - 1)

        @block.tensor
        def _(pe):
            for n, (f, m) in enumerate(HID):
                if n >= 2:
                    pe.wait_ge(s_hlo, n - 1)
                cut = slice(m * 512, (m + 1) * 512)
                product(pe, ps[n % 2][:, :], [(wp1[0][:, 0, f * P:(f + 1) * P], wp1[1][:, 0, f * P:(f + 1) * P],
                                               pet[0][:, 0, cut], pet[1][:, 0, cut])]).then_inc(s_hid, 1)
            pe.wait_ge(s_hlo, len(HID))
            for m in range(LT):
                if m >= 2:
                    pe.wait_ge(s_bias, m - 1)
                product(pe, ps[m % 2][:, :], [(hp[0][:, f, m * P:(m + 1) * P], hp[1][:, f, m * P:(m + 1) * P],
                                               wp2[0][:, f, :], wp2[1][:, f, :]) for f in range(KH)])\
                    .then_inc(s_row, 1)
            pe.wait_ge(s_bias, LT)
            for n in range(2 * NP):
                pe.wait_ge(s_glo, n + 1)
                if n >= 2:
                    pe.wait_ge(s_g1, n - 1)
                product(pe, ps[n % 2][:, :], [(dft[0][:, 0, :], dft[1][:, 0, :], gh[:, n % 2, :], gl[:, n % 2, :])])\
                    .then_inc(s_spec, 1)


def context(nc, T, zhi, zlo, const):
    with ExitStack() as ctx:
        ctx.enter_context(nc.cleanup_on_exit())
        def sb(n, shape, dt=F32):
            return ctx.enter_context(nc.sbuf_tensor(f"ctx_{n}", shape, dt))

        def sem(n):
            return nc.alloc_semaphore(name=f"ctx_{n}")

        win = [sb(f"win{h}", [P, KC, D], F32R) for h in "hl"]
        ct = [sb(f"ct{h}", [P, KC, ZROWS], F32R) for h in "hl"]
        split_weights(nc, "cw", [(T["W_in"], *win, None), (T["ctxT"], *ct, None)])
        vec = {n: sb(n, [P, D]) for n in ("b_in", "g_ln", "beta_ln")}
        z = sb("z", [P, 3, D])
        zh = sb("zh", [P, 2, D], F32R)
        zl = sb("zl", [P, 2, D], F32R)
        stats = sb("stats", [P, 2, 6])
        mv = sb("mv", [P, 2, 2])
        veps = sb("veps", [P, 2])
        rstd = sb("rstd", [P, 2])
        ps = [ctx.enter_context(nc.psum_tensor(f"ctx_ps{n}", [P, D], F32)) for n in range(2)]
        s_in, s_mm = sem("vectors_loaded"), sem("z_product_done")
        s_d = sem("z_steps")
        s_veps, s_rstd = sem("veps_done"), sem("rstd_done")
        s_hi, s_lo = sem("z_hi_done"), sem("z_lo_done")
        s_st = [sem(f"z_stored{n}") for n in range(2)]
        block = ctx.enter_context(nc.Block())
        rows = [min(P, ZROWS - n * P) for n in range(ZT)]

        @block.sync
        def _(sp):
            for n in vec:
                sp.dma_start(vec[n][:, :], bcast(T[n])).then_inc(s_in, 16)
            for n in range(ZT):
                sp.wait_ge(s_lo, n + 1)
                r = rows[n]
                sp.dma_start(zhi[n * P:n * P + r, :], zh[0:r, n % 2, :].bitcast(F32)).then_inc(s_st[n % 2], 16)
                sp.dma_start(zlo[n * P:n * P + r, :], zl[0:r, n % 2, :].bitcast(F32)).then_inc(s_st[n % 2], 16)
            for k in range(2):
                sp.wait_ge(s_st[k], 32 * (ZT // 2))

        @block.tensor
        def _(pe):
            for n in range(ZT):
                if n >= 2:
                    pe.wait_ge(s_d, 6 * (n - 2) + 1)
                r, at = rows[n], n * P
                product(pe, ps[n % 2][0:r, :], [(ct[0][:, k, at:at + r], ct[1][:, k, at:at + r],
                                                 win[0][:, k, :], win[1][:, k, :]) for k in range(KC)])\
                    .then_inc(s_mm, 1)

        @block.gpsimd
        def _(pool):
            for n in range(ZT):
                r, k = rows[n], n % 2
                pool.wait_ge(s_d, 6 * n + 3)
                nc.gpsimd.tensor_scalar(veps[0:r, k:k + 1], mv[0:r, k, 1:2], 1.0, EPS, ALU.mult, ALU.add)\
                  .then_inc(s_veps, 1)
                pool.wait_ge(s_veps, n + 1)
                nc.gpsimd.tensor_tensor(rstd[0:r, k:k + 1], veps[0:r, k:k + 1], const[0:r, 0, 0:1], ALU.pow)\
                  .then_inc(s_rstd, 1)

        @block.scalar
        def _(act):
            for n in range(ZT):
                r, k = rows[n], n % 2
                act.wait_ge(s_d, 6 * n + 6)
                if n >= 2:
                    act.wait_ge(s_st[k], 32 * (n // 2))
                nc.scalar.activation(zh[0:r, k, :], z[0:r, 2, :], ACT.Copy).then_inc(s_hi, 1)

        @block.vector
        def _(dve):
            dve.wait_ge(s_in, 48)
            for n in range(ZT):
                r, k = rows[n], n % 2
                c = 6 * n
                dve.wait_ge(s_mm, n + 1)
                nc.vector.tensor_tensor(z[0:r, 0, :], ps[k][0:r, :], vec["b_in"][0:r, :], ALU.add).then_inc(s_d, 1)
                dve.wait_ge(s_d, c + 1)
                nc.vector.bn_stats(stats[0:r, k, :], z[0:r, 0, :]).then_inc(s_d, 1)
                dve.wait_ge(s_d, c + 2)
                nc.vector.bn_aggr(mv[0:r, k, :], stats[0:r, k, :]).then_inc(s_d, 1)
                dve.wait_ge(s_rstd, n + 1)
                dve.wait_ge(s_d, c + 3)
                nc.vector.tensor_scalar(z[0:r, 1, :], z[0:r, 0, :], mv[0:r, k, 0:1], rstd[0:r, k:k + 1],
                                        ALU.subtract, ALU.mult).then_inc(s_d, 1)
                dve.wait_ge(s_d, c + 4)
                nc.vector.tensor_tensor(z[0:r, 0, :], z[0:r, 1, :], vec["g_ln"][0:r, :], ALU.mult).then_inc(s_d, 1)
                dve.wait_ge(s_d, c + 5)
                nc.vector.tensor_tensor(z[0:r, 2, :], z[0:r, 0, :], vec["beta_ln"][0:r, :], ALU.add)\
                  .then_inc(s_d, 1)
                dve.wait_ge(s_d, c + 6)
                dve.wait_ge(s_hi, n + 1)
                if n >= 2:
                    dve.wait_ge(s_st[k], 32 * (n // 2))
                nc.vector.tensor_tensor(zl[0:r, k, :], z[0:r, 2, :], zh[0:r, k, :].bitcast(F32),
                                        ALU.subtract).then_inc(s_lo, 1)


class Ffn:

    def __init__(self, nc, ctx, name, nf, func, w1, w2, b1):
        def sb(n, shape, dt=F32):
            return ctx.enter_context(nc.sbuf_tensor(f"{name}_{n}", shape, dt))

        def sem(n):
            return nc.alloc_semaphore(name=f"{name}_{n}")

        self.nc, self.nf, self.func, self.w1, self.w2, self.b1 = nc, nf, func, w1, w2, b1
        self.xT = [sb(f"xT{h}", [P, KC, 512], F32R) for h in "hl"]
        self.hid = [sb(f"hid{h}", [P, 2, 512], F32R) for h in "hl"]
        self.acc = [ctx.enter_context(nc.psum_tensor(f"{name}_acc{t}", [P, D], F32)) for t in range(NT)]
        self.up = [ctx.enter_context(nc.psum_tensor(f"{name}_up{t}", [P, 512], F32)) for t in range(2)]
        self.side = [ctx.enter_context(nc.psum_tensor(f"{name}_side{t}", [P, 512], F32)) for t in range(2)]
        self.s_up = sem("hidden_product_done")
        self.s_act = sem("hidden_act_done")
        self.s_hi = sem("hidden_hi_done")
        self.s_hid = sem("hidden_split_primed")
        self.s_down = sem("hidden_used_primed")
        self.s_acc = sem("outputs_free_primed")
        self.s_t = sem("transposed")
        self.s_thi = sem("transposed_hi_done")
        self.s_xT = sem("input_ready")

    def prime(self, eng):
        eng.sem_inc(self.s_hid, 2)
        eng.sem_inc(self.s_down, 2)
        eng.sem_inc(self.s_acc, 1)

    def up_product(self, pe, u, f):
        if f == 0:
            pe.wait_ge(self.s_xT, NT * u + NT)
        pe.wait_ge(self.s_hid, self.nf * u + f + 1)
        cut = slice(f * P, (f + 1) * P)
        product(pe, self.up[f % 2][:, :], [(self.w1[0][:, k, cut], self.w1[1][:, k, cut],
                                            self.xT[0][:, k, :], self.xT[1][:, k, :]) for k in range(KC)])\
            .then_inc(self.s_up, 1)

    def down_product(self, pe, u, f):
        if f == 0:
            pe.wait_ge(self.s_acc, u + 1)
        pe.wait_ge(self.s_hid, self.nf * u + f + 3)
        for t in range(NT):
            cut = slice(t * P, (t + 1) * P)
            pairs = passes(self.hid[0][:, f % 2, cut], self.hid[1][:, f % 2, cut],
                           self.w2[0][:, f, :], self.w2[1][:, f, :])
            for n, (a, b) in enumerate(pairs):
                last = pe.matmul(self.acc[t][:, :], a, b, start=(f == 0 and n == 0),
                                 stop=(f == self.nf - 1 and n == 2), skip_group_check=True)
        last.then_inc(self.s_down, 1)

    def transpose(self, pe, src, ident, t):
        for k in range(KC):
            last = pe.transpose(self.side[t % 2][:, k * P:(k + 1) * P], src[:, k * P:(k + 1) * P], ident)
        last.then_inc(self.s_t, 1)

    def activate(self, act, u, f):
        act.wait_ge(self.s_up, self.nf * u + f + 1)
        self.nc.scalar.activation(self.up[f % 2][:, :], self.up[f % 2][:, :], self.func,
                                  bias=self.b1[:, f:f + 1]).then_inc(self.s_act, 1)
        act.wait_ge(self.s_act, self.nf * u + f + 1)
        act.wait_ge(self.s_down, self.nf * u + f + 1)
        self.nc.scalar.activation(self.hid[0][:, f % 2, :], self.up[f % 2][:, :], ACT.Copy)\
            .then_inc(self.s_hi, 1)

    def input_hi(self, act, u, t):
        act.wait_ge(self.s_t, NT * u + t + 1)
        side = self.side[t % 2][:, :].rearrange("p (k n) -> p k n", k=KC)
        self.nc.scalar.activation(self.xT[0][:, :, t * P:(t + 1) * P], side, ACT.Copy).then_inc(self.s_thi, 1)

    def hidden_lo(self, dve, u, f):
        dve.wait_ge(self.s_hi, self.nf * u + f + 1)
        self.nc.vector.tensor_tensor(self.hid[1][:, f % 2, :], self.up[f % 2][:, :],
                                     self.hid[0][:, f % 2, :].bitcast(F32), ALU.subtract)\
            .then_inc(self.s_hid, 1)

    def input_lo(self, dve, u, t):
        dve.wait_ge(self.s_thi, NT * u + t + 1)
        side = self.side[t % 2][:, :].rearrange("p (k n) -> p k n", k=KC)
        cut = slice(t * P, (t + 1) * P)
        self.nc.vector.tensor_tensor(self.xT[1][:, :, cut], side, self.xT[0][:, :, cut].bitcast(F32),
                                     ALU.subtract).then_inc(self.s_xT, 1)


def pairs_loop(eng, body, n):
    with eng.Fori(0, n - 1) as i:
        for par in range(2):
            body(2 * i + par, i, par, False)
    for par in range(2):
        body(2 * (n - 1) + par, n - 1, par, par == 1)


def stage_a(nc, T, G1, G2, zhi, zlo, y_dram, ident, const):
    with ExitStack() as ctx:
        ctx.enter_context(nc.cleanup_on_exit())
        def sb(n, shape, dt=F32):
            return ctx.enter_context(nc.sbuf_tensor(f"a_{n}", shape, dt))

        def sem(n):
            return nc.alloc_semaphore(name=f"a_{n}")

        w1 = [sb(f"w1{h}", [P, KC, F], F32R) for h in "hl"]
        w2 = [sb(f"w2{h}", [P, NF, D], F32R) for h in "hl"]
        b1 = sb("b1", [P, NF])
        fz = [sb(f"fz{h}", [P, 1, 4 * P], F32R) for h in "hl"]
        inv = [sb(f"inv{h}", [P, 1, 4 * P], F32R) for h in "hl"]
        split_weights(nc, "aw", [(T["W1a"], *w1, T["g1"]), (T["W1b"], *w2, None), (T["dft_z"], *fz, None),
                                 (T["dft_inv"], *inv, None)], (T["be1"], T["b1a"], b1))
        ffn = Ffn(nc, ctx, "af", NF, ACT.Silu, w1, w2, b1)
        X = [sb(f"x{p}", [P, NT, D]) for p in range(2)]
        hat = sb("hat", [P, 2, D])
        b2 = sb("b2", [P, D])
        zn = [sb(f"zn{h}", [CTX, D], F32R) for h in "hl"]
        zs = sb("zs", [P, 4, DH])
        pr = [sb(f"pr{h}", [P, NP, D], F32R) for h in "hl"]
        ta = [sb(f"ta{n}", [P, 2, DH]) for n in range(2)]
        tb = sb("tb", [P, 2, DH])
        ln0 = LayerNorm(nc, sb, sem, "ln0", const)
        ln1 = LayerNorm(nc, sb, sem, "ln1", const)
        NG = 6
        s_vec = sem("vectors_loaded")
        s_x = [sem(f"x_loaded{p}") for p in range(2)]
        s_ys = [sem(f"y_stored_primed{p}") for p in range(2)]
        s_zn = sem("zn_loaded")
        s_xn = sem("x_normalised")
        s_hat = sem("x_hat_done")
        s_xb = sem("x_bias_added")
        s_z = sem("z_spectrum_done")
        s_zc = sem("z_spectrum_copied")
        s_zu = sem("z_spectrum_used_primed")
        s_pc = sem("product_steps")
        s_phi = sem("product_hi_done")
        s_p = sem("product_split")
        s_i = sem("convolution_done_primed")
        s_r = sem("ffn_output_done")
        s_y = sem("y_done_primed")
        block = ctx.enter_context(nc.Block())
        y_rows = y_dram.rearrange("b (t p) d -> b p t d", p=P)
        x_rows = T["x"].rearrange("b (t p) d -> b p t d", p=P)

        def next_count(i, par):
            return i + par

        @block.sync
        def _(sp):
            for p in range(2):
                sp.sem_inc(s_ys[p], 16)
            sp.dma_start(X[0][:, :, :], x_rows[0]).then_inc(s_x[0], 16)
            sp.dma_start(b2[:, :], bcast(T["b1b"])).then_inc(s_vec, 16)
            sp.dma_start(zn[0][:, :].bitcast(F32), zhi[0:CTX, :]).then_inc(s_zn, 16)
            sp.dma_start(zn[1][:, :].bitcast(F32), zlo[0:CTX, :]).then_inc(s_zn, 16)

            def body(b, i, par, last):
                if not last:
                    n = next_count(i, par)
                    sp.wait_ge(s_ys[1 - par], 16 * n + 16)
                    sp.dma_start(X[1 - par][:, :, :], x_rows[bass.ds(b + 1, 1)].rearrange("o p t d -> (o p) t d"))\
                      .then_inc(s_x[1 - par], 16)
                    sp.wait_ge(s_z, 2 * b + 2)
                    for h, src in ((0, zhi), (1, zlo)):
                        sp.dma_start(zn[h][:, :].bitcast(F32), src[bass.ds((b + 1) * CTX, CTX), :]).then_inc(s_zn, 16)
                sp.wait_ge(s_y, NT * b + 2 * NT)
                sp.dma_start(y_rows[bass.ds(b, 1)].rearrange("o p t d -> (o p) t d"), X[par][:, :, :])\
                  .then_inc(s_ys[par], 16)

            pairs_loop(sp, body, NB // 2)
            for p in range(2):
                sp.wait_ge(s_ys[p], 16 * (NB // 2) + 16)

        @block.gpsimd
        def _(pool):
            def norms(n, par):
                ln0.pool(pool, n)
                ln1.pool(pool, n)
                for t in range(NT):
                    pool.wait_ge(s_hat, NT * n + t + 1)
                    nc.gpsimd.tensor_tensor(X[par][:, t, :], X[par][:, t, :], b2[:, :], ALU.add).then_inc(s_xb, 1)

            pool.wait_ge(s_vec, 16)
            norms(0, 0)

            def body(b, i, par, last):
                if not last:
                    norms(b + 1, 1 - par)

            pairs_loop(pool, body, NB // 2)

        @block.scalar
        def _(act):
            for t in range(NT):
                ffn.input_hi(act, 0, t)

            def product_hi(b, g):
                act.wait_ge(s_pc, 7 * NG * b + 7 * g + 7)
                if g == 0:
                    act.wait_ge(s_i, NT * b + NT)
                half, q = g // 3, g % 3
                nc.scalar.activation(pr[0][:, 2 * q:2 * q + 2, half * DH:(half + 1) * DH], ta[g % 2][:, :, :],
                                     ACT.Copy).then_inc(s_phi, 1)

            def z_copy(b, half):
                act.wait_ge(s_z, 2 * b + half + 1)
                act.wait_ge(s_zu, 2 * b + half + 1)
                for n in range(2):
                    done = nc.scalar.activation(zs[:, 2 * n:2 * n + 2, :],
                                                ffn.side[n][:, :].rearrange("p (a n) -> p a n", a=2), ACT.Copy)
                done.then_inc(s_zc, 1)

            def body(b, i, par, last):
                for f in range(NF):
                    ffn.activate(act, b, f)
                    if f == 0:
                        z_copy(b, 0)
                    if f >= 2 and f - 2 < NG:
                        product_hi(b, f - 2)
                    if f == 3:
                        z_copy(b, 1)
                if not last:
                    for t in range(NT):
                        ffn.input_hi(act, b + 1, t)

            pairs_loop(act, body, NB // 2)

        @block.vector
        def _(dve):
            def norm_a(n, par, count):
                dve.wait_ge(s_x[par], 16 * count)
                ln0.dve(dve, X[par], n)

            def norm_b(n, par):
                dve.wait_ge(ln0.s_rstd, n + 1)
                for t in range(NT):
                    ln0.apply(X[par][:, t, :], X[par][:, t, :], t).then_inc(s_xn, 1)
                dve.wait_ge(s_xn, NT * n + NT)
                ln1.dve(dve, X[par], n)

            def hat_tile(n, par, t):
                if t == 0:
                    dve.wait_ge(ln1.s_rstd, n + 1)
                if t >= 2:
                    dve.wait_ge(ffn.s_t, NT * n + t - 1)
                ln1.apply(hat[:, t % 2, :], X[par][:, t, :], t).then_inc(s_hat, 1)

            def group(b, g):
                half, q = g // 3, g % 3
                c = 7 * NG * b + 7 * g
                if q == 0:
                    dve.wait_ge(s_zc, 2 * b + half + 1)
                G = [(G1, 0), (G2, 0), (G1, 1), (G2, 1)]
                for n, (g_, ph) in enumerate(G):
                    out = ta[g % 2] if n == 0 else tb
                    spec = zs[:, n:n + 1, :].broadcast_to([P, 2, DH])
                    if n >= 2:
                        dve.wait_ge(s_pc, c + 2 * n - 1)
                    mul = nc.vector.tensor_tensor(out[:, :, :], g_[:, ph, 2 * q:2 * q + 2, half * DH:(half + 1) * DH],
                                                  spec, ALU.mult)
                    mul.then_inc(s_pc, 1)
                    if n:
                        dve.wait_ge(s_pc, c + 2 * n)
                        nc.vector.tensor_tensor(ta[g % 2][:, :, :], ta[g % 2][:, :, :], tb[:, :, :], ALU.add)\
                          .then_inc(s_pc, 1)
                if q == 2:
                    dve.wait_ge(s_pc, c + 7)
                    dve.sem_inc(s_zu, 1)

            def product_lo(b, g):
                dve.wait_ge(s_phi, NG * b + g + 1)
                if g == 0:
                    dve.wait_ge(s_i, NT * b + NT)
                half, q = g // 3, g % 3
                dst = (slice(None), slice(2 * q, 2 * q + 2), slice(half * DH, (half + 1) * DH))
                nc.vector.tensor_tensor(pr[1][dst], ta[g % 2][:, :, :], pr[0][dst].bitcast(F32), ALU.subtract)\
                  .then_inc(s_p, 1)

            def output(b, par, t):
                dve.wait_ge(s_xb, NT * b + t + 1)
                if t == 0:
                    dve.wait_ge(ffn.s_down, NF * b + NF + 2)
                r = nc.vector.tensor_tensor(X[par][:, t, :], ffn.acc[t][:, :], X[par][:, t, :], ALU.add)
                r.then_inc(s_r, 1)
                dve.wait_ge(s_r, NT * b + t + 1)
                dve.wait_ge(s_i, NT * b + NT + t + 1)
                nc.vector.tensor_tensor(X[par][:, t, :], ffn.side[t % 2][:, :], X[par][:, t, :], ALU.mult)\
                  .then_inc(s_y, 1)

            ffn.prime(dve)
            dve.sem_inc(s_zu, 1)
            dve.sem_inc(s_i, NT)
            dve.sem_inc(s_y, NT)
            norm_a(0, 0, 1)
            norm_b(0, 0)
            for t in range(NT):
                hat_tile(0, 0, t)
                if t >= 1:
                    ffn.input_lo(dve, 0, t - 1)
            ffn.input_lo(dve, 0, NT - 1)

            def body(b, i, par, last):
                for f in range(NF):
                    ffn.hidden_lo(dve, b, f)
                    if f >= 2:
                        product_lo(b, f - 2)
                    if f >= 1 and f - 1 < NG:
                        group(b, f - 1)
                    if not last:
                        if f == 0:
                            norm_a(b + 1, 1 - par, next_count(i, par) + 1)
                        if f == 2:
                            norm_b(b + 1, 1 - par)
                        if f == 5:
                            hat_tile(b + 1, 1 - par, 0)
                            hat_tile(b + 1, 1 - par, 1)
                if not last:
                    ffn.input_lo(dve, b + 1, 0)
                    ffn.input_lo(dve, b + 1, 1)
                    hat_tile(b + 1, 1 - par, 2)
                    hat_tile(b + 1, 1 - par, 3)
                    ffn.input_lo(dve, b + 1, 2)
                    ffn.input_lo(dve, b + 1, 3)
                for t in range(NT):
                    output(b, par, t)
                dve.wait_ge(s_r, NT * b + NT)
                dve.sem_inc(ffn.s_acc, 1)

            pairs_loop(dve, body, NB // 2)

        @block.tensor
        def _(pe):
            def z_spectrum(b, half):
                if half == 0:
                    pe.wait_ge(s_zn, 32 * b + 32)
                    pe.wait_ge(s_y, NT * b + NT)
                else:
                    pe.wait_ge(s_zc, 2 * b + 1)
                cut = slice(half * DH, (half + 1) * DH)
                for n in range(4):
                    m = slice(n * P, (n + 1) * P)
                    last = product(pe, ffn.side[n // 2][:, (n % 2) * DH:(n % 2 + 1) * DH],
                                   [(fz[0][0:CTX, 0, m], fz[1][0:CTX, 0, m], zn[0][:, cut], zn[1][:, cut])])
                last.then_inc(s_z, 1)

            def inverse(b, t):
                if t == 0:
                    pe.wait_ge(s_p, NG * b + NG)
                if t >= 2:
                    pe.wait_ge(s_y, NT * b + NT + t - 1)
                terms = []
                for n, p in enumerate(PIECES[t]):
                    m = slice((2 * (t % 2) + n) * P, (2 * (t % 2) + n + 1) * P)
                    terms.append((inv[0][:, 0, m], inv[1][:, 0, m], pr[0][:, p, :], pr[1][:, p, :]))
                product(pe, ffn.side[t % 2][:, :], terms).then_inc(s_i, 1)

            def transpose(n, t):
                pe.wait_ge(s_hat, NT * n + t + 1)
                ffn.transpose(pe, hat[:, t % 2, :], ident, t)

            for t in range(NT):
                if t >= 2:
                    pe.wait_ge(ffn.s_xT, t - 1)
                transpose(0, t)

            def body(b, i, par, last):
                for f in range(NF):
                    ffn.up_product(pe, b, f)
                    if f == 0:
                        z_spectrum(b, 0)
                    if f == 1:
                        z_spectrum(b, 1)
                    if f >= 2:
                        ffn.down_product(pe, b, f - 2)
                pe.wait_ge(s_zc, 2 * b + 2)
                if not last:
                    transpose(b + 1, 0)
                    transpose(b + 1, 1)
                ffn.down_product(pe, b, NF - 2)
                if not last:
                    for t in (2, 3):
                        pe.wait_ge(ffn.s_xT, NT * b + NT + t - 1)
                        transpose(b + 1, t)
                ffn.down_product(pe, b, NF - 1)
                for t in range(NT):
                    if t < 2 and not last:
                        pe.wait_ge(ffn.s_xT, NT * b + NT + 3 + t)
                    inverse(b, t)

            pairs_loop(pe, body, NB // 2)


def stage_b(nc, T, y_dram, u_dram, xs_dram, ident, const, tri, base, rank, score):
    with ExitStack() as ctx:
        ctx.enter_context(nc.cleanup_on_exit())
        def sb(n, shape, dt=F32):
            return ctx.enter_context(nc.sbuf_tensor(f"b_{n}", shape, dt))

        def sem(n):
            return nc.alloc_semaphore(name=f"b_{n}")

        w1 = [sb(f"w1{h}", [P, KC, F], F32R) for h in "hl"]
        w2 = [sb(f"w2{h}", [P, NF, D], F32R) for h in "hl"]
        b1 = sb("b1", [P, NF])
        split_weights(nc, "bw", [(T["W2a"], *w1, T["g2"]), (T["W2b"], *w2, None)], (T["be2"], T["b2a"], b1))
        ffn = Ffn(nc, ctx, "bf", NF, ACT.Silu, w1, w2, b1)
        Y = [sb(f"y{p}", [P, NT, D]) for p in range(2)]
        X = sb("x", [P, NT, D])
        hat = sb("hat", [P, 2, D])
        b2 = sb("b2", [P, D])
        wr = sb("wr", [P, D])
        x1 = sb("x1", [P, NT, D])
        xm = sb("xm", [P, NT, D])
        us = sb("us", [P, NT, D])
        junk = sb("junk", [P, D])
        ones = sb("ones", [P, P])
        sc = sb("sc", [P, NT])
        scb = sb("scb", [P, NT, P])
        cnt = sb("cnt", [P, 2, NT])
        rk = sb("rk", [P, NT])
        row = sb("row", [P, NT], U32)
        ln0 = LayerNorm(nc, sb, sem, "bln0", const)
        ln1 = LayerNorm(nc, sb, sem, "bln1", const)
        s_vec = sem("vectors_loaded")
        s_yl = [sem(f"y_loaded{p}") for p in range(2)]
        s_x = sem("x_loaded")
        s_hat = sem("y_hat_done")
        s_yb = sem("y_bias_added")
        s_r = sem("ffn_output_done")
        s_x1 = sem("x1_done")
        s_xm = sem("x1_normalised")
        s_sc = sem("scores_done")
        s_scb = sem("scores_spread")
        s_one = sem("ones_done")
        s_st = sem("scores_transposed")
        s_cnt = sem("ranks_counted")
        s_rk = sem("rank_done")
        s_row = sem("row_done")
        s_keep = sem("rank_kept")
        s_u = sem("u_done")
        s_us = sem("u_stored")
        s_sct = sem("rows_scattered")
        s_go = sem("scatter_started")
        block = ctx.enter_context(nc.Block())
        rows = lambda d: d.rearrange("b (t p) d -> b p t d", p=P)
        one = lambda d, b: rows(d)[bass.ds(b, 1)].rearrange("o p t d -> (o p) t d")

        def loop(eng, body):
            n = NB // 2
            for par in range(2):
                body(par, 0, par, par == 0, False)
            with eng.Fori(1, n - 1) as i:
                for par in range(2):
                    body(2 * i + par, i, par, False, False)
            for par in range(2):
                body(2 * (n - 1) + par, n - 1, par, False, par == 1)

        @block.sync
        def _(sp):
            sp.dma_start(Y[0][:, :, :], one(y_dram, 0)).then_inc(s_yl[0], 16)
            sp.dma_start(b2[:, :], bcast(T["b2b"])).then_inc(s_vec, 16)
            sp.dma_start(wr[:, :], bcast(T["w_router"])).then_inc(s_vec, 16)

            def body(b, i, par, first, last):
                if not first:
                    sp.wait_ge(s_x1, NT * b)
                sp.dma_start(X[:, :, :], one(T["x"], b)).then_inc(s_x, 16)
                if not last:
                    if not first:
                        sp.wait_ge(s_r, NT * b)
                    sp.dma_start(Y[1 - par][:, :, :], one(y_dram, b + 1)).then_inc(s_yl[1 - par], 16)
                if not first:
                    sp.wait_ge(s_u, NT * b)
                    sp.dma_start(one(u_dram, b - 1), us[:, :, :]).then_inc(s_us, 16)

            loop(sp, body)
            sp.wait_ge(s_u, NT * NB)
            sp.dma_start(one(u_dram, NB - 1), us[:, :, :]).then_inc(s_us, 16)
            sp.wait_ge(s_us, 16 * NB)

        @block.gpsimd
        def _(pool):
            def add_bias(n, par):
                for t in range(NT):
                    pool.wait_ge(s_hat, NT * n + t + 1)
                    nc.gpsimd.tensor_tensor(Y[par][:, t, :], Y[par][:, t, :], b2[:, :], ALU.add).then_inc(s_yb, 1)

            def post(n, first=False):
                ln1.pool(pool, n)
                if not first:
                    pool.wait_ge(s_us, 16 * n)
                for t in range(NT):
                    pool.wait_ge(s_xm, NT * n + t + 1)
                    nc.gpsimd.tensor_tensor(us[:, t, :], x1[:, t, :], xm[:, t, :], ALU.add).then_inc(s_u, 1)

            def scatter(n):
                pool.wait_ge(s_row, n + 1)
                pool.sem_inc(s_go, 1)
                for t in range(NT):
                    pool.indirect_dma_start(xs_dram[:, :], bass.IndirectOffsetOnAxis(ap=row[:, t:t + 1], axis=0),
                                            xm[:, t, :], None).then_inc(s_sct, 16)

            pool.wait_ge(s_vec, 32)
            ln0.pool(pool, 0)
            add_bias(0, 0)

            def body(b, i, par, first, last):
                if not first:
                    post(b - 1, isinstance(b, int) and b == 1)
                if not last:
                    ln0.pool(pool, b + 1)
                if not first:
                    scatter(b - 1)
                if not last:
                    add_bias(b + 1, 1 - par)

            loop(pool, body)
            post(NB - 1)
            scatter(NB - 1)
            pool.wait_ge(s_sct, 16 * NT * NB)

        @block.scalar
        def _(act):
            for t in range(NT):
                ffn.input_hi(act, 0, t)

            def body(b, i, par, first, last):
                for f in range(NF):
                    ffn.activate(act, b, f)
                if not last:
                    for t in range(NT):
                        ffn.input_hi(act, b + 1, t)

            loop(act, body)

        @block.vector
        def _(dve):
            def hat_tile(n, par, t):
                if t == 0:
                    dve.wait_ge(ln0.s_rstd, n + 1)
                if t >= 2:
                    dve.wait_ge(ffn.s_t, NT * n + t - 1)
                ln0.apply(hat[:, t % 2, :], Y[par][:, t, :], t).then_inc(s_hat, 1)

            def output(b, par, t, first):
                dve.wait_ge(s_yb, NT * b + t + 1)
                if t == 0:
                    dve.wait_ge(ffn.s_down, NF * b + NF + 2)
                    dve.wait_ge(s_x, 16 * b + 16)
                    if not first:
                        dve.wait_ge(s_u, NT * b)
                nc.vector.tensor_tensor(x1[:, t, :], ffn.acc[t][:, :], Y[par][:, t, :], ALU.add).then_inc(s_r, 1)
                dve.wait_ge(s_r, NT * b + t + 1)
                nc.vector.tensor_tensor(x1[:, t, :], x1[:, t, :], X[:, t, :], ALU.add).then_inc(s_x1, 1)

            def normalise(n, first):
                dve.wait_ge(ln1.s_rstd, n + 1)
                if not first:
                    dve.wait_ge(s_sct, 16 * NT * n)
                for t in range(NT):
                    ln1.apply(xm[:, t, :], x1[:, t, :], t).then_inc(s_xm, 1)

            def scores(n):
                for t in range(NT):
                    dve.wait_ge(s_xm, NT * n + t + 1)
                    nc.vector.tensor_tensor_reduce(junk[:, :], xm[:, t, :], wr[:, :], 1.0, 0.0, ALU.mult,
                                                   ALU.add, sc[:, t:t + 1]).then_inc(s_sc, 1)
                    dve.wait_ge(s_sc, NT * n + t + 1)
                    nc.vector.tensor_scalar(scb[:, t, :], ones[:, :], sc[:, t:t + 1], None, ALU.mult)\
                      .then_inc(s_scb, 1)

            def count(n, t):
                if t == 0:
                    dve.wait_ge(s_st, n + 1)
                nc.vector.tensor_scalar(junk[:, :], ffn.side[0][:, :], sc[:, t:t + 1], None, ALU.is_gt, ALU.add,
                                        accum_out=cnt[:, 0, t:t + 1]).then_inc(s_cnt, 1)
                dve.wait_ge(s_cnt, 2 * NT * n + 2 * t + 1)
                nc.vector.scalar_tensor_tensor(junk[:, :], ffn.side[0][:, :], sc[:, t:t + 1],
                                               tri[:, (NT - 1 - t) * P:(NT - 1 - t) * P + S],
                                               ALU.is_equal, ALU.mult, accum_out=cnt[:, 1, t:t + 1])\
                  .then_inc(s_cnt, 1)
                dve.wait_ge(s_cnt, 2 * NT * n + 2 * t + 2)

            def ranks(n):
                nc.vector.tensor_tensor(rk[:, :], cnt[:, 0, :], cnt[:, 1, :], ALU.add).then_inc(s_rk, 1)
                dve.wait_ge(s_rk, n + 1)
                nc.vector.tensor_tensor(row[:, :], rk[:, :], base[:, bass.ds(n * NT, NT)], ALU.add)\
                  .then_inc(s_row, 1)
                nc.vector.tensor_copy(rank[:, bass.ds(n * NT, NT)], rk[:, :]).then_inc(s_keep, 1)
                nc.vector.tensor_copy(score[:, bass.ds(n * NT, NT)], sc[:, :]).then_inc(s_keep, 1)
                dve.wait_ge(s_keep, 2 * n + 2)

            ffn.prime(dve)
            nc.vector.memset(ones[:, :], 1.0).then_inc(s_one, 1)
            dve.wait_ge(s_one, 1)
            dve.wait_ge(s_vec, 32)
            dve.wait_ge(s_yl[0], 16)
            ln0.dve(dve, Y[0], 0)
            for t in range(NT):
                hat_tile(0, 0, t)
                if t >= 1:
                    ffn.input_lo(dve, 0, t - 1)
            ffn.input_lo(dve, 0, NT - 1)

            def body(b, i, par, first, last):
                for f in range(NF):
                    if not first:
                        if f == 0:
                            ln1.dve(dve, x1, b - 1)
                        if f == 1:
                            normalise(b - 1, isinstance(b, int) and b == 1)
                        if f == 2:
                            scores(b - 1)
                        if 3 <= f < 3 + NT:
                            count(b - 1, f - 3)
                        if f == 7:
                            ranks(b - 1)
                    ffn.hidden_lo(dve, b, f)
                    if not last:
                        if f == 3:
                            dve.wait_ge(s_yl[1 - par], 16 * (i + par) + 16)
                            ln0.dve(dve, Y[1 - par], b + 1)
                        if f == 5:
                            hat_tile(b + 1, 1 - par, 0)
                            hat_tile(b + 1, 1 - par, 1)
                if not last:
                    ffn.input_lo(dve, b + 1, 0)
                    ffn.input_lo(dve, b + 1, 1)
                    hat_tile(b + 1, 1 - par, 2)
                    hat_tile(b + 1, 1 - par, 3)
                    ffn.input_lo(dve, b + 1, 2)
                    ffn.input_lo(dve, b + 1, 3)
                for t in range(NT):
                    output(b, par, t, first)
                dve.wait_ge(s_x1, NT * b + NT)
                dve.sem_inc(ffn.s_acc, 1)

            loop(dve, body)
            n = NB - 1
            ln1.dve(dve, x1, n)
            normalise(n, False)
            scores(n)
            for t in range(NT):
                count(n, t)
            ranks(n)

        @block.tensor
        def _(pe):
            def transpose(n, t):
                pe.wait_ge(s_hat, NT * n + t + 1)
                ffn.transpose(pe, hat[:, t % 2, :], ident, t)

            def spread_scores(n, xt):
                pe.wait_ge(s_scb, NT * n + NT)
                pe.wait_ge(ffn.s_xT, xt)
                for t in range(NT):
                    last = pe.transpose(ffn.side[0][:, t * P:(t + 1) * P], scb[:, t, :], ident)
                last.then_inc(s_st, 1)

            for t in range(NT):
                if t >= 2:
                    pe.wait_ge(ffn.s_xT, t - 1)
                transpose(0, t)

            def body(b, i, par, first, last):
                for f in range(NF):
                    ffn.up_product(pe, b, f)
                    if f == 3 and not first:
                        spread_scores(b - 1, NT * b + NT)
                    if f >= 2:
                        ffn.down_product(pe, b, f - 2)
                if not last:
                    if not first:
                        pe.wait_ge(s_cnt, 2 * NT * b)
                    transpose(b + 1, 0)
                    transpose(b + 1, 1)
                ffn.down_product(pe, b, NF - 2)
                if not last:
                    for t in (2, 3):
                        pe.wait_ge(ffn.s_xT, NT * b + NT + t - 1)
                        transpose(b + 1, t)
                ffn.down_product(pe, b, NF - 1)

            loop(pe, body)
            pe.wait_ge(s_cnt, 2 * NT * (NB - 1))
            spread_scores(NB - 1, NT * NB)


def stage_c(nc, T, u_dram, xs_dram, upd_dram, out, ident, rank, score):
    with ExitStack() as ctx:
        ctx.enter_context(nc.cleanup_on_exit())
        def sb(n, shape, dt=F32):
            return ctx.enter_context(nc.sbuf_tensor(f"c_{n}", shape, dt))

        def sem(n):
            return nc.alloc_semaphore(name=f"c_{n}")

        w1 = [sb(f"w1{h}", [P, KC, FM], F32R) for h in "hl"]
        w2 = [sb(f"w2{h}", [P, NFM, D], F32R) for h in "hl"]
        split_weights(nc, "cw2", [(T["W1"], *w1, None), (T["W2"], *w2, None)])
        b1 = sb("b1", [P, NFM])
        ffn = Ffn(nc, ctx, "cf", NFM, ACT.Gelu_apprx_tanh, w1, w2, b1)
        sel = sb("sel", [P, NT, D])
        upd = sb("upd", [P, NT, D])
        b2 = sb("b2", [P, D])
        gat = sb("gat", [P, NT, D])
        us = sb("us", [P, NT, D])
        NC = NB * NT
        weight = sb("weight", [P, NC])
        cbase = sb("cbase", [P, NC])
        issel = sb("issel", [P, NC])
        t1 = sb("t1", [P, NC])
        t2 = sb("t2", [P, NC])
        idx = sb("idx", [P, NC], U32)
        idxb = sb("idxb", [P, NT], U32)
        wtb = sb("wtb", [P, NT])
        zrow = sb("zrow", [1, D])
        NPAIR = NB // 2
        s_vec, s_idx, s_wt, s_zr, s_zs = (sem("vectors_loaded"), sem("index_steps"), sem("weights_done"),
                                          sem("zero_row_done"), sem("zero_row_stored"))
        s_sel = sem("rows_loaded")
        s_u = sem("update_done")
        s_us = sem("update_stored")
        s_ul = sem("u_loaded")
        s_gat = sem("update_gathered")
        s_go = sem("gather_started")
        s_ix = sem("indices_picked")
        s_o = sem("output_done")
        s_os = sem("output_stored")
        block = ctx.enter_context(nc.Block())
        rows = lambda d: d.rearrange("b (t p) d -> b p t d", p=P)
        one = lambda d, b: rows(d)[bass.ds(b, 1)].rearrange("o p t d -> (o p) t d")
        xs = xs_dram.rearrange("(b r) d -> b r d", b=NB)
        xs_rows = xs[:, 0:TOP, :].rearrange("(q e) (h p) d -> q p e h d", e=2, p=P)
        upd_rows = upd_dram[0:2 * TOP, :].rearrange("(t p) d -> p t d", p=P)

        def loop(eng, body):
            body(0, True, False)
            with eng.Fori(1, NPAIR - 1) as q:
                body(q, False, False)
            body(NPAIR - 1, False, True)

        @block.sync
        def _(sp):
            sp.dma_start(b1[:, :], T["b1"]).then_inc(s_vec, 16)
            sp.dma_start(b2[:, :], bcast(T["b2"])).then_inc(s_vec, 16)
            sp.dma_start(cbase[:, :], T["base_sel"]).then_inc(s_vec, 16)
            sp.wait_ge(s_zr, 1)
            sp.dma_start(upd_dram[2 * TOP:2 * TOP + 1, :], zrow[:, :]).then_inc(s_zs, 16)

            def load(q):
                for e in range(2):
                    src = xs_rows[bass.ds(q, 1), :, e].rearrange("o p h d -> (o p) h d")
                    sp.dma_start(sel[:, 2 * e:2 * e + 2, :], src).then_inc(s_sel, 16)

            def load_u(b, first):
                if not first:
                    sp.wait_ge(s_os, 16 * b)
                sp.dma_start(us[:, :, :], one(u_dram, b)).then_inc(s_ul, 16)

            def store(b):
                sp.wait_ge(s_o, NT * b + NT)
                sp.dma_start(one(out, b), us[:, :, :]).then_inc(s_os, 16)

            load(0)

            def body(q, first, last):
                if not last:
                    sp.wait_ge(ffn.s_t, NT * q + NT)
                    load(q + 1)
                if not first:
                    for e in range(2):
                        load_u(2 * q - 2 + e, isinstance(q, int) and q == 1 and e == 0)
                        store(2 * q - 2 + e)
                sp.wait_ge(s_u, NT * q + NT)
                sp.dma_start(upd_rows, upd[:, :, :])\
                  .then_inc(s_us, 16)

            loop(sp, body)
            for e in range(2):
                load_u(NB - 2 + e, False)
                store(NB - 2 + e)
            sp.wait_ge(s_os, 16 * NB)

        @block.gpsimd
        def _(pool):
            pool.wait_ge(s_zs, 16)

            def gather(b, q, first):
                pool.wait_ge(s_us, 16 * q + 16)
                pool.wait_ge(s_ix, 2 * b + 2)
                if not first:
                    pool.wait_ge(s_o, NT * b)
                pool.sem_inc(s_go, 1)
                for t in range(NT):
                    pool.indirect_dma_start(gat[:, t, :], None, upd_dram[:, :],
                                            bass.IndirectOffsetOnAxis(ap=idxb[:, t:t + 1], axis=0))\
                        .then_inc(s_gat, 16)

            def body(q, first, last):
                if not first:
                    for e in range(2):
                        gather(2 * q - 2 + e, q - 1, isinstance(q, int) and q == 1 and e == 0)

            loop(pool, body)
            for e in range(2):
                gather(NB - 2 + e, NPAIR - 1, False)

        @block.scalar
        def _(act):
            nc.scalar.activation(weight[:, :], score[:, :], ACT.Sigmoid).then_inc(s_wt, 1)
            for t in range(NT):
                ffn.input_hi(act, 0, t)
            act.wait_ge(s_vec, 48)

            def body(q, first, last):
                for f in range(NFM):
                    ffn.activate(act, q, f)
                if not last:
                    for t in range(NT):
                        ffn.input_hi(act, q + 1, t)

            loop(act, body)

        @block.vector
        def _(dve):
            ffn.prime(dve)
            nc.vector.memset(zrow[:, :], 0.0).then_inc(s_zr, 1)
            dve.wait_ge(s_vec, 48)
            nc.vector.tensor_scalar(issel[:, :], rank[:, :], float(TOP), None, ALU.is_lt).then_inc(s_idx, 1)
            nc.vector.tensor_tensor(t1[:, :], rank[:, :], cbase[:, :], ALU.add).then_inc(s_idx, 1)
            dve.wait_ge(s_idx, 2)
            nc.vector.tensor_tensor(t2[:, :], t1[:, :], issel[:, :], ALU.mult).then_inc(s_idx, 1)
            dve.wait_ge(s_idx, 3)
            nc.vector.tensor_scalar(idx[:, :], t2[:, :], float(2 * TOP), None, ALU.add).then_inc(s_idx, 1)
            dve.wait_ge(s_idx, 4)
            dve.wait_ge(s_wt, 1)
            for t in range(NT):
                ffn.input_lo(dve, 0, t)

            def pick(b, first):
                if not first:
                    dve.wait_ge(s_gat, 16 * NT * b)
                    dve.wait_ge(s_o, NT * b)
                nc.vector.tensor_copy(idxb[:, :], idx[:, bass.ds(NT * b, NT)]).then_inc(s_ix, 1)
                nc.vector.tensor_copy(wtb[:, :], weight[:, bass.ds(NT * b, NT)]).then_inc(s_ix, 1)

            def finish(b):
                dve.wait_ge(s_ix, 2 * b + 2)
                dve.wait_ge(s_gat, 16 * NT * b + 16 * NT)
                dve.wait_ge(s_ul, 16 * b + 16)
                for t in range(NT):
                    nc.vector.scalar_tensor_tensor(us[:, t, :], gat[:, t, :], wtb[:, t:t + 1], us[:, t, :],
                                                   ALU.mult, ALU.add).then_inc(s_o, 1)

            def body(q, first, last):
                for f in range(NFM):
                    if not first:
                        if f in (0, 8):
                            pick(2 * q - 2 + f // 8, isinstance(q, int) and q == 1 and f == 0)
                        if f in (5, 13):
                            finish(2 * q - 2 + f // 8)
                    ffn.hidden_lo(dve, q, f)
                if not last:
                    for t in range(NT):
                        ffn.input_lo(dve, q + 1, t)
                dve.wait_ge(ffn.s_down, NFM * q + NFM + 2)
                if not first:
                    dve.wait_ge(s_us, 16 * q)
                for t in range(NT):
                    nc.vector.tensor_tensor(upd[:, t, :], ffn.acc[t][:, :], b2[:, :], ALU.add).then_inc(s_u, 1)
                dve.wait_ge(s_u, NT * q + NT)
                dve.sem_inc(ffn.s_acc, 1)

            loop(dve, body)
            for e in range(2):
                pick(NB - 2 + e, False)
                finish(NB - 2 + e)

        @block.tensor
        def _(pe):
            def transpose(n, t):
                if t == 0:
                    pe.wait_ge(s_sel, 32 * n + 32)
                ffn.transpose(pe, sel[:, t, :], ident, t)

            for t in range(NT):
                if t >= 2:
                    pe.wait_ge(ffn.s_xT, t - 1)
                transpose(0, t)

            def body(q, first, last):
                for f in range(NFM):
                    ffn.up_product(pe, q, f)
                    if f >= 2:
                        ffn.down_product(pe, q, f - 2)
                if not last:
                    transpose(q + 1, 0)
                    transpose(q + 1, 1)
                ffn.down_product(pe, q, NFM - 2)
                if not last:
                    for t in (2, 3):
                        pe.wait_ge(ffn.s_xT, NT * q + NT + t - 1)
                        transpose(q + 1, t)
                ffn.down_product(pe, q, NFM - 1)

            loop(pe, body)


def program(nc, T, out):
    gpad = nc.dram_tensor("gpad", [GROWS, D], F32, kind="Internal").ap()
    zhi = nc.dram_tensor("zhi", [ZROWS, D], F32, kind="Internal").ap()
    zlo = nc.dram_tensor("zlo", [ZROWS, D], F32, kind="Internal").ap()
    y_dram = nc.dram_tensor("y_mid", [NB, S, D], F32, kind="Internal").ap()
    u_dram = nc.dram_tensor("u_mid", [NB, S, D], F32, kind="Internal").ap()
    xs_dram = nc.dram_tensor("rows_by_rank", [NB * S, D], F32, kind="Internal").ap()
    upd_dram = nc.dram_tensor("updates", [2 * TOP + 1, D], F32, kind="Internal").ap()
    with ExitStack() as ctx:
        def sb(n, shape, dt=F32):
            return ctx.enter_context(nc.sbuf_tensor(n, shape, dt))

        ident = sb("ident", [P, P])
        const = sb("minus_half_and_eps", [P, 2, NT])
        with nc.semaphore("ident_loaded") as s_id, nc.semaphore("const_done") as s_c, nc.Block() as block:
            @block.sync
            def _(sp):
                sp.dma_start(ident[:, :], T["ident"]).then_inc(s_id, 16)
                sp.wait_ge(s_id, 16)

            @block.vector
            def _(dve):
                nc.vector.memset(const[:, 0, :], -0.5).then_inc(s_c, 1)
                nc.vector.memset(const[:, 1, :], EPS).then_inc(s_c, 1)
                dve.wait_ge(s_c, 2)
        context(nc, T, zhi, zlo, const)
        with ExitStack() as gctx:
            G1 = gctx.enter_context(nc.sbuf_tensor("G1", [P, 2, NP, D], F32))
            G2 = gctx.enter_context(nc.sbuf_tensor("G2", [P, 2, NP, D], F32))
            filters(nc, T, G1, G2, gpad)
            stage_a(nc, T, G1, G2, zhi, zlo, y_dram, ident[:, :], const)
        rank = sb("rank", [P, NB * NT])
        score = sb("score", [P, NB * NT])
        with ExitStack() as bctx:
            tri = bctx.enter_context(nc.sbuf_tensor("tri", [P, (NT - 1) * P + S], F32))
            base = bctx.enter_context(nc.sbuf_tensor("base", [P, NB * NT], F32))
            with nc.semaphore("tri_loaded") as s_id, nc.Block() as block:
                @block.sync
                def _(sp):
                    sp.dma_start(tri[:, :], T["tri"]).then_inc(s_id, 16)
                    sp.dma_start(base[:, :], T["base_all"]).then_inc(s_id, 16)
                    sp.wait_ge(s_id, 32)
            stage_b(nc, T, y_dram, u_dram, xs_dram, ident[:, :], const, tri, base, rank, score)
        stage_c(nc, T, u_dram, xs_dram, upd_dram, out, ident[:, :], rank, score)


_INS = {'x': 'x', 'ctx_1024': 'ctxT', 'L0_xattn_pe': 'peT', 'L0_xattn_W_in': 'W_in', 'L0_xattn_b_in': 'b_in',
        'L0_xattn_g_ln': 'g_ln', 'L0_xattn_beta_ln': 'beta_ln', 'L0_xattn_Wp1': 'Wp1', 'L0_xattn_bp1': 'bp1',
        'L0_xattn_Wp2': 'Wp2', 'L0_xattn_bp2': 'bp2', 'L0_xattn_a': 'a', 'L0_xattn_g1': 'g1',
        'L0_xattn_be1': 'be1', 'L0_xattn_W1a': 'W1a', 'L0_xattn_b1a': 'b1a', 'L0_xattn_W1b': 'W1b',
        'L0_xattn_b1b': 'b1b', 'L0_xattn_g2': 'g2', 'L0_xattn_be2': 'be2', 'L0_xattn_W2a': 'W2a',
        'L0_xattn_b2a': 'b2a', 'L0_xattn_W2b': 'W2b', 'L0_xattn_b2b': 'b2b', 'L0_ffn_w_router': 'w_router',
        'L0_ffn_W1': 'W1', 'L0_ffn_b1': 'b1', 'L0_ffn_W2': 'W2', 'L0_ffn_b2': 'b2'}


_COLUMNS = ("bp1", "g1", "be1", "b1a", "g2", "be2", "b2a", "b1")


def _constants(np):
    k, n = np.arange(64), np.arange(P)
    angle = np.pi * np.outer(n, 2 * k + 1) / P
    cos, sin = np.cos(angle), np.sin(angle)
    c = {"dft_g": np.concatenate([cos, -sin], 1)}
    fz = np.zeros((P, 4, P))
    for ph in range(2):
        rows = np.arange(ph, CTX, 2)
        j = np.arange(len(rows))
        fz[rows, 2 * ph] = np.concatenate([cos[j], cos[j]], 1)
        fz[rows, 2 * ph + 1] = np.concatenate([sin[j], -sin[j]], 1)
    c["dft_z"] = fz.reshape(P, 4 * P)
    inv = np.zeros((P, 4, P))
    for t in range(2):
        for m, p in enumerate(PIECES[t]):
            end = EDGES[p + 1]
            for col in range(P):
                u = t * P + col
                if EDGES[p] <= u < end:
                    at = u - EDGES[p] + HALO
                    inv[:64, 2 * t + m, col] = cos[at] / 64
                    inv[64:, 2 * t + m, col] = -sin[at] / 64
    c["dft_inv"] = inv.reshape(P, 4 * P)
    c["negl"] = -(np.arange(L // P)[None, :] * P + n[:, None])
    c["ident"] = np.eye(P)
    c["tri"] = (np.arange((NT - 1) * P + S)[None, :] < (NT - 1) * P + n[:, None])
    b = np.repeat(np.arange(NB), NT)[None, :]
    c["base_all"] = np.repeat(b * S, P, 0)
    c["base_sel"] = np.repeat((b % 2) * TOP - 2 * TOP, P, 0)
    return {name: np.ascontiguousarray(v, dtype=np.float32) for name, v in c.items()}


def kernel(**inputs):
    import numpy as _np
    import concourse.bacc as _bacc
    from concourse import mybir as _mybir
    from concourse.bass_utils import run_bass_kernel_spmd as _run

    nc = _bacc.Bacc("TRN2", target_bir_lowering=False, num_devices=1)
    arrays, T = {}, {}
    for name, short in _INS.items():
        a = _np.asarray(inputs[name])
        if short == "ctxT":
            a = a.reshape(ZROWS, D).T
        if short == "peT":
            a = a.T
        if short in _COLUMNS:
            a = a.reshape(-1, P).T
        arrays[f"in_{short}"] = _np.ascontiguousarray(a)
    for short, a in _constants(_np).items():
        arrays[f"in_{short}"] = a
    for full, a in arrays.items():
        T[full[3:]] = nc.dram_tensor(full, a.shape, _mybir.dt.from_np(a.dtype), kind="ExternalInput").ap()
    out = nc.dram_tensor("out_0", (NB, S, D), _mybir.dt.float32, kind="ExternalOutput").ap()
    program(nc, T, out)
    r = _run(nc, [arrays], core_ids=[0])
    return r.results[0]["out_0"]
```

```python
from contextlib import ExitStack

import concourse.bass as bass
from concourse import mybir

ALU = mybir.AluOpType
ACT = mybir.ActivationFunctionType
F32 = mybir.dt.float32
F32R = mybir.dt.float32r
I32 = mybir.dt.int32
U32 = mybir.dt.uint32

P = 128
EPS = 1e-5
D = 512
KC = D // P
NB, S = 16, 512
NT = S // P
F = 1024
NF = F // P
FM = 2048
NFM = FM // P
CTX = 77
ZROWS = NB * CTX
ZT = -(-ZROWS // P)
L = 1024
DP = 128
H = DP + D
KH = H // P
TOP = S // 2
HALO = (CTX - 1) // 2
EDGES = [0, 86, 172, 256, 342, 428]
NP = len(EDGES)
PIECES = [(0, 1), (1, 2), (3, 4), (4, 5)]
PAD = 2 * HALO + 2
GROWS = 2 * (EDGES[-1] + P) + PAD
DH = D // 2


class LayerNorm:

    def __init__(self, nc, sb, sem, name, const):
        self.nc, self.const = nc, const
        self.stats = sb(name + "_stats", [P, NT, 6])
        self.mv = sb(name + "_mv", [P, NT, 2])
        self.veps = sb(name + "_veps", [P, NT])
        self.rstd = sb(name + "_rstd", [P, NT])
        self.s_stats = sem(name + "_stats_done")
        self.s_seen = sem(name + "_stats_seen")
        self.s_mv = sem(name + "_mean_var_done")
        self.s_veps = sem(name + "_veps_done")
        self.s_rstd = sem(name + "_rstd_done")
        self.prod = sb(name + "_prod", [P, NT])
        self.shift = sb(name + "_shift", [P, NT])
        self.s_prod = sem(name + "_mean_times_rstd")
        self.s_shift = sem(name + "_shift_done")

    def dve(self, dve, x, n, used=None):
        for t in range(NT):
            self.nc.vector.bn_stats(self.stats[:, t, :], x[:, t, :]).then_inc(self.s_stats, 1)
        dve.wait_ge(self.s_stats, NT * n + NT)
        dve.sem_inc(self.s_seen, 1)
        for t in range(NT):
            self.nc.vector.bn_aggr(self.mv[:, t, :], self.stats[:, t, :]).then_inc(self.s_mv, 1)

    def pool(self, pool, n, shift=False):
        pool.wait_ge(self.s_mv, NT * n + NT)
        self.nc.gpsimd.tensor_tensor(self.veps[:, :], self.mv[:, :, 1], self.const[:, 1, :],
                                     ALU.add).then_inc(self.s_veps, 1)
        pool.wait_ge(self.s_veps, n + 1)
        self.nc.gpsimd.tensor_tensor(self.rstd[:, :], self.veps[:, :], self.const[:, 0, :],
                                     ALU.pow).then_inc(self.s_rstd, 1)
        if shift:
            pool.wait_ge(self.s_rstd, n + 1)
            self.nc.gpsimd.tensor_tensor(self.prod[:, :], self.mv[:, :, 0], self.rstd[:, :], ALU.mult)\
                .then_inc(self.s_prod, 1)
            pool.wait_ge(self.s_prod, n + 1)
            self.nc.gpsimd.tensor_tensor(self.shift[:, :], self.const[:, 2, :], self.prod[:, :],
                                         ALU.subtract).then_inc(self.s_shift, 1)

    def apply(self, out, x, t):
        return self.nc.vector.tensor_scalar(out, x, self.mv[:, t, 0:1], self.rstd[:, t:t + 1],
                                            ALU.subtract, ALU.mult)


class SecondLayerNorm:

    def __init__(self, nc, sb, sem, name, const):
        self.nc, self.const = nc, const
        self.sum = sb(name + "_sum", [P, NT])
        self.mean = sb(name + "_minus_mean", [P, NT])
        self.sq = sb(name + "_sq", [P, NT])
        self.var = sb(name + "_var", [P, NT])
        self.veps = sb(name + "_veps", [P, NT])
        self.rstd = sb(name + "_rstd", [P, NT])
        self.shift = sb(name + "_shift", [P, NT])
        self.s_mean = sem(name + "_mean_done")
        self.s_sq = sem(name + "_squares_done")
        self.s_step = sem(name + "_steps")
        self.s_rstd = sem(name + "_shift_done")

    def pool_mean(self, pool, n, s_sum):
        pool.wait_ge(s_sum, NT * n + NT)
        self.nc.gpsimd.tensor_tensor(self.mean[:, :], self.sum[:, :], self.const[:, 3, :], ALU.mult)\
            .then_inc(self.s_mean, 1)

    def pool_rstd(self, pool, n):
        pool.wait_ge(self.s_sq, NT * n + NT)
        self.nc.gpsimd.tensor_tensor(self.var[:, :], self.sq[:, :], self.const[:, 4, :], ALU.mult)\
            .then_inc(self.s_step, 1)
        pool.wait_ge(self.s_step, 3 * n + 1)
        self.nc.gpsimd.tensor_tensor(self.veps[:, :], self.var[:, :], self.const[:, 1, :], ALU.add)\
            .then_inc(self.s_step, 1)
        pool.wait_ge(self.s_step, 3 * n + 2)
        self.nc.gpsimd.tensor_tensor(self.rstd[:, :], self.veps[:, :], self.const[:, 0, :], ALU.pow)\
            .then_inc(self.s_step, 1)
        pool.wait_ge(self.s_step, 3 * n + 3)
        self.nc.gpsimd.tensor_tensor(self.shift[:, :], self.mean[:, :], self.rstd[:, :], ALU.mult)\
            .then_inc(self.s_rstd, 1)


def bcast(vec, n=P):
    return vec.rearrange("(a n) -> a n", a=1).broadcast_to([n, vec.shape[0]])


def split_weights(nc, name, jobs, bias=None):
    with ExitStack() as ctx:
        ctx.enter_context(nc.cleanup_on_exit())
        def sb(n, shape, dt=F32):
            return ctx.enter_context(nc.sbuf_tensor(f"{name}_{n}", shape, dt))

        def sem(n):
            return nc.alloc_semaphore(name=f"{name}_{n}")

        chunks = [(j, k) for j, job in enumerate(jobs) for k in range(job[1].shape[1])]
        R = 4
        width = max(job[1].shape[2] for job in jobs)
        ring = sb("ring", [P, R, width])
        cols = sb("cols", [P, 3, 16])
        s_in = [sem(f"chunk_loaded{r}") for r in range(R)]
        s_cols = sem("cols_loaded")
        s_hi = sem("hi_done")
        s_lo = sem("lo_done")
        s_bias = sem("bias_product")
        s_out = sem("bias_done")
        scaled = [j for j, job in enumerate(jobs) if job[3] is not None]
        KB = jobs[0][1].shape[1]
        NBI = jobs[0][1].shape[2] // P
        if bias is not None:
            ps = ctx.enter_context(nc.psum_tensor(f"{name}_ps", [P, 512], F32))
        block = ctx.enter_context(nc.Block())
        ncols = 16 * (len(scaled) + (2 if bias is not None else 0))

        @block.sync
        def _(sp):
            if scaled:
                sp.dma_start(cols[:, 0, 0:KB], jobs[scaled[0]][3])\
                  .then_inc(s_cols, 16)
            if bias is not None:
                sp.dma_start(cols[:, 1, 0:KB], bias[0]).then_inc(s_cols, 16)
                sp.dma_start(cols[:, 2, 0:NBI], bias[1]).then_inc(s_cols, 16)
            for n, (j, k) in enumerate(chunks):
                w, hi = jobs[j][0], jobs[j][1]
                if n >= R:
                    sp.wait_ge(s_lo, n - R + 1)
                    if bias is not None and n - R < KB:
                        sp.wait_ge(s_bias, 1)
                sp.dma_start(ring[:, n % R, 0:hi.shape[2]], w[k * P:(k + 1) * P, :]).then_inc(s_in[n % R], 16)

        @block.scalar
        def _(act):
            if ncols:
                act.wait_ge(s_cols, ncols)
            for n, (j, k) in enumerate(chunks):
                _, hi, lo, scale = jobs[j]
                act.wait_ge(s_in[n % R], 16 * (n // R + 1))
                src = ring[:, n % R, 0:hi.shape[2]]
                if scale is None:
                    nc.scalar.activation(hi[:, k, :], src, ACT.Copy).then_inc(s_hi, 1)
                else:
                    nc.scalar.activation(hi[:, k, :], src, ACT.Copy, scale=cols[:, 0, k:k + 1]).then_inc(s_hi, 1)

        @block.vector
        def _(dve):
            if ncols:
                dve.wait_ge(s_cols, ncols)
            for n, (j, k) in enumerate(chunks):
                _, hi, lo, scale = jobs[j]
                dve.wait_ge(s_in[n % R], 16 * (n // R + 1))
                dve.wait_ge(s_hi, n + 1)
                src = ring[:, n % R, 0:hi.shape[2]]
                h = hi[:, k, :].bitcast(F32)
                if scale is None:
                    nc.vector.tensor_tensor(lo[:, k, :], src, h, ALU.subtract).then_inc(s_lo, 1)
                else:
                    nc.vector.scalar_tensor_tensor(lo[:, k, :], src, cols[:, 0, k:k + 1], h,
                                                   ALU.mult, ALU.subtract).then_inc(s_lo, 1)
                if bias is not None and n == KB - 1:
                    dve.wait_ge(s_bias, 1)
                    nc.vector.tensor_tensor(bias[2][:, :], ps[:, 0:NBI], cols[:, 2, 0:NBI],
                                            ALU.add).then_inc(s_out, 1)

        @block.tensor
        def _(pe):
            if bias is not None:
                pe.wait_ge(s_cols, ncols)
                for k in range(KB):
                    pe.wait_ge(s_in[k % R], 16)
                for f in range(NBI):
                    for k in range(KB):
                        last = pe.matmul(ps[:, f:f + 1], ring[:, k, f * P:(f + 1) * P], cols[:, 1, k:k + 1],
                                         start=(k == 0), stop=(k == KB - 1))
                last.then_inc(s_bias, 1)


def passes(a_hi, a_lo, b_hi, b_lo):
    return ((a_hi, b_hi), (a_lo, b_hi), (a_hi, b_lo))


def product(pe, out, terms):
    pairs = [p for t in terms for p in passes(*t)]
    for n, (a, b) in enumerate(pairs):
        last = pe.matmul(out, a, b, start=(n == 0), stop=(n == len(pairs) - 1))
    return last


def filters(nc, T, G1, G2, gpad):
    with ExitStack() as ctx:
        ctx.enter_context(nc.cleanup_on_exit())
        def sb(n, shape, dt=F32):
            return ctx.enter_context(nc.sbuf_tensor(f"flt_{n}", shape, dt))

        def sem(n):
            return nc.alloc_semaphore(name=f"flt_{n}")

        wp1 = [sb(f"wp1{h}", [P, 1, H], F32R) for h in "hl"]
        wp2 = [sb(f"wp2{h}", [P, KH, D], F32R) for h in "hl"]
        pet = [sb(f"pet{h}", [P, 1, L], F32R) for h in "hl"]
        dft = [sb(f"dft{h}", [P, 1, P], F32R) for h in "hl"]
        split_weights(nc, "fw", [(T["Wp1"], *wp1, None), (T["Wp2"], *wp2, None), (T["peT"], *pet, None),
                                 (T["dft_g"], *dft, None)])
        hp = [sb(f"hp{h}", [P, KH, L], F32R) for h in "hl"]
        bp1 = sb("bp1", [P, KH])
        bp2 = sb("bp2", [P, D])
        negl = sb("negl", [P, L // P])
        a_col = sb("a", [P, 1])
        ea = sb("ea", [P, 1])
        arg = sb("arg", [P, L // P])
        win = sb("win", [P, L // P])
        tmp = sb("tmp", [P, 2, D])
        wh = sb("wh", [P, 2, D])
        zero = sb("zero", [P, D])
        gin = sb("gin", [P, 2, D])
        gh = sb("gh", [P, 2, D], F32R)
        gl = sb("gl", [P, 2, D], F32R)
        ps = [ctx.enter_context(nc.psum_tensor(f"flt_ps{n}", [P, D], F32)) for n in range(2)]
        s_in = sem("vectors_loaded")
        s_ea, s_arg, s_win = sem("exp_a_done"), sem("arg_done"), sem("window_done")
        s_hid, s_silu, s_hhi, s_hlo = sem("hidden_done"), sem("silu_done"), sem("hidden_hi_done"), sem("hidden_lo_done")
        s_row, s_bias, s_wh = sem("filter_done"), sem("filter_bias_added"), sem("windowed_done")
        s_st = [sem(f"windowed_stored{n}") for n in range(2)]
        s_zero, s_pad = sem("zero_done"), sem("pads_stored")
        s_gin = [sem(f"piece_loaded{n}") for n in range(2)]
        s_ghi, s_glo, s_spec, s_g1, s_g2 = (sem("piece_hi_done"), sem("piece_lo_done"), sem("spectrum_done"),
                                            sem("g1_done"), sem("g2_done"))
        block = ctx.enter_context(nc.Block())
        HID = [(f, m) for f in range(KH) for m in range(L // 512)]
        LT = L // P
        PC = [(ph, p) for p in range(NP) for ph in range(2)]

        @block.sync
        def _(sp):
            sp.dma_start(bp1[:, :], T["bp1"]).then_inc(s_in, 16)
            sp.dma_start(bp2[:, :], bcast(T["bp2"])).then_inc(s_in, 16)
            sp.dma_start(negl[:, :], T["negl"]).then_inc(s_in, 16)
            sp.dma_start(a_col[:, :], bcast(T["a"])).then_inc(s_in, 16)
            sp.wait_ge(s_zero, 1)
            sp.dma_start(gpad[0:PAD, :], zero[0:PAD, :]).then_inc(s_pad, 16)
            tail = GROWS - PAD - L
            sp.dma_start(gpad[PAD + L:GROWS, :], zero[0:tail, :]).then_inc(s_pad, 16)
            for m in range(LT):
                sp.wait_ge(s_wh, m + 1)
                sp.dma_start(gpad[PAD + m * P:PAD + (m + 1) * P, :], wh[:, m % 2, :]).then_inc(s_st[m % 2], 16)
            sp.wait_ge(s_pad, 32)
            for n in range(2):
                sp.wait_ge(s_st[n], 16 * (LT // 2))
            for n, (ph, p) in enumerate(PC):
                if n >= 2:
                    sp.wait_ge(s_glo, n - 1)
                r = 2 * EDGES[p] + 2 - ph
                sp.dma_start(gin[:, n % 2, :], gpad[r:r + 2 * P - 1:2, :]).then_inc(s_gin[n % 2], 16)
            sp.wait_ge(s_g1, 2 * NP)
            sp.dma_start(G2[0:64, :, :, :], G1[64:P, :, :, :]).then_inc(s_g2, 16)
            sp.dma_start(G2[64:P, :, :, :], G1[0:64, :, :, :]).then_inc(s_g2, 16)
            sp.wait_ge(s_g2, 32)

        @block.scalar
        def _(act):
            act.wait_ge(s_in, 64)
            nc.scalar.activation(ea[:, :], a_col[:, :], ACT.Exp).then_inc(s_ea, 1)
            act.wait_ge(s_arg, 1)
            nc.scalar.activation(win[:, :], arg[:, :], ACT.Exp).then_inc(s_win, 1)
            for n, (f, m) in enumerate(HID):
                act.wait_ge(s_hid, n + 1)
                nc.scalar.activation(ps[n % 2][:, :], ps[n % 2][:, :], ACT.Silu,
                                     bias=bp1[:, f:f + 1]).then_inc(s_silu, 1)
                act.wait_ge(s_silu, n + 1)
                nc.scalar.activation(hp[0][:, f, m * 512:(m + 1) * 512], ps[n % 2][:, :], ACT.Copy)\
                  .then_inc(s_hhi, 1)
            act.wait_ge(s_win, 1)
            for m in range(LT):
                act.wait_ge(s_bias, m + 1)
                if m >= 2:
                    act.wait_ge(s_st[m % 2], 16 * (m // 2))
                nc.scalar.activation(wh[:, m % 2, :], tmp[:, m % 2, :], ACT.Copy, scale=win[:, m:m + 1])\
                  .then_inc(s_wh, 1)
            for n in range(2 * NP):
                act.wait_ge(s_gin[n % 2], 16 * (n // 2 + 1))
                if n >= 2:
                    act.wait_ge(s_spec, n - 1)
                nc.scalar.activation(gh[:, n % 2, :], gin[:, n % 2, :], ACT.Copy).then_inc(s_ghi, 1)

        def g1_copy(dve, n):
            ph, p = PC[n]
            dve.wait_ge(s_spec, n + 1)
            nc.vector.tensor_copy(G1[:, ph, p, :], ps[n % 2][:, :]).then_inc(s_g1, 1)

        @block.vector
        def _(dve):
            nc.vector.memset(zero[:, :], 0.0).then_inc(s_zero, 1)
            dve.wait_ge(s_in, 64)
            dve.wait_ge(s_ea, 1)
            nc.vector.tensor_scalar(arg[:, :], negl[:, :], ea[:, 0:1], None, ALU.mult).then_inc(s_arg, 1)
            for n, (f, m) in enumerate(HID):
                dve.wait_ge(s_hhi, n + 1)
                nc.vector.tensor_tensor(hp[1][:, f, m * 512:(m + 1) * 512], ps[n % 2][:, :],
                                        hp[0][:, f, m * 512:(m + 1) * 512].bitcast(F32),
                                        ALU.subtract).then_inc(s_hlo, 1)
            for m in range(LT):
                dve.wait_ge(s_row, m + 1)
                if m >= 2:
                    dve.wait_ge(s_wh, m - 1)
                nc.vector.tensor_tensor(tmp[:, m % 2, :], ps[m % 2][:, :], bp2[:, :], ALU.add)\
                  .then_inc(s_bias, 1)
            for n, (ph, p) in enumerate(PC):
                dve.wait_ge(s_ghi, n + 1)
                if n >= 2:
                    dve.wait_ge(s_spec, n - 1)
                nc.vector.tensor_tensor(gl[:, n % 2, :], gin[:, n % 2, :], gh[:, n % 2, :].bitcast(F32),
                                        ALU.subtract).then_inc(s_glo, 1)
                if n >= 1:
                    g1_copy(dve, n - 1)
            g1_copy(dve, 2 * NP - 1)

        @block.tensor
        def _(pe):
            for n, (f, m) in enumerate(HID):
                if n >= 2:
                    pe.wait_ge(s_hlo, n - 1)
                cut = slice(m * 512, (m + 1) * 512)
                product(pe, ps[n % 2][:, :], [(wp1[0][:, 0, f * P:(f + 1) * P], wp1[1][:, 0, f * P:(f + 1) * P],
                                               pet[0][:, 0, cut], pet[1][:, 0, cut])]).then_inc(s_hid, 1)
            pe.wait_ge(s_hlo, len(HID))
            for m in range(LT):
                if m >= 2:
                    pe.wait_ge(s_bias, m - 1)
                product(pe, ps[m % 2][:, :], [(hp[0][:, f, m * P:(m + 1) * P], hp[1][:, f, m * P:(m + 1) * P],
                                               wp2[0][:, f, :], wp2[1][:, f, :]) for f in range(KH)])\
                    .then_inc(s_row, 1)
            pe.wait_ge(s_bias, LT)
            for n in range(2 * NP):
                pe.wait_ge(s_glo, n + 1)
                if n >= 2:
                    pe.wait_ge(s_g1, n - 1)
                product(pe, ps[n % 2][:, :], [(dft[0][:, 0, :], dft[1][:, 0, :], gh[:, n % 2, :], gl[:, n % 2, :])])\
                    .then_inc(s_spec, 1)


def context(nc, T, zhi, zlo, const):
    with ExitStack() as ctx:
        ctx.enter_context(nc.cleanup_on_exit())
        def sb(n, shape, dt=F32):
            return ctx.enter_context(nc.sbuf_tensor(f"ctx_{n}", shape, dt))

        def sem(n):
            return nc.alloc_semaphore(name=f"ctx_{n}")

        win = [sb(f"win{h}", [P, KC, D], F32R) for h in "hl"]
        ct = [sb(f"ct{h}", [P, KC, ZROWS], F32R) for h in "hl"]
        split_weights(nc, "cw", [(T["W_in"], *win, None), (T["ctxT"], *ct, None)])
        vec = {n: sb(n, [P, D]) for n in ("b_in", "g_ln", "beta_ln")}
        z = sb("z", [P, 3, D])
        zh = sb("zh", [P, 2, D], F32R)
        zl = sb("zl", [P, 2, D], F32R)
        stats = sb("stats", [P, 2, 6])
        mv = sb("mv", [P, 2, 2])
        veps = sb("veps", [P, 2])
        rstd = sb("rstd", [P, 2])
        ps = [ctx.enter_context(nc.psum_tensor(f"ctx_ps{n}", [P, D], F32)) for n in range(2)]
        s_in, s_mm = sem("vectors_loaded"), sem("z_product_done")
        s_d = sem("z_steps")
        s_veps, s_rstd = sem("veps_done"), sem("rstd_done")
        s_hi, s_lo = sem("z_hi_done"), sem("z_lo_done")
        s_st = [sem(f"z_stored{n}") for n in range(2)]
        block = ctx.enter_context(nc.Block())
        rows = [min(P, ZROWS - n * P) for n in range(ZT)]

        @block.sync
        def _(sp):
            for n in vec:
                sp.dma_start(vec[n][:, :], bcast(T[n])).then_inc(s_in, 16)
            for n in range(ZT):
                sp.wait_ge(s_lo, n + 1)
                r = rows[n]
                sp.dma_start(zhi[n * P:n * P + r, :], zh[0:r, n % 2, :].bitcast(F32)).then_inc(s_st[n % 2], 16)
                sp.dma_start(zlo[n * P:n * P + r, :], zl[0:r, n % 2, :].bitcast(F32)).then_inc(s_st[n % 2], 16)
            for k in range(2):
                sp.wait_ge(s_st[k], 32 * (ZT // 2))

        @block.tensor
        def _(pe):
            for n in range(ZT):
                if n >= 2:
                    pe.wait_ge(s_d, 6 * (n - 2) + 1)
                r, at = rows[n], n * P
                product(pe, ps[n % 2][0:r, :], [(ct[0][:, k, at:at + r], ct[1][:, k, at:at + r],
                                                 win[0][:, k, :], win[1][:, k, :]) for k in range(KC)])\
                    .then_inc(s_mm, 1)

        @block.gpsimd
        def _(pool):
            for n in range(ZT):
                r, k = rows[n], n % 2
                pool.wait_ge(s_d, 6 * n + 3)
                nc.gpsimd.tensor_scalar(veps[0:r, k:k + 1], mv[0:r, k, 1:2], 1.0, EPS, ALU.mult, ALU.add)\
                  .then_inc(s_veps, 1)
                pool.wait_ge(s_veps, n + 1)
                nc.gpsimd.tensor_tensor(rstd[0:r, k:k + 1], veps[0:r, k:k + 1], const[0:r, 0, 0:1], ALU.pow)\
                  .then_inc(s_rstd, 1)

        @block.scalar
        def _(act):
            for n in range(ZT):
                r, k = rows[n], n % 2
                act.wait_ge(s_d, 6 * n + 6)
                if n >= 2:
                    act.wait_ge(s_st[k], 32 * (n // 2))
                nc.scalar.activation(zh[0:r, k, :], z[0:r, 2, :], ACT.Copy).then_inc(s_hi, 1)

        @block.vector
        def _(dve):
            dve.wait_ge(s_in, 48)
            for n in range(ZT):
                r, k = rows[n], n % 2
                c = 6 * n
                dve.wait_ge(s_mm, n + 1)
                nc.vector.tensor_tensor(z[0:r, 0, :], ps[k][0:r, :], vec["b_in"][0:r, :], ALU.add).then_inc(s_d, 1)
                dve.wait_ge(s_d, c + 1)
                nc.vector.bn_stats(stats[0:r, k, :], z[0:r, 0, :]).then_inc(s_d, 1)
                dve.wait_ge(s_d, c + 2)
                nc.vector.bn_aggr(mv[0:r, k, :], stats[0:r, k, :]).then_inc(s_d, 1)
                dve.wait_ge(s_rstd, n + 1)
                dve.wait_ge(s_d, c + 3)
                nc.vector.tensor_scalar(z[0:r, 1, :], z[0:r, 0, :], mv[0:r, k, 0:1], rstd[0:r, k:k + 1],
                                        ALU.subtract, ALU.mult).then_inc(s_d, 1)
                dve.wait_ge(s_d, c + 4)
                nc.vector.tensor_tensor(z[0:r, 0, :], z[0:r, 1, :], vec["g_ln"][0:r, :], ALU.mult).then_inc(s_d, 1)
                dve.wait_ge(s_d, c + 5)
                nc.vector.tensor_tensor(z[0:r, 2, :], z[0:r, 0, :], vec["beta_ln"][0:r, :], ALU.add)\
                  .then_inc(s_d, 1)
                dve.wait_ge(s_d, c + 6)
                dve.wait_ge(s_hi, n + 1)
                if n >= 2:
                    dve.wait_ge(s_st[k], 32 * (n // 2))
                nc.vector.tensor_tensor(zl[0:r, k, :], z[0:r, 2, :], zh[0:r, k, :].bitcast(F32),
                                        ALU.subtract).then_inc(s_lo, 1)


class Ffn:

    def __init__(self, nc, ctx, name, nf, func, w1, w2, b1):
        def sb(n, shape, dt=F32):
            return ctx.enter_context(nc.sbuf_tensor(f"{name}_{n}", shape, dt))

        def sem(n):
            return nc.alloc_semaphore(name=f"{name}_{n}")

        self.nc, self.nf, self.func, self.w1, self.w2, self.b1 = nc, nf, func, w1, w2, b1
        self.xT = [sb(f"xT{h}", [P, KC, 512], F32R) for h in "hl"]
        self.hid = [sb(f"hid{h}", [P, 2, 512], F32R) for h in "hl"]
        self.acc = [ctx.enter_context(nc.psum_tensor(f"{name}_acc{t}", [P, D], F32)) for t in range(NT)]
        self.up = [ctx.enter_context(nc.psum_tensor(f"{name}_up{t}", [P, 512], F32)) for t in range(2)]
        self.side = [ctx.enter_context(nc.psum_tensor(f"{name}_side{t}", [P, 512], F32)) for t in range(2)]
        self.s_up = sem("hidden_product_done")
        self.s_act = sem("hidden_act_done")
        self.s_hi = sem("hidden_hi_done")
        self.s_hid = sem("hidden_split_primed")
        self.s_down = sem("hidden_used_primed")
        self.s_acc = sem("outputs_free_primed")
        self.s_t = sem("transposed")
        self.s_thi = sem("transposed_hi_done")
        self.s_xT = sem("input_ready")

    def prime(self, eng):
        eng.sem_inc(self.s_hid, 2)
        eng.sem_inc(self.s_down, 2)
        eng.sem_inc(self.s_acc, 1)

    def up_product(self, pe, u, f):
        if f == 0:
            pe.wait_ge(self.s_xT, NT * u + NT)
        pe.wait_ge(self.s_hid, self.nf * u + f + 1)
        cut = slice(f * P, (f + 1) * P)
        product(pe, self.up[f % 2][:, :], [(self.w1[0][:, k, cut], self.w1[1][:, k, cut],
                                            self.xT[0][:, k, :], self.xT[1][:, k, :]) for k in range(KC)])\
            .then_inc(self.s_up, 1)

    def down_product(self, pe, u, f):
        if f == 0:
            pe.wait_ge(self.s_acc, u + 1)
        pe.wait_ge(self.s_hid, self.nf * u + f + 3)
        for t in range(NT):
            cut = slice(t * P, (t + 1) * P)
            pairs = passes(self.hid[0][:, f % 2, cut], self.hid[1][:, f % 2, cut],
                           self.w2[0][:, f, :], self.w2[1][:, f, :])
            for n, (a, b) in enumerate(pairs):
                last = pe.matmul(self.acc[t][:, :], a, b, start=(f == 0 and n == 0),
                                 stop=(f == self.nf - 1 and n == 2), skip_group_check=True)
        last.then_inc(self.s_down, 1)

    def transpose(self, pe, src, ident, t):
        for k in range(KC):
            last = pe.transpose(self.side[t % 2][:, k * P:(k + 1) * P], src[:, k * P:(k + 1) * P], ident)
        last.then_inc(self.s_t, 1)

    def activate(self, act, u, f):
        act.wait_ge(self.s_up, self.nf * u + f + 1)
        self.nc.scalar.activation(self.up[f % 2][:, :], self.up[f % 2][:, :], self.func,
                                  bias=self.b1[:, f:f + 1]).then_inc(self.s_act, 1)
        act.wait_ge(self.s_act, self.nf * u + f + 1)
        act.wait_ge(self.s_down, self.nf * u + f + 1)
        self.nc.scalar.activation(self.hid[0][:, f % 2, :], self.up[f % 2][:, :], ACT.Copy)\
            .then_inc(self.s_hi, 1)

    def input_hi(self, act, u, t):
        act.wait_ge(self.s_t, NT * u + t + 1)
        side = self.side[t % 2][:, :].rearrange("p (k n) -> p k n", k=KC)
        self.nc.scalar.activation(self.xT[0][:, :, t * P:(t + 1) * P], side, ACT.Copy).then_inc(self.s_thi, 1)

    def hidden_lo(self, dve, u, f):
        dve.wait_ge(self.s_hi, self.nf * u + f + 1)
        self.nc.vector.tensor_tensor(self.hid[1][:, f % 2, :], self.up[f % 2][:, :],
                                     self.hid[0][:, f % 2, :].bitcast(F32), ALU.subtract)\
            .then_inc(self.s_hid, 1)

    def input_lo(self, dve, u, t):
        dve.wait_ge(self.s_thi, NT * u + t + 1)
        side = self.side[t % 2][:, :].rearrange("p (k n) -> p k n", k=KC)
        cut = slice(t * P, (t + 1) * P)
        self.nc.vector.tensor_tensor(self.xT[1][:, :, cut], side, self.xT[0][:, :, cut].bitcast(F32),
                                     ALU.subtract).then_inc(self.s_xT, 1)


def pairs_loop(eng, body, n):
    with eng.Fori(0, n - 1) as i:
        for par in range(2):
            body(2 * i + par, i, par, False)
    for par in range(2):
        body(2 * (n - 1) + par, n - 1, par, par == 1)


def stage_a(nc, T, G1, G2, zhi, zlo, y_dram, ident, const):
    with ExitStack() as ctx:
        ctx.enter_context(nc.cleanup_on_exit())
        def sb(n, shape, dt=F32):
            return ctx.enter_context(nc.sbuf_tensor(f"a_{n}", shape, dt))

        def sem(n):
            return nc.alloc_semaphore(name=f"a_{n}")

        w1 = [sb(f"w1{h}", [P, KC, F], F32R) for h in "hl"]
        w2 = [sb(f"w2{h}", [P, NF, D], F32R) for h in "hl"]
        b1 = sb("b1", [P, NF])
        fz = [sb(f"fz{h}", [P, 1, 4 * P], F32R) for h in "hl"]
        inv = [sb(f"inv{h}", [P, 1, 4 * P], F32R) for h in "hl"]
        split_weights(nc, "aw", [(T["W1a"], *w1, T["g1"]), (T["W1b"], *w2, None), (T["dft_z"], *fz, None),
                                 (T["dft_inv"], *inv, None)], (T["be1"], T["b1a"], b1))
        ffn = Ffn(nc, ctx, "af", NF, ACT.Silu, w1, w2, b1)
        X = [sb(f"x{p}", [P, NT, D]) for p in range(2)]
        hat = sb("hat", [P, 2, D])
        b2 = sb("b2", [P, D])
        zn = [sb(f"zn{h}", [CTX, D], F32R) for h in "hl"]
        zs = sb("zs", [P, 4, DH])
        pr = [sb(f"pr{h}", [P, NP, D], F32R) for h in "hl"]
        ta = [sb(f"ta{n}", [P, 2, DH]) for n in range(2)]
        tb = [sb(f"tb{n}", [P, 2, DH]) for n in range(2)]
        ln0 = LayerNorm(nc, sb, sem, "ln0", const)
        ln1 = SecondLayerNorm(nc, sb, sem, "ln1", const)
        NG = 6
        GROUP_STEP = [0, 1, 3, 4, 5, 6]
        s_vec = sem("vectors_loaded")
        s_x = [sem(f"x_loaded{p}") for p in range(2)]
        s_ys = [sem(f"y_stored_primed{p}") for p in range(2)]
        s_zn = sem("zn_loaded")
        s_xn = sem("x_normalised")
        s_hat = sem("x_hat_done")
        s_xb = sem("x_bias_added")
        s_z = sem("z_spectrum_done")
        s_zc = sem("z_spectrum_copied")
        s_zu = sem("z_spectrum_used_primed")
        s_pc = sem("product_steps_primed")
        s_phi = sem("product_hi_done")
        s_p = sem("product_split_primed")
        s_i = sem("convolution_done_primed")
        s_r = sem("ffn_output_done")
        s_y = sem("y_done_primed")
        block = ctx.enter_context(nc.Block())
        y_rows = y_dram.rearrange("b (t p) d -> b p t d", p=P)
        x_rows = T["x"].rearrange("b (t p) d -> b p t d", p=P)

        def conv_bank(t):
            return (ffn.up[t] if t < 2 else ffn.side[t - 2])[:, :]

        def next_count(i, par):
            return i + par

        @block.sync
        def _(sp):
            for p in range(2):
                sp.sem_inc(s_ys[p], 16)
            sp.dma_start(X[0][:, :, :], x_rows[0]).then_inc(s_x[0], 16)
            sp.dma_start(b2[:, :], bcast(T["b1b"])).then_inc(s_vec, 16)
            sp.dma_start(zn[0][:, :].bitcast(F32), zhi[0:CTX, :]).then_inc(s_zn, 16)
            sp.dma_start(zn[1][:, :].bitcast(F32), zlo[0:CTX, :]).then_inc(s_zn, 16)

            def body(b, i, par, last):
                if not last:
                    n = next_count(i, par)
                    sp.wait_ge(s_ys[1 - par], 16 * n + 16)
                    sp.dma_start(X[1 - par][:, :, :], x_rows[bass.ds(b + 1, 1)].rearrange("o p t d -> (o p) t d"))\
                      .then_inc(s_x[1 - par], 16)
                    sp.wait_ge(s_z, 2 * b + 2)
                    for h, src in ((0, zhi), (1, zlo)):
                        sp.dma_start(zn[h][:, :].bitcast(F32), src[bass.ds((b + 1) * CTX, CTX), :]).then_inc(s_zn, 16)
                sp.wait_ge(s_y, NT * b + 2 * NT)
                sp.dma_start(y_rows[bass.ds(b, 1)].rearrange("o p t d -> (o p) t d"), X[par][:, :, :])\
                  .then_inc(s_ys[par], 16)

            pairs_loop(sp, body, NB // 2)
            for p in range(2):
                sp.wait_ge(s_ys[p], 16 * (NB // 2) + 16)

        @block.gpsimd
        def _(pool):
            def norms(n):
                ln0.pool(pool, n, shift=True)
                ln1.pool_mean(pool, n, s_xn)
                ln1.pool_rstd(pool, n)

            def add_bias(n, par):
                for t in range(NT):
                    pool.wait_ge(s_hat, NT * n + t + 1)
                    nc.gpsimd.tensor_tensor(X[par][:, t, :], X[par][:, t, :], b2[:, :], ALU.add).then_inc(s_xb, 1)

            pool.wait_ge(s_vec, 16)
            norms(0)
            add_bias(0, 0)

            def product_lo(b, g):
                pool.wait_ge(s_phi, NG * b + g + 1)
                half, q = g // 3, g % 3
                dst = (slice(None), slice(2 * q, 2 * q + 2), slice(half * DH, (half + 1) * DH))
                nc.gpsimd.tensor_tensor(pr[1][dst], ta[g % 2][:, :, :], pr[0][dst].bitcast(F32), ALU.subtract)\
                  .then_inc(s_p, 1)

            def body(b, i, par, last):
                product_lo(b, 0)
                if not last:
                    ln0.pool(pool, b + 1, shift=True)
                product_lo(b, 1)
                product_lo(b, 2)
                if not last:
                    ln1.pool_mean(pool, b + 1, s_xn)
                product_lo(b, 3)
                product_lo(b, 4)
                if not last:
                    ln1.pool_rstd(pool, b + 1)
                product_lo(b, 5)
                if not last:
                    add_bias(b + 1, 1 - par)

            pairs_loop(pool, body, NB // 2)

        @block.scalar
        def _(act):
            def normalise(n, par, t):
                if t == 0:
                    act.wait_ge(ln0.s_shift, n + 1)
                nc.scalar.activation(X[par][:, t, :], X[par][:, t, :], ACT.Identity, bias=ln0.shift[:, t:t + 1],
                                     scale=ln0.rstd[:, t:t + 1], accum_out=ln1.sum[:, t:t + 1]).then_inc(s_xn, 1)

            def squares(n, par, t):
                if t == 0:
                    act.wait_ge(ln1.s_mean, n + 1)
                    act.wait_ge(ffn.s_t, NT * n)
                if t >= 2:
                    act.wait_ge(ln1.s_sq, NT * n + t - 1)
                nc.scalar.activation(hat[:, t % 2, :], X[par][:, t, :], ACT.Square, bias=ln1.mean[:, t:t + 1],
                                     accum_out=ln1.sq[:, t:t + 1]).then_inc(ln1.s_sq, 1)

            def hat_tile(n, par, t):
                if t == 0:
                    act.wait_ge(ln1.s_rstd, n + 1)
                if t >= 2:
                    act.wait_ge(ffn.s_t, NT * n + t - 1)
                nc.scalar.activation(hat[:, t % 2, :], X[par][:, t, :], ACT.Identity, bias=ln1.shift[:, t:t + 1],
                                     scale=ln1.rstd[:, t:t + 1]).then_inc(s_hat, 1)

            for t in range(NT):
                normalise(0, 0, t)
            act.wait_ge(s_xn, NT)
            for t in range(NT):
                squares(0, 0, t)
            hat_tile(0, 0, 0)
            hat_tile(0, 0, 1)
            ffn.input_hi(act, 0, 0)
            ffn.input_hi(act, 0, 1)
            hat_tile(0, 0, 2)
            hat_tile(0, 0, 3)
            ffn.input_hi(act, 0, 2)
            ffn.input_hi(act, 0, 3)

            def product_hi(b, g):
                act.wait_ge(s_pc, 7 * NG * b + 7 * g + 14)
                if g == 0:
                    act.wait_ge(s_i, NT * b + NT)
                half, q = g // 3, g % 3
                nc.scalar.activation(pr[0][:, 2 * q:2 * q + 2, half * DH:(half + 1) * DH], ta[g % 2][:, :, :],
                                     ACT.Copy).then_inc(s_phi, 1)

            def z_copy(b, half):
                act.wait_ge(s_z, 2 * b + half + 1)
                act.wait_ge(s_zu, 2 * b + half + 1)
                for n in range(2):
                    done = nc.scalar.activation(zs[:, 2 * n:2 * n + 2, :],
                                                ffn.side[n][:, :].rearrange("p (a n) -> p a n", a=2), ACT.Copy)
                done.then_inc(s_zc, 1)

            def body(b, i, par, last):
                for f in range(NF):
                    ffn.activate(act, b, f)
                    if f == 0:
                        z_copy(b, 0)
                    if f == 4:
                        z_copy(b, 1)
                    if f in GROUP_STEP[1:]:
                        product_hi(b, GROUP_STEP.index(f) - 1)
                    if f == 7:
                        product_hi(b, NG - 1)
                    if not last:
                        if f in (3, 4):
                            normalise(b + 1, 1 - par, 2 * f - 6)
                            normalise(b + 1, 1 - par, 2 * f - 5)
                        if f == 5:
                            act.wait_ge(s_xn, NT * b + 2 * NT)
                        if f in (5, 6):
                            squares(b + 1, 1 - par, 2 * f - 10)
                            squares(b + 1, 1 - par, 2 * f - 9)
                        if f == 7:
                            hat_tile(b + 1, 1 - par, 0)
                            hat_tile(b + 1, 1 - par, 1)
                if not last:
                    ffn.input_hi(act, b + 1, 0)
                    ffn.input_hi(act, b + 1, 1)
                    hat_tile(b + 1, 1 - par, 2)
                    hat_tile(b + 1, 1 - par, 3)
                    ffn.input_hi(act, b + 1, 2)
                    ffn.input_hi(act, b + 1, 3)

            pairs_loop(act, body, NB // 2)

        @block.vector
        def _(dve):
            def norm_a(n, par, count):
                dve.wait_ge(s_x[par], 16 * count)
                ln0.dve(dve, X[par], n)

            def group(b, g):
                half, q = g // 3, g % 3
                c = 7 * NG * b + 7 * g + 7
                if q == 0:
                    dve.wait_ge(s_zc, 2 * b + half + 1)
                dve.wait_ge(s_p, NG * b + g + 1)
                acc = ta[g % 2][:, :, :]

                def multiply(n, out):
                    G, ph = (G1, G2)[n % 2], n // 2
                    nc.vector.tensor_tensor(out, G[:, ph, 2 * q:2 * q + 2, half * DH:(half + 1) * DH],
                                            zs[:, n:n + 1, :].broadcast_to([P, 2, DH]), ALU.mult).then_inc(s_pc, 1)

                def add(term):
                    nc.vector.tensor_tensor(acc, acc, term, ALU.add).then_inc(s_pc, 1)

                t0, t1 = tb[g % 2][:, :, :], tb[1 - g % 2][:, :, :]
                multiply(0, acc)
                dve.wait_ge(s_pc, c - 1)
                multiply(1, t0)
                dve.wait_ge(s_pc, c)
                multiply(2, t1)
                dve.wait_ge(s_pc, c + 2)
                add(t0)
                dve.wait_ge(s_pc, c + 4)
                multiply(3, t0)
                add(t1)
                dve.wait_ge(s_pc, c + 6)
                add(t0)
                if q == 2:
                    dve.wait_ge(s_pc, c + 7)
                    dve.sem_inc(s_zu, 1)

            def output(b, par, t):
                dve.wait_ge(s_xb, NT * b + t + 1)
                if t == 0:
                    dve.wait_ge(ffn.s_down, NF * b + NF + 2)
                r = nc.vector.tensor_tensor(X[par][:, t, :], ffn.acc[t][:, :], X[par][:, t, :], ALU.add)
                r.then_inc(s_r, 1)
                dve.wait_ge(s_r, NT * b + t + 1)
                dve.wait_ge(s_i, NT * b + NT + t + 1)
                nc.vector.tensor_tensor(X[par][:, t, :], conv_bank(t), X[par][:, t, :], ALU.mult)\
                  .then_inc(s_y, 1)

            ffn.prime(dve)
            dve.sem_inc(s_zu, 1)
            dve.sem_inc(s_p, 2)
            dve.sem_inc(s_pc, 7)
            dve.sem_inc(s_i, NT)
            dve.sem_inc(s_y, NT)
            norm_a(0, 0, 1)
            for t in range(NT):
                ffn.input_lo(dve, 0, t)

            def body(b, i, par, last):
                for f in range(NF):
                    ffn.hidden_lo(dve, b, f)
                    if f in GROUP_STEP:
                        group(b, GROUP_STEP.index(f))
                    if not last and f == 2:
                        norm_a(b + 1, 1 - par, next_count(i, par) + 1)
                if not last:
                    for t in range(NT):
                        ffn.input_lo(dve, b + 1, t)
                for t in range(NT):
                    output(b, par, t)
                dve.wait_ge(s_r, NT * b + NT)
                dve.sem_inc(ffn.s_acc, 1)

            pairs_loop(dve, body, NB // 2)

        @block.tensor
        def _(pe):
            def z_spectrum(b, half):
                if half == 0:
                    pe.wait_ge(s_zn, 32 * b + 32)
                    pe.wait_ge(s_y, NT * b + NT)
                else:
                    pe.wait_ge(s_zc, 2 * b + 1)
                cut = slice(half * DH, (half + 1) * DH)
                for n in range(4):
                    m = slice(n * P, (n + 1) * P)
                    last = product(pe, ffn.side[n // 2][:, (n % 2) * DH:(n % 2 + 1) * DH],
                                   [(fz[0][0:CTX, 0, m], fz[1][0:CTX, 0, m], zn[0][:, cut], zn[1][:, cut])])
                last.then_inc(s_z, 1)

            def inverse(b, t):
                if t == 0:
                    pe.wait_ge(s_p, NG * b + NG + 2)
                terms = []
                for n, p in enumerate(PIECES[t]):
                    m = slice((2 * (t % 2) + n) * P, (2 * (t % 2) + n + 1) * P)
                    terms.append((inv[0][:, 0, m], inv[1][:, 0, m], pr[0][:, p, :], pr[1][:, p, :]))
                product(pe, conv_bank(t), terms).then_inc(s_i, 1)

            def transpose(n, t):
                pe.wait_ge(s_hat, NT * n + t + 1)
                ffn.transpose(pe, hat[:, t % 2, :], ident, t)

            for t in range(NT):
                if t >= 2:
                    pe.wait_ge(ffn.s_xT, t - 1)
                transpose(0, t)

            def body(b, i, par, last):
                for f in range(NF):
                    if f < 2:
                        pe.wait_ge(s_y, NT * b + f + 1)
                    ffn.up_product(pe, b, f)
                    if f == 0:
                        z_spectrum(b, 0)
                    if f == 1:
                        z_spectrum(b, 1)
                    if f >= 2:
                        ffn.down_product(pe, b, f - 2)
                pe.wait_ge(s_zc, 2 * b + 2)
                if not last:
                    transpose(b + 1, 0)
                    transpose(b + 1, 1)
                ffn.down_product(pe, b, NF - 2)
                if not last:
                    for t in (2, 3):
                        pe.wait_ge(ffn.s_xT, NT * b + NT + t - 1)
                        transpose(b + 1, t)
                for t in (0, 1):
                    pe.wait_ge(ffn.s_hid, NF * b + NF + 1 + t)
                    inverse(b, t)
                ffn.down_product(pe, b, NF - 1)
                for t in (2, 3):
                    if not last:
                        pe.wait_ge(ffn.s_xT, NT * b + NT + 1 + t)
                    inverse(b, t)

            pairs_loop(pe, body, NB // 2)


def stage_b(nc, T, y_dram, u_dram, xs_dram, ident, const, tri, base, rank, score):
    with ExitStack() as ctx:
        ctx.enter_context(nc.cleanup_on_exit())
        def sb(n, shape, dt=F32):
            return ctx.enter_context(nc.sbuf_tensor(f"b_{n}", shape, dt))

        def sem(n):
            return nc.alloc_semaphore(name=f"b_{n}")

        w1 = [sb(f"w1{h}", [P, KC, F], F32R) for h in "hl"]
        w2 = [sb(f"w2{h}", [P, NF, D], F32R) for h in "hl"]
        b1 = sb("b1", [P, NF])
        split_weights(nc, "bw", [(T["W2a"], *w1, T["g2"]), (T["W2b"], *w2, None)], (T["be2"], T["b2a"], b1))
        ffn = Ffn(nc, ctx, "bf", NF, ACT.Silu, w1, w2, b1)
        Y = [sb(f"y{p}", [P, NT, D]) for p in range(2)]
        X = sb("x", [P, NT, D])
        hat = sb("hat", [P, 2, D])
        b2 = sb("b2", [P, D])
        wr = sb("wr", [P, D])
        x1 = sb("x1", [P, NT, D])
        xm = sb("xm", [P, NT, D])
        us = sb("us", [P, NT, D])
        junk = sb("junk", [P, D])
        ones = sb("ones", [P, P])
        sc = sb("sc", [P, NT])
        scb = sb("scb", [P, NT, P])
        cnt = sb("cnt", [P, 2, NT])
        rk = sb("rk", [P, NT])
        row = sb("row", [P, NT], U32)
        ln0 = LayerNorm(nc, sb, sem, "bln0", const)
        ln1 = LayerNorm(nc, sb, sem, "bln1", const)
        s_vec = sem("vectors_loaded")
        s_yl = [sem(f"y_loaded{p}") for p in range(2)]
        s_x = sem("x_loaded")
        s_hat = sem("y_hat_done")
        s_yb = sem("y_bias_added")
        s_r = sem("ffn_output_done")
        s_x1 = sem("x1_done")
        s_xm = sem("x1_normalised")
        s_sc = sem("scores_done")
        s_scb = sem("scores_spread")
        s_one = sem("ones_done")
        s_st = sem("scores_transposed")
        s_cnt = sem("ranks_counted")
        s_rk = sem("rank_done")
        s_row = sem("row_done")
        s_keep = sem("rank_kept")
        s_u = sem("u_done")
        s_us = sem("u_stored")
        s_sct = sem("rows_scattered")
        s_go = sem("scatter_started")
        block = ctx.enter_context(nc.Block())
        rows = lambda d: d.rearrange("b (t p) d -> b p t d", p=P)
        one = lambda d, b: rows(d)[bass.ds(b, 1)].rearrange("o p t d -> (o p) t d")

        def loop(eng, body):
            n = NB // 2
            for par in range(2):
                body(par, 0, par, par == 0, False)
            with eng.Fori(1, n - 1) as i:
                for par in range(2):
                    body(2 * i + par, i, par, False, False)
            for par in range(2):
                body(2 * (n - 1) + par, n - 1, par, False, par == 1)

        @block.sync
        def _(sp):
            sp.dma_start(Y[0][:, :, :], one(y_dram, 0)).then_inc(s_yl[0], 16)
            sp.dma_start(b2[:, :], bcast(T["b2b"])).then_inc(s_vec, 16)
            sp.dma_start(wr[:, :], bcast(T["w_router"])).then_inc(s_vec, 16)

            def body(b, i, par, first, last):
                if not first:
                    sp.wait_ge(s_x1, NT * b)
                sp.dma_start(X[:, :, :], one(T["x"], b)).then_inc(s_x, 16)
                if not last:
                    if not first:
                        sp.wait_ge(s_r, NT * b)
                    sp.dma_start(Y[1 - par][:, :, :], one(y_dram, b + 1)).then_inc(s_yl[1 - par], 16)
                if not first:
                    sp.wait_ge(s_u, NT * b)
                    sp.dma_start(one(u_dram, b - 1), us[:, :, :]).then_inc(s_us, 16)

            loop(sp, body)
            sp.wait_ge(s_u, NT * NB)
            sp.dma_start(one(u_dram, NB - 1), us[:, :, :]).then_inc(s_us, 16)
            sp.wait_ge(s_us, 16 * NB)

        @block.gpsimd
        def _(pool):
            def add_bias(n, par):
                for t in range(NT):
                    pool.wait_ge(s_hat, NT * n + t + 1)
                    nc.gpsimd.tensor_tensor(Y[par][:, t, :], Y[par][:, t, :], b2[:, :], ALU.add).then_inc(s_yb, 1)

            def post(n, first=False):
                if not first:
                    pool.wait_ge(s_us, 16 * n)
                for t in range(NT):
                    pool.wait_ge(s_xm, NT * n + t + 1)
                    nc.gpsimd.tensor_tensor(us[:, t, :], x1[:, t, :], xm[:, t, :], ALU.add).then_inc(s_u, 1)

            def scatter(n):
                pool.wait_ge(s_row, n + 1)
                pool.sem_inc(s_go, 1)
                for t in range(NT):
                    pool.indirect_dma_start(xs_dram[:, :], bass.IndirectOffsetOnAxis(ap=row[:, t:t + 1], axis=0),
                                            xm[:, t, :], None).then_inc(s_sct, 16)

            pool.wait_ge(s_vec, 32)
            ln0.pool(pool, 0, shift=True)
            add_bias(0, 0)

            def body(b, i, par, first, last):
                if not first:
                    ln1.pool(pool, b - 1, shift=True)
                if not last:
                    ln0.pool(pool, b + 1, shift=True)
                if not first:
                    post(b - 1, isinstance(b, int) and b == 1)
                    scatter(b - 1)
                if not last:
                    add_bias(b + 1, 1 - par)

            loop(pool, body)
            ln1.pool(pool, NB - 1, shift=True)
            post(NB - 1)
            scatter(NB - 1)
            pool.wait_ge(s_sct, 16 * NT * NB)

        @block.scalar
        def _(act):
            def hat_tile(n, par, t):
                if t == 0:
                    act.wait_ge(ln0.s_shift, n + 1)
                    act.wait_ge(s_yl[par], 16)
                if t >= 2:
                    act.wait_ge(ffn.s_t, NT * n + t - 1)
                nc.scalar.activation(hat[:, t % 2, :], Y[par][:, t, :], ACT.Identity, bias=ln0.shift[:, t:t + 1],
                                     scale=ln0.rstd[:, t:t + 1]).then_inc(s_hat, 1)

            def normalise(n, first):
                act.wait_ge(ln1.s_shift, n + 1)
                if not first:
                    act.wait_ge(s_sct, 16 * NT * n)
                for t in range(NT):
                    nc.scalar.activation(xm[:, t, :], x1[:, t, :], ACT.Identity, bias=ln1.shift[:, t:t + 1],
                                         scale=ln1.rstd[:, t:t + 1]).then_inc(s_xm, 1)

            hat_tile(0, 0, 0)
            hat_tile(0, 0, 1)
            ffn.input_hi(act, 0, 0)
            ffn.input_hi(act, 0, 1)
            hat_tile(0, 0, 2)
            hat_tile(0, 0, 3)
            ffn.input_hi(act, 0, 2)
            ffn.input_hi(act, 0, 3)

            def body(b, i, par, first, last):
                for f in range(NF):
                    ffn.activate(act, b, f)
                    if f == 2 and not first:
                        normalise(b - 1, isinstance(b, int) and b == 1)
                    if f in (5, 6) and not last:
                        hat_tile(b + 1, 1 - par, f - 5)
                if not last:
                    ffn.input_hi(act, b + 1, 0)
                    ffn.input_hi(act, b + 1, 1)
                    hat_tile(b + 1, 1 - par, 2)
                    hat_tile(b + 1, 1 - par, 3)
                    ffn.input_hi(act, b + 1, 2)
                    ffn.input_hi(act, b + 1, 3)

            loop(act, body)
            normalise(NB - 1, False)

        @block.vector
        def _(dve):
            def output(b, par, t, first):
                dve.wait_ge(s_yb, NT * b + t + 1)
                if t == 0:
                    dve.wait_ge(ffn.s_down, NF * b + NF + 2)
                    if not first:
                        dve.wait_ge(s_u, NT * b)
                nc.vector.tensor_tensor(x1[:, t, :], ffn.acc[t][:, :], Y[par][:, t, :], ALU.add).then_inc(s_r, 1)

            def residual(n):
                dve.wait_ge(s_x, 16 * n + 16)
                dve.wait_ge(s_r, NT * n + NT)
                for t in range(NT):
                    nc.vector.tensor_tensor(x1[:, t, :], x1[:, t, :], X[:, t, :], ALU.add).then_inc(s_x1, 1)

            def x1_stats(n):
                dve.wait_ge(s_x1, NT * n + NT)
                ln1.dve(dve, x1, n)

            def scores(n, tiles):
                for t in tiles:
                    dve.wait_ge(s_xm, NT * n + t + 1)
                    nc.vector.tensor_tensor_reduce(junk[:, :], xm[:, t, :], wr[:, :], 1.0, 0.0, ALU.mult,
                                                   ALU.add, sc[:, t:t + 1]).then_inc(s_sc, 1)
                    dve.wait_ge(s_sc, NT * n + t + 1)
                    nc.vector.tensor_scalar(scb[:, t, :], ones[:, :], sc[:, t:t + 1], None, ALU.mult)\
                      .then_inc(s_scb, 1)

            def count(n, t):
                if t == 0:
                    dve.wait_ge(s_st, n + 1)
                nc.vector.tensor_scalar(junk[:, :], ffn.side[0][:, :], sc[:, t:t + 1], None, ALU.is_gt, ALU.add,
                                        accum_out=cnt[:, 0, t:t + 1]).then_inc(s_cnt, 1)
                dve.wait_ge(s_cnt, 2 * NT * n + 2 * t + 1)
                nc.vector.scalar_tensor_tensor(junk[:, :], ffn.side[0][:, :], sc[:, t:t + 1],
                                               tri[:, (NT - 1 - t) * P:(NT - 1 - t) * P + S],
                                               ALU.is_equal, ALU.mult, accum_out=cnt[:, 1, t:t + 1])\
                  .then_inc(s_cnt, 1)
                dve.wait_ge(s_cnt, 2 * NT * n + 2 * t + 2)

            def ranks(n):
                nc.vector.tensor_tensor(rk[:, :], cnt[:, 0, :], cnt[:, 1, :], ALU.add).then_inc(s_rk, 1)
                dve.wait_ge(s_rk, n + 1)
                nc.vector.tensor_tensor(row[:, :], rk[:, :], base[:, bass.ds(n * NT, NT)], ALU.add)\
                  .then_inc(s_row, 1)
                nc.vector.tensor_copy(rank[:, bass.ds(n * NT, NT)], rk[:, :]).then_inc(s_keep, 1)
                nc.vector.tensor_copy(score[:, bass.ds(n * NT, NT)], sc[:, :]).then_inc(s_keep, 1)
                dve.wait_ge(s_keep, 2 * n + 2)

            ffn.prime(dve)
            nc.vector.memset(ones[:, :], 1.0).then_inc(s_one, 1)
            dve.wait_ge(s_one, 1)
            dve.wait_ge(s_vec, 32)
            dve.wait_ge(s_yl[0], 16)
            ln0.dve(dve, Y[0], 0)
            for t in range(NT):
                ffn.input_lo(dve, 0, t)

            def body(b, i, par, first, last):
                for f in range(NF):
                    ffn.hidden_lo(dve, b, f)
                    if not first:
                        if f == 0:
                            residual(b - 1)
                        if f == 1:
                            x1_stats(b - 1)
                        if f == 3:
                            scores(b - 1, (0, 1, 2))
                        if f == 4:
                            scores(b - 1, (3,))
                        if f in (5, 6):
                            count(b - 1, 2 * f - 10)
                            count(b - 1, 2 * f - 9)
                        if f == 6:
                            ranks(b - 1)
                    if not last and f == 2:
                        dve.wait_ge(s_yl[1 - par], 16 * (i + par) + 16)
                        ln0.dve(dve, Y[1 - par], b + 1)
                if not last:
                    for t in range(NT):
                        ffn.input_lo(dve, b + 1, t)
                for t in range(NT):
                    output(b, par, t, first)
                dve.wait_ge(s_r, NT * b + NT)
                dve.sem_inc(ffn.s_acc, 1)

            loop(dve, body)
            n = NB - 1
            residual(n)
            x1_stats(n)
            scores(n, range(NT))
            for t in range(NT):
                count(n, t)
            ranks(n)

        @block.tensor
        def _(pe):
            def transpose(n, t):
                pe.wait_ge(s_hat, NT * n + t + 1)
                ffn.transpose(pe, hat[:, t % 2, :], ident, t)

            def spread_scores(n, xt):
                pe.wait_ge(s_scb, NT * n + NT)
                pe.wait_ge(ffn.s_xT, xt)
                for t in range(NT):
                    last = pe.transpose(ffn.side[0][:, t * P:(t + 1) * P], scb[:, t, :], ident)
                last.then_inc(s_st, 1)

            for t in range(NT):
                if t >= 2:
                    pe.wait_ge(ffn.s_xT, t - 1)
                transpose(0, t)

            def body(b, i, par, first, last):
                for f in range(NF):
                    ffn.up_product(pe, b, f)
                    if f == 5 and not first:
                        spread_scores(b - 1, NT * b + NT)
                    if f >= 2:
                        ffn.down_product(pe, b, f - 2)
                if not last:
                    if not first:
                        pe.wait_ge(s_cnt, 2 * NT * b)
                    transpose(b + 1, 0)
                    transpose(b + 1, 1)
                ffn.down_product(pe, b, NF - 2)
                if not last:
                    for t in (2, 3):
                        pe.wait_ge(ffn.s_xT, NT * b + NT + t - 1)
                        transpose(b + 1, t)
                ffn.down_product(pe, b, NF - 1)

            loop(pe, body)
            pe.wait_ge(s_cnt, 2 * NT * (NB - 1))
            spread_scores(NB - 1, NT * NB)


def stage_c(nc, T, u_dram, xs_dram, upd_dram, out, ident, rank, score):
    with ExitStack() as ctx:
        ctx.enter_context(nc.cleanup_on_exit())
        def sb(n, shape, dt=F32):
            return ctx.enter_context(nc.sbuf_tensor(f"c_{n}", shape, dt))

        def sem(n):
            return nc.alloc_semaphore(name=f"c_{n}")

        w1 = [sb(f"w1{h}", [P, KC, FM], F32R) for h in "hl"]
        w2 = [sb(f"w2{h}", [P, NFM, D], F32R) for h in "hl"]
        split_weights(nc, "cw2", [(T["W1"], *w1, None), (T["W2"], *w2, None)])
        b1 = sb("b1", [P, NFM])
        ffn = Ffn(nc, ctx, "cf", NFM, ACT.Gelu_apprx_tanh, w1, w2, b1)
        sel = sb("sel", [P, NT, D])
        upd = sb("upd", [P, NT, D])
        b2 = sb("b2", [P, D])
        gat = sb("gat", [P, NT, D])
        us = sb("us", [P, NT, D])
        NC = NB * NT
        weight = sb("weight", [P, NC])
        cbase = sb("cbase", [P, NC])
        issel = sb("issel", [P, NC])
        t1 = sb("t1", [P, NC])
        t2 = sb("t2", [P, NC])
        idx = sb("idx", [P, NC], U32)
        idxb = sb("idxb", [P, NT], U32)
        wtb = sb("wtb", [P, NT])
        zrow = sb("zrow", [1, D])
        NPAIR = NB // 2
        s_vec, s_idx, s_wt, s_zr, s_zs = (sem("vectors_loaded"), sem("index_steps"), sem("weights_done"),
                                          sem("zero_row_done"), sem("zero_row_stored"))
        s_sel = sem("rows_loaded")
        s_u = sem("update_done")
        s_us = sem("update_stored")
        s_ul = sem("u_loaded")
        s_gat = sem("update_gathered")
        s_go = sem("gather_started")
        s_ix = sem("indices_picked")
        s_o = sem("output_done")
        s_os = sem("output_stored")
        block = ctx.enter_context(nc.Block())
        rows = lambda d: d.rearrange("b (t p) d -> b p t d", p=P)
        one = lambda d, b: rows(d)[bass.ds(b, 1)].rearrange("o p t d -> (o p) t d")
        xs = xs_dram.rearrange("(b r) d -> b r d", b=NB)
        xs_rows = xs[:, 0:TOP, :].rearrange("(q e) (h p) d -> q p e h d", e=2, p=P)
        upd_rows = upd_dram[0:2 * TOP, :].rearrange("(t p) d -> p t d", p=P)

        def loop(eng, body):
            body(0, True, False)
            with eng.Fori(1, NPAIR - 1) as q:
                body(q, False, False)
            body(NPAIR - 1, False, True)

        @block.sync
        def _(sp):
            sp.dma_start(b1[:, :], T["b1"]).then_inc(s_vec, 16)
            sp.dma_start(b2[:, :], bcast(T["b2"])).then_inc(s_vec, 16)
            sp.dma_start(cbase[:, :], T["base_sel"]).then_inc(s_vec, 16)
            sp.wait_ge(s_zr, 1)
            sp.dma_start(upd_dram[2 * TOP:2 * TOP + 1, :], zrow[:, :]).then_inc(s_zs, 16)

            def load(q):
                for e in range(2):
                    src = xs_rows[bass.ds(q, 1), :, e].rearrange("o p h d -> (o p) h d")
                    sp.dma_start(sel[:, 2 * e:2 * e + 2, :], src).then_inc(s_sel, 16)

            def load_u(b, first):
                if not first:
                    sp.wait_ge(s_os, 16 * b)
                sp.dma_start(us[:, :, :], one(u_dram, b)).then_inc(s_ul, 16)

            def store(b):
                sp.wait_ge(s_o, NT * b + NT)
                sp.dma_start(one(out, b), us[:, :, :]).then_inc(s_os, 16)

            load(0)

            def body(q, first, last):
                if not last:
                    sp.wait_ge(ffn.s_t, NT * q + NT)
                    load(q + 1)
                if not first:
                    for e in range(2):
                        load_u(2 * q - 2 + e, isinstance(q, int) and q == 1 and e == 0)
                        store(2 * q - 2 + e)
                sp.wait_ge(s_u, NT * q + NT)
                sp.dma_start(upd_rows, upd[:, :, :])\
                  .then_inc(s_us, 16)

            loop(sp, body)
            for e in range(2):
                load_u(NB - 2 + e, False)
                store(NB - 2 + e)
            sp.wait_ge(s_os, 16 * NB)

        @block.gpsimd
        def _(pool):
            pool.wait_ge(s_zs, 16)

            def gather(b, q, first):
                pool.wait_ge(s_us, 16 * q + 16)
                pool.wait_ge(s_ix, 2 * b + 2)
                if not first:
                    pool.wait_ge(s_o, NT * b)
                pool.sem_inc(s_go, 1)
                for t in range(NT):
                    pool.indirect_dma_start(gat[:, t, :], None, upd_dram[:, :],
                                            bass.IndirectOffsetOnAxis(ap=idxb[:, t:t + 1], axis=0))\
                        .then_inc(s_gat, 16)

            def body(q, first, last):
                if not first:
                    for e in range(2):
                        gather(2 * q - 2 + e, q - 1, isinstance(q, int) and q == 1 and e == 0)

            loop(pool, body)
            for e in range(2):
                gather(NB - 2 + e, NPAIR - 1, False)

        @block.scalar
        def _(act):
            nc.scalar.activation(weight[:, :], score[:, :], ACT.Sigmoid).then_inc(s_wt, 1)
            for t in range(NT):
                ffn.input_hi(act, 0, t)
            act.wait_ge(s_vec, 48)

            def body(q, first, last):
                for f in range(NFM):
                    ffn.activate(act, q, f)
                if not last:
                    for t in range(NT):
                        ffn.input_hi(act, q + 1, t)

            loop(act, body)

        @block.vector
        def _(dve):
            ffn.prime(dve)
            nc.vector.memset(zrow[:, :], 0.0).then_inc(s_zr, 1)
            dve.wait_ge(s_vec, 48)
            nc.vector.tensor_scalar(issel[:, :], rank[:, :], float(TOP), None, ALU.is_lt).then_inc(s_idx, 1)
            nc.vector.tensor_tensor(t1[:, :], rank[:, :], cbase[:, :], ALU.add).then_inc(s_idx, 1)
            dve.wait_ge(s_idx, 2)
            nc.vector.tensor_tensor(t2[:, :], t1[:, :], issel[:, :], ALU.mult).then_inc(s_idx, 1)
            dve.wait_ge(s_idx, 3)
            nc.vector.tensor_scalar(idx[:, :], t2[:, :], float(2 * TOP), None, ALU.add).then_inc(s_idx, 1)
            dve.wait_ge(s_idx, 4)
            dve.wait_ge(s_wt, 1)
            for t in range(NT):
                ffn.input_lo(dve, 0, t)

            def pick(b, first):
                if not first:
                    dve.wait_ge(s_gat, 16 * NT * b)
                    dve.wait_ge(s_o, NT * b)
                nc.vector.tensor_copy(idxb[:, :], idx[:, bass.ds(NT * b, NT)]).then_inc(s_ix, 1)
                nc.vector.tensor_copy(wtb[:, :], weight[:, bass.ds(NT * b, NT)]).then_inc(s_ix, 1)

            def finish(b):
                dve.wait_ge(s_ix, 2 * b + 2)
                dve.wait_ge(s_gat, 16 * NT * b + 16 * NT)
                dve.wait_ge(s_ul, 16 * b + 16)
                for t in range(NT):
                    nc.vector.scalar_tensor_tensor(us[:, t, :], gat[:, t, :], wtb[:, t:t + 1], us[:, t, :],
                                                   ALU.mult, ALU.add).then_inc(s_o, 1)

            def body(q, first, last):
                for f in range(NFM):
                    if not first:
                        if f in (0, 8):
                            pick(2 * q - 2 + f // 8, isinstance(q, int) and q == 1 and f == 0)
                        if f in (5, 13):
                            finish(2 * q - 2 + f // 8)
                    ffn.hidden_lo(dve, q, f)
                if not last:
                    for t in range(NT):
                        ffn.input_lo(dve, q + 1, t)
                dve.wait_ge(ffn.s_down, NFM * q + NFM + 2)
                if not first:
                    dve.wait_ge(s_us, 16 * q)
                for t in range(NT):
                    nc.vector.tensor_tensor(upd[:, t, :], ffn.acc[t][:, :], b2[:, :], ALU.add).then_inc(s_u, 1)
                dve.wait_ge(s_u, NT * q + NT)
                dve.sem_inc(ffn.s_acc, 1)

            loop(dve, body)
            for e in range(2):
                pick(NB - 2 + e, False)
                finish(NB - 2 + e)

        @block.tensor
        def _(pe):
            def transpose(n, t):
                if t == 0:
                    pe.wait_ge(s_sel, 32 * n + 32)
                ffn.transpose(pe, sel[:, t, :], ident, t)

            for t in range(NT):
                if t >= 2:
                    pe.wait_ge(ffn.s_xT, t - 1)
                transpose(0, t)

            def body(q, first, last):
                for f in range(NFM):
                    ffn.up_product(pe, q, f)
                    if f >= 2:
                        ffn.down_product(pe, q, f - 2)
                if not last:
                    transpose(q + 1, 0)
                    transpose(q + 1, 1)
                ffn.down_product(pe, q, NFM - 2)
                if not last:
                    for t in (2, 3):
                        pe.wait_ge(ffn.s_xT, NT * q + NT + t - 1)
                        transpose(q + 1, t)
                ffn.down_product(pe, q, NFM - 1)

            loop(pe, body)


def program(nc, T, out):
    gpad = nc.dram_tensor("gpad", [GROWS, D], F32, kind="Internal").ap()
    zhi = nc.dram_tensor("zhi", [ZROWS, D], F32, kind="Internal").ap()
    zlo = nc.dram_tensor("zlo", [ZROWS, D], F32, kind="Internal").ap()
    y_dram = nc.dram_tensor("y_mid", [NB, S, D], F32, kind="Internal").ap()
    u_dram = nc.dram_tensor("u_mid", [NB, S, D], F32, kind="Internal").ap()
    xs_dram = nc.dram_tensor("rows_by_rank", [NB * S, D], F32, kind="Internal").ap()
    upd_dram = nc.dram_tensor("updates", [2 * TOP + 1, D], F32, kind="Internal").ap()
    with ExitStack() as ctx:
        def sb(n, shape, dt=F32):
            return ctx.enter_context(nc.sbuf_tensor(n, shape, dt))

        ident = sb("ident", [P, P])
        values = (-0.5, EPS, 0.0, -1.0 / D, 1.0 / D)
        const = sb("constants", [P, len(values), NT])
        with nc.semaphore("ident_loaded") as s_id, nc.semaphore("const_done") as s_c, nc.Block() as block:
            @block.sync
            def _(sp):
                sp.dma_start(ident[:, :], T["ident"]).then_inc(s_id, 16)
                sp.wait_ge(s_id, 16)

            @block.vector
            def _(dve):
                for k, v in enumerate(values):
                    nc.vector.memset(const[:, k, :], v).then_inc(s_c, 1)
                dve.wait_ge(s_c, len(values))
        context(nc, T, zhi, zlo, const)
        with ExitStack() as gctx:
            G1 = gctx.enter_context(nc.sbuf_tensor("G1", [P, 2, NP, D], F32))
            G2 = gctx.enter_context(nc.sbuf_tensor("G2", [P, 2, NP, D], F32))
            filters(nc, T, G1, G2, gpad)
            stage_a(nc, T, G1, G2, zhi, zlo, y_dram, ident[:, :], const)
        rank = sb("rank", [P, NB * NT])
        score = sb("score", [P, NB * NT])
        with ExitStack() as bctx:
            tri = bctx.enter_context(nc.sbuf_tensor("tri", [P, (NT - 1) * P + S], F32))
            base = bctx.enter_context(nc.sbuf_tensor("base", [P, NB * NT], F32))
            with nc.semaphore("tri_loaded") as s_id, nc.Block() as block:
                @block.sync
                def _(sp):
                    sp.dma_start(tri[:, :], T["tri"]).then_inc(s_id, 16)
                    sp.dma_start(base[:, :], T["base_all"]).then_inc(s_id, 16)
                    sp.wait_ge(s_id, 32)
            stage_b(nc, T, y_dram, u_dram, xs_dram, ident[:, :], const, tri, base, rank, score)
        stage_c(nc, T, u_dram, xs_dram, upd_dram, out, ident[:, :], rank, score)


_INS = {'x': 'x', 'ctx_1024': 'ctxT', 'L0_xattn_pe': 'peT', 'L0_xattn_W_in': 'W_in', 'L0_xattn_b_in': 'b_in',
        'L0_xattn_g_ln': 'g_ln', 'L0_xattn_beta_ln': 'beta_ln', 'L0_xattn_Wp1': 'Wp1', 'L0_xattn_bp1': 'bp1',
        'L0_xattn_Wp2': 'Wp2', 'L0_xattn_bp2': 'bp2', 'L0_xattn_a': 'a', 'L0_xattn_g1': 'g1',
        'L0_xattn_be1': 'be1', 'L0_xattn_W1a': 'W1a', 'L0_xattn_b1a': 'b1a', 'L0_xattn_W1b': 'W1b',
        'L0_xattn_b1b': 'b1b', 'L0_xattn_g2': 'g2', 'L0_xattn_be2': 'be2', 'L0_xattn_W2a': 'W2a',
        'L0_xattn_b2a': 'b2a', 'L0_xattn_W2b': 'W2b', 'L0_xattn_b2b': 'b2b', 'L0_ffn_w_router': 'w_router',
        'L0_ffn_W1': 'W1', 'L0_ffn_b1': 'b1', 'L0_ffn_W2': 'W2', 'L0_ffn_b2': 'b2'}


_COLUMNS = ("bp1", "g1", "be1", "b1a", "g2", "be2", "b2a", "b1")


def _constants(np):
    k, n = np.arange(64), np.arange(P)
    angle = np.pi * np.outer(n, 2 * k + 1) / P
    cos, sin = np.cos(angle), np.sin(angle)
    c = {"dft_g": np.concatenate([cos, -sin], 1)}
    fz = np.zeros((P, 4, P))
    for ph in range(2):
        rows = np.arange(ph, CTX, 2)
        j = np.arange(len(rows))
        fz[rows, 2 * ph] = np.concatenate([cos[j], cos[j]], 1)
        fz[rows, 2 * ph + 1] = np.concatenate([sin[j], -sin[j]], 1)
    c["dft_z"] = fz.reshape(P, 4 * P)
    inv = np.zeros((P, 4, P))
    for t in range(2):
        for m, p in enumerate(PIECES[t]):
            end = EDGES[p + 1]
            for col in range(P):
                u = t * P + col
                if EDGES[p] <= u < end:
                    at = u - EDGES[p] + HALO
                    inv[:64, 2 * t + m, col] = cos[at] / 64
                    inv[64:, 2 * t + m, col] = -sin[at] / 64
    c["dft_inv"] = inv.reshape(P, 4 * P)
    c["negl"] = -(np.arange(L // P)[None, :] * P + n[:, None])
    c["ident"] = np.eye(P)
    c["tri"] = (np.arange((NT - 1) * P + S)[None, :] < (NT - 1) * P + n[:, None])
    b = np.repeat(np.arange(NB), NT)[None, :]
    c["base_all"] = np.repeat(b * S, P, 0)
    c["base_sel"] = np.repeat((b % 2) * TOP - 2 * TOP, P, 0)
    return {name: np.ascontiguousarray(v, dtype=np.float32) for name, v in c.items()}


def kernel(**inputs):
    import numpy as _np
    import concourse.bacc as _bacc
    from concourse import mybir as _mybir
    from concourse.bass_utils import run_bass_kernel_spmd as _run

    nc = _bacc.Bacc("TRN2", target_bir_lowering=False, num_devices=1)
    arrays, T = {}, {}
    for name, short in _INS.items():
        a = _np.asarray(inputs[name])
        if short == "ctxT":
            a = a.reshape(ZROWS, D).T
        if short == "peT":
            a = a.T
        if short in _COLUMNS:
            a = a.reshape(-1, P).T
        arrays[f"in_{short}"] = _np.ascontiguousarray(a)
    for short, a in _constants(_np).items():
        arrays[f"in_{short}"] = a
    for full, a in arrays.items():
        T[full[3:]] = nc.dram_tensor(full, a.shape, _mybir.dt.from_np(a.dtype), kind="ExternalInput").ap()
    out = nc.dram_tensor("out_0", (NB, S, D), _mybir.dt.float32, kind="ExternalOutput").ap()
    program(nc, T, out)
    r = _run(nc, [arrays], core_ids=[0])
    return r.results[0]["out_0"]
```

```python
from contextlib import ExitStack

import concourse.bass as bass
from concourse import mybir

ALU = mybir.AluOpType
ACT = mybir.ActivationFunctionType
F32 = mybir.dt.float32
F32R = mybir.dt.float32r
I32 = mybir.dt.int32
U32 = mybir.dt.uint32

P = 128
EPS = 1e-5
D = 512
KC = D // P
NB, S = 16, 512
NT = S // P
F = 1024
NF = F // P
FM = 2048
NFM = FM // P
CTX = 77
ZROWS = NB * CTX
ZT = -(-ZROWS // P)
L = 1024
DP = 128
H = DP + D
KH = H // P
TOP = S // 2
HALO = (CTX - 1) // 2
EDGES = [0, 86, 172, 256, 342, 428]
NP = len(EDGES)
PIECES = [(0, 1), (1, 2), (3, 4), (4, 5)]
PAD = 2 * HALO + 2
GROWS = 2 * (EDGES[-1] + P) + PAD
DH = D // 2


class LayerNorm:

    def __init__(self, nc, sb, sem, name, const):
        self.nc, self.const = nc, const
        self.stats = sb(name + "_stats", [P, NT, 6])
        self.mv = sb(name + "_mv", [P, NT, 2])
        self.veps = sb(name + "_veps", [P, NT])
        self.rstd = sb(name + "_rstd", [P, NT])
        self.s_stats = sem(name + "_stats_done")
        self.s_seen = sem(name + "_stats_seen")
        self.s_mv = sem(name + "_mean_var_done")
        self.s_veps = sem(name + "_veps_done")
        self.s_rstd = sem(name + "_rstd_done")
        self.prod = sb(name + "_prod", [P, NT])
        self.shift = sb(name + "_shift", [P, NT])
        self.s_prod = sem(name + "_mean_times_rstd")
        self.s_shift = sem(name + "_shift_done")

    def dve(self, dve, x, n):
        for t in range(NT):
            self.nc.vector.bn_stats(self.stats[:, t, :], x[:, t, :]).then_inc(self.s_stats, 1)
        dve.wait_ge(self.s_stats, NT * n + NT)
        dve.sem_inc(self.s_seen, 1)
        for t in range(NT):
            self.nc.vector.bn_aggr(self.mv[:, t, :], self.stats[:, t, :]).then_inc(self.s_mv, 1)

    def pool(self, pool, n, shift=False):
        pool.wait_ge(self.s_mv, NT * n + NT)
        self.nc.gpsimd.tensor_tensor(self.veps[:, :], self.mv[:, :, 1], self.const[:, 1, :],
                                     ALU.add).then_inc(self.s_veps, 1)
        pool.wait_ge(self.s_veps, n + 1)
        self.nc.gpsimd.tensor_tensor(self.rstd[:, :], self.veps[:, :], self.const[:, 0, :],
                                     ALU.pow).then_inc(self.s_rstd, 1)
        if shift:
            pool.wait_ge(self.s_rstd, n + 1)
            self.nc.gpsimd.tensor_tensor(self.prod[:, :], self.mv[:, :, 0], self.rstd[:, :], ALU.mult)\
                .then_inc(self.s_prod, 1)
            pool.wait_ge(self.s_prod, n + 1)
            self.nc.gpsimd.tensor_tensor(self.shift[:, :], self.const[:, 2, :], self.prod[:, :],
                                         ALU.subtract).then_inc(self.s_shift, 1)


class SecondLayerNorm:

    def __init__(self, nc, sb, sem, name, const):
        self.nc, self.const = nc, const
        self.sum = sb(name + "_sum", [P, NT])
        self.mean = sb(name + "_minus_mean", [P, NT])
        self.sq = sb(name + "_sq", [P, NT])
        self.var = sb(name + "_var", [P, NT])
        self.veps = sb(name + "_veps", [P, NT])
        self.rstd = sb(name + "_rstd", [P, NT])
        self.shift = sb(name + "_shift", [P, NT])
        self.s_mean = sem(name + "_mean_done")
        self.s_sq = sem(name + "_squares_done")
        self.s_step = sem(name + "_steps")
        self.s_rstd = sem(name + "_shift_done")

    def pool_mean(self, pool, n, s_sum):
        pool.wait_ge(s_sum, NT * n + NT)
        self.nc.gpsimd.tensor_tensor(self.mean[:, :], self.sum[:, :], self.const[:, 3, :], ALU.mult)\
            .then_inc(self.s_mean, 1)

    def pool_rstd(self, pool, n):
        pool.wait_ge(self.s_sq, NT * n + NT)
        self.nc.gpsimd.tensor_tensor(self.var[:, :], self.sq[:, :], self.const[:, 4, :], ALU.mult)\
            .then_inc(self.s_step, 1)
        pool.wait_ge(self.s_step, 3 * n + 1)
        self.nc.gpsimd.tensor_tensor(self.veps[:, :], self.var[:, :], self.const[:, 1, :], ALU.add)\
            .then_inc(self.s_step, 1)
        pool.wait_ge(self.s_step, 3 * n + 2)
        self.nc.gpsimd.tensor_tensor(self.rstd[:, :], self.veps[:, :], self.const[:, 0, :], ALU.pow)\
            .then_inc(self.s_step, 1)
        pool.wait_ge(self.s_step, 3 * n + 3)
        self.nc.gpsimd.tensor_tensor(self.shift[:, :], self.mean[:, :], self.rstd[:, :], ALU.mult)\
            .then_inc(self.s_rstd, 1)


def bcast(vec, n=P):
    return vec.rearrange("(a n) -> a n", a=1).broadcast_to([n, vec.shape[0]])


class Halves:

    def __init__(self, nc, sem, name, src, hi, lo, raw, scale=None, parts=1):
        self.nc, self.src, self.hi, self.lo, self.raw, self.scale, self.parts = nc, src, hi, lo, raw, scale, parts
        self.K = hi.shape[1]
        self.s_raw = [sem(f"{name}_loaded{n}") for n in range(parts)]
        self.s_hi = sem(f"{name}_hi_done")
        self.s_lo = sem(f"{name}_split")

    def load(self, sp, parts=None):
        n = self.K // self.parts
        src = self.src if len(self.src.shape) > 2 else self.src.rearrange("(k p) n -> p k n", p=P)
        for j in range(self.parts) if parts is None else parts:
            at = slice(j * n, (j + 1) * n) if n > 1 else j
            sp.dma_start(self.raw[:, at], src[:, at]).then_inc(self.s_raw[j], 16)

    def loaded(self, eng, k):
        eng.wait_ge(self.s_raw[k * self.parts // self.K], 16)

    def split_hi(self, act, k):
        self.loaded(act, k)
        scale = {} if self.scale is None else {"scale": self.scale[:, k:k + 1]}
        self.nc.scalar.activation(self.hi[:, k], self.raw[:, k], ACT.Copy, **scale).then_inc(self.s_hi, 1)

    def split_lo(self, dve, k):
        dve.wait_ge(self.s_hi, k + 1)
        hi = self.hi[:, k].bitcast(F32)
        if self.scale is None:
            op = self.nc.vector.tensor_tensor(self.lo[:, k], self.raw[:, k], hi, ALU.subtract)
        else:
            op = self.nc.vector.scalar_tensor_tensor(self.lo[:, k], self.raw[:, k], self.scale[:, k:k + 1],
                                                     hi, ALU.mult, ALU.subtract)
        op.then_inc(self.s_lo, 1)


def normalise(nc, x, t, ln0, ln1, s_xn):
    nc.scalar.activation(x[:, t, :], x[:, t, :], ACT.Identity, bias=ln0.shift[:, t:t + 1],
                         scale=ln0.rstd[:, t:t + 1], accum_out=ln1.sum[:, t:t + 1]).then_inc(s_xn, 1)


def square(nc, x, t, out, ln1):
    nc.scalar.activation(out, x[:, t, :], ACT.Square, bias=ln1.mean[:, t:t + 1],
                         accum_out=ln1.sq[:, t:t + 1]).then_inc(ln1.s_sq, 1)


def bias_chunk(pe, out, raw, beta, k):
    for h in range(2):
        last = pe.matmul(out[h][0:1, :], beta[:, k:k + 1], raw[:, h * 512:(h + 1) * 512],
                         start=(k == 0), stop=(k == KC - 1), skip_group_check=True)
    return last


def passes(a_hi, a_lo, b_hi, b_lo):
    return ((a_hi, b_hi), (a_lo, b_hi), (a_hi, b_lo))


def product(pe, out, terms):
    pairs = [p for t in terms for p in passes(*t)]
    for n, (a, b) in enumerate(pairs):
        last = pe.matmul(out, a, b, start=(n == 0), stop=(n == len(pairs) - 1))
    return last


def cut3(flat, at, k, n):
    return flat[:, at:at + k * n].rearrange("p (k n) -> p k n", k=k)


class Place:

    def __init__(self, nc, ctx, name, n, at=None):
        if at is None:
            at = -(-nc.sbuf_base // 32) * 32
            self.split = ctx.enter_context(nc.sbuf_tensor(name, [P, n], F32R))
        else:
            self.split = nc.alloc_sbuf_tensor_at(name, [P, n], F32R, offset=at)
        self.raw = nc.alloc_sbuf_tensor_at(f"{name}_raw", [P, n], F32, offset=at)
        self.at = at

    def halves(self, at, k, n):
        hi, lo = (slice(at + h * k * n, at + (h + 1) * k * n) for h in range(2))
        return [t.rearrange("p (k n) -> p k n", k=k) for t in (self.split[:, hi], self.split[:, lo], self.raw[:, lo])]


def setup(nc, T, weights, spectra, tables, b1, zhi, zlo, gpad, const, s_g2, X0, s_x0,
          b_cols, s_bcols, ln0, ln1, s_xn, bias_dram, s_bst):
    with ExitStack() as ctx:
        ctx.enter_context(nc.cleanup_on_exit())
        def sb(n, shape, dt=F32):
            return ctx.enter_context(nc.sbuf_tensor(f"set_{n}", shape, dt))

        def sem(n):
            return nc.alloc_semaphore(name=f"set_{n}")

        net = Place(nc, None, "set_network", 2 * (KH * D + H + L), spectra.at)
        wp2 = net.halves(0, KH, D)
        wp1 = net.halves(2 * KH * D, 1, H)
        pet = net.halves(2 * KH * D + 2 * H, 1, L)
        ct = weights.halves(0, KC, ZROWS)
        win = weights.halves(2 * KC * ZROWS, KC, D)
        dft = Place(nc, ctx, "set_dft", 2 * P).halves(0, 1, P)
        fz, inv = stage_a_tables(tables)
        w1, w2 = ffn_weights(weights)
        G1, G2 = (spectra.raw[:, n * 2 * NP * D:(n + 1) * 2 * NP * D] for n in range(2))
        g1c, be1c, b1c = (sb(n, [P, KC if n != "b1c" else NF]) for n in ("g1c", "be1c", "b1c"))
        m_wp1 = Halves(nc, sem, "wp1", T["Wp1"], *wp1)
        m_pet = Halves(nc, sem, "positions", T["peT"], *pet)
        m_wp2 = Halves(nc, sem, "wp2", T["Wp2"], *wp2)
        m_win = Halves(nc, sem, "w_in", T["W_in"], *win)
        m_ct = Halves(nc, sem, "context", T["ctxT"], *ct, parts=KC)
        m_dft = Halves(nc, sem, "dft_g", T["dft_g"], *dft)
        m_fz = Halves(nc, sem, "dft_z", T["dft_z"], *fz)
        m_inv = Halves(nc, sem, "dft_inv", T["dft_inv"], *inv)
        m_w1 = Halves(nc, sem, "w1a", T["W1a"], *w1, scale=g1c, parts=2)
        m_w2 = Halves(nc, sem, "w1b", T["W1b"], *w2, parts=4)
        place = Place(nc, ctx, "set_hidden", 2 * KH * L)
        hp = place.halves(0, KH, L)
        w2a = [place.raw[:, c * L:c * L + F] for c in (3, 4, KH + 3, KH + 4)]
        s_w2a = [sem(f"w2a_loaded{k}") for k in range(KC)]
        bp1 = sb("bp1", [P, KH])
        bp2 = sb("bp2", [P, D])
        negl = sb("negl", [P, L // P])
        a_col = sb("a", [P, 1])
        ea = sb("ea", [P, 1])
        arg = sb("arg", [P, L // P])
        win_l = sb("window", [P, L // P])
        RW = 4
        wh = sb("wh", [P, RW, D])
        zero = sb("zero", [P, D])
        R = 4
        RG = 6
        gh, gl, gin = (t[:, 0:3, :].rearrange("p k (a d) -> p (k a) d", d=D) for t in hp)
        vec = {n: sb(n, [P, D]) for n in ("b_in", "g_ln", "beta_ln")}
        RZ = 3
        z0 = sb("z0", [P, 2, D])
        zh = sb("zh", [P, RZ, D], F32R)
        zl = sb("zl", [P, RZ, D], F32R)
        z1 = zl[:, :, :].bitcast(F32)
        stats = sb("stats", [P, 2, 6])
        mv = sb("mv", [P, 2, 2])
        veps = sb("veps", [P, 2])
        rstd = sb("rstd", [P, 2])
        ps = [ctx.enter_context(nc.psum_tensor(f"set_ps{n}", [P, D], F32)) for n in range(R)]
        zps = [ctx.enter_context(nc.psum_tensor(f"set_zps{n}", [P, D], F32)) for n in range(2)]
        bias_row = [[z0[0:1, h, :] for h in range(2)], [vec[n][0:1, :] for n in ("b_in", "g_ln")]]
        bps = [ctx.enter_context(nc.psum_tensor(f"set_bps{n}", [P, D], F32)) for n in range(2)]
        s_bp2 = sem("filter_bias_loaded")
        s_in, s_vec = sem("filter_vectors_loaded"), sem("context_vectors_loaded")
        s_cols = sem("columns_loaded")
        s_ea, s_arg, s_win = sem("exp_a_done"), sem("arg_done"), sem("window_done")
        s_hid, s_silu, s_hhi, s_hlo = sem("hidden_done"), sem("silu_done"), sem("hidden_hi_done"), sem("hidden_lo_done")
        s_row, s_bias, s_wh = sem("filter_done"), sem("filter_bias_added"), sem("windowed_done")
        s_st = [sem(f"windowed_stored{n}") for n in range(RW)]
        s_zero, s_pad = sem("zero_done"), sem("pads_stored")
        s_gin = [sem(f"piece_loaded{n}") for n in range(RG)]
        s_ghi, s_glo, s_spec, s_g1 = sem("piece_hi_done"), sem("piece_lo_done"), sem("spectrum_done"), sem("g1_done")
        s_mm, s_z0 = sem("z_product_done"), sem("z_bias_added")
        s_zstat, s_mv = sem("z_stats_done"), sem("z_mean_var_done")
        s_veps, s_rstd, s_n = sem("veps_done"), sem("rstd_done"), sem("z_normalised")
        s_gb = sem("z_scale_shift_steps")
        s_zhi, s_zlo = sem("z_hi_done"), sem("z_lo_done")
        s_zst = [sem(f"z_stored{n}") for n in range(RZ)]
        s_b, s_brow = sem("bias_chunk_done"), sem("bias_row_copied")
        s_bcol, s_bout = sem("bias_column_loaded"), sem("bias_done")
        bias_col = sb("bias_col", [P, NF])
        assert nc.sbuf_base <= nc.sbuf_top - 1 * NT * D * 4
        block = ctx.enter_context(nc.Block())
        HID = [(f, m) for f in range(KH) for m in range(L // 512)]
        NH = len(HID)
        LT = L // P
        PC = [(ph, p) for p in range(NP) for ph in range(2)]
        rows = [min(P, ZROWS - n * P) for n in range(ZT)]

        def store_windowed(sp, m):
            sp.wait_ge(s_wh, m + 1)
            sp.dma_start(gpad[PAD + m * P:PAD + (m + 1) * P, :], wh[:, m % RW, :]).then_inc(s_st[m % RW], 16)

        def store_bias(sp, c):
            sp.wait_ge(s_brow, 2 * c + 2)
            for h in range(2):
                sp.dma_start(bias_dram[c:c + 1, h * 512:(h + 1) * 512], bias_row[c][h]).then_inc(s_bst[c], 16)

        def swap(sp, q):
            sp.wait_ge(s_g1, 4 * q + 4)
            cut = slice(4 * q * D, (4 * q + 4) * D)
            sp.dma_start(G2[0:64, cut], G1[64:P, cut]).then_inc(s_g2, 16)
            sp.dma_start(G2[64:P, cut], G1[0:64, cut]).then_inc(s_g2, 16)

        @block.sync
        def _(sp):
            m_wp1.load(sp)
            m_pet.load(sp)
            sp.dma_start(bp1[:, :], T["bp1"]).then_inc(s_in, 16)
            sp.dma_start(negl[:, :], T["negl"]).then_inc(s_in, 16)
            sp.dma_start(a_col[:, :], bcast(T["a"])).then_inc(s_in, 16)
            m_win.load(sp)
            m_ct.load(sp)
            for n in vec:
                sp.dma_start(vec[n][:, :], bcast(T[n])).then_inc(s_vec, 16)
            m_wp2.load(sp)
            sp.dma_start(bp2[:, :], bcast(T["bp2"])).then_inc(s_bp2, 16)
            for m in (m_dft, m_fz, m_inv):
                m.load(sp)
            sp.dma_start(g1c[:, :], T["g1"]).then_inc(s_cols, 16)
            sp.dma_start(be1c[:, :], T["be1"]).then_inc(s_cols, 16)
            sp.dma_start(b1c[:, :], T["b1a"]).then_inc(s_cols, 16)
            for n, v in enumerate(("g2", "be2", "b2a")):
                sp.dma_start(b_cols[n][:, :], T[v]).then_inc(s_bcols, 16)
            sp.dma_start(X0[:, :, :], T["x"].rearrange("b (t p) d -> b p t d", p=P)[0]).then_inc(s_x0, 16)
            sp.wait_ge(s_zero, 1)
            sp.dma_start(gpad[0:PAD, :], zero[0:PAD, :]).then_inc(s_pad, 16)
            tail = GROWS - PAD - L
            sp.dma_start(gpad[PAD + L:GROWS, :], zero[0:tail, :]).then_inc(s_pad, 16)
            for n in range(ZT):
                sp.wait_ge(s_zlo, n + 1)
                r = rows[n]
                sp.dma_start(zhi[n * P:n * P + r, :], zh[0:r, n % RZ, :].bitcast(F32)).then_inc(s_zst[n % RZ], 16)
                sp.dma_start(zlo[n * P:n * P + r, :], zl[0:r, n % RZ, :].bitcast(F32)).then_inc(s_zst[n % RZ], 16)
            sp.wait_ge(s_mm, ZT)
            m_w1.load(sp)
            for m in range(LT):
                store_windowed(sp, m)
                if m % 2:
                    m_w2.load(sp, (m // 2,))
            sp.wait_ge(s_pad, 32)
            for n in range(RW):
                sp.wait_ge(s_st[n], 16 * (LT // RW))
            sp.wait_ge(s_row, LT)
            for n, (ph, p) in enumerate(PC):
                if n >= RG:
                    sp.wait_ge(s_spec, n - RG + 1)
                r = 2 * EDGES[p] + 2 - ph
                sp.dma_start(gin[:, n % RG, :], gpad[r:r + 2 * P - 1:2, :]).then_inc(s_gin[n % RG], 16)
                if n in (3, 4, 5, 6):
                    sp.dma_start(w2a[n - 3], T["W2a"][(n - 3) * P:(n - 2) * P, :]).then_inc(s_w2a[n - 3], 16)
                if n == 8:
                    store_bias(sp, 0)
                if n == 10:
                    sp.wait_ge(s_bst[0], 32)
                    sp.dma_start(bias_col[:, :], bias_dram[0].rearrange("(f p) -> p f", p=P),
                                 allow_slow_non_contiguous=True).then_inc(s_bcol, 16)
                if n in (7, 11):
                    swap(sp, n // 4 - 1)
            store_bias(sp, 1)
            swap(sp, 2)
            for n in range(RZ):
                sp.wait_ge(s_zst[n], 32 * len(range(n, ZT, RZ)))

        @block.gpsimd
        def _(pool):
            pool.wait_ge(s_vec, 48)

            def power(n):
                r, k = rows[n], n % 2
                pool.wait_ge(s_mv, n + 1)
                nc.gpsimd.tensor_scalar(veps[0:r, k:k + 1], mv[0:r, k, 1:2], 1.0, EPS, ALU.mult, ALU.add)\
                  .then_inc(s_veps, 1)
                pool.wait_ge(s_veps, n + 1)
                nc.gpsimd.tensor_tensor(rstd[0:r, k:k + 1], veps[0:r, k:k + 1], const[0:r, 0, 0:1], ALU.pow)\
                  .then_inc(s_rstd, 1)

            def affine(n):
                r, at = rows[n], z1[0:rows[n], n % RZ, :]
                pool.wait_ge(s_n, n + 1)
                nc.gpsimd.tensor_tensor(at, at, vec["g_ln"][0:r, :], ALU.mult).then_inc(s_gb, 1)
                pool.wait_ge(s_gb, 2 * n + 1)
                nc.gpsimd.tensor_tensor(at, at, vec["beta_ln"][0:r, :], ALU.add).then_inc(s_gb, 1)

            for n in range(ZT + 1):
                if n < ZT:
                    power(n)
                if n >= 1:
                    affine(n - 1)
            ln0.pool(pool, 0, shift=True)
            ln1.pool_mean(pool, 0, s_xn)
            ln1.pool_rstd(pool, 0)

        @block.scalar
        def _(act):
            m_wp1.split_hi(act, 0)
            m_pet.split_hi(act, 0)
            act.wait_ge(s_in, 48)
            nc.scalar.activation(ea[:, :], a_col[:, :], ACT.Exp).then_inc(s_ea, 1)
            act.wait_ge(s_arg, 1)
            nc.scalar.activation(win_l[:, :], arg[:, :], ACT.Exp).then_inc(s_win, 1)

            def hidden(n):
                f, m = HID[n]
                act.wait_ge(s_hid, n + 1)
                nc.scalar.activation(ps[n % R][:, :], ps[n % R][:, :], ACT.Silu,
                                     bias=bp1[:, f:f + 1]).then_inc(s_silu, 1)
                act.wait_ge(s_silu, n + 1)
                nc.scalar.activation(hp[0][:, f, m * 512:(m + 1) * 512], ps[n % R][:, :], ACT.Copy)\
                  .then_inc(s_hhi, 1)

            def z_hi(n):
                act.wait_ge(s_gb, 2 * n + 2)
                if n >= RZ:
                    act.wait_ge(s_zst[n % RZ], 32 * (n // RZ))
                nc.scalar.activation(zh[0:rows[n], n % RZ, :], z1[0:rows[n], n % RZ, :], ACT.Copy).then_inc(s_zhi, 1)

            for n in range(4):
                hidden(n)
            for k in range(KC):
                m_win.split_hi(act, k)
                m_ct.split_hi(act, k)
            for n in range(4, NH):
                hidden(n)
            for k in range(KH):
                m_wp2.split_hi(act, k)
            for m in (m_dft, m_fz, m_inv):
                m.split_hi(act, 0)
            for n in range(ZT):
                z_hi(n)
            act.wait_ge(s_win, 1)
            act.wait_ge(s_cols, 48)
            for m in range(LT):
                act.wait_ge(s_bias, m + 1)
                nc.scalar.activation(wh[:, m % RW, :], wh[:, m % RW, :], ACT.Copy, scale=win_l[:, m:m + 1])\
                  .then_inc(s_wh, 1)
                if m == 1:
                    act.wait_ge(ln0.s_shift, 1)
                    for t in range(NT):
                        normalise(nc, X0, t, ln0, ln1, s_xn)
                if m == 5:
                    act.wait_ge(s_xn, NT)
                    act.wait_ge(ln1.s_mean, 1)
                    act.wait_ge(s_pad, 32)
                    act.wait_ge(s_gb, 2 * ZT)
                    for t in range(NT):
                        if t >= 2:
                            act.wait_ge(ln1.s_sq, t - 1)
                        square(nc, X0, t, (zero, vec["beta_ln"])[t % 2][:, :], ln1)
            for k in range(KC):
                m_w1.split_hi(act, k)
            def g1_copy(n):
                act.wait_ge(s_spec, n + 1)
                nc.scalar.activation(G1[:, n * D:(n + 1) * D], ps[n % R][:, :], ACT.Copy).then_inc(s_g1, 1)

            for n in range(2 * NP):
                act.wait_ge(s_gin[n % RG], 16 * (n // RG + 1))
                nc.scalar.activation(gh[:, n % RG, :], gin[:, n % RG, :], ACT.Copy).then_inc(s_ghi, 1)
                if n >= 2 * NP - NF:
                    m_w2.split_hi(act, n - (2 * NP - NF))
                if n >= 2:
                    g1_copy(n - 2)
            g1_copy(2 * NP - 2)
            g1_copy(2 * NP - 1)

        @block.vector
        def _(dve):
            nc.vector.memset(zero[:, :], 0.0).then_inc(s_zero, 1)
            m_wp1.split_lo(dve, 0)
            m_pet.split_lo(dve, 0)
            dve.wait_ge(s_ea, 1)
            nc.vector.tensor_scalar(arg[:, :], negl[:, :], ea[:, 0:1], None, ALU.mult).then_inc(s_arg, 1)

            def hidden_lo(n):
                f, m = HID[n]
                dve.wait_ge(s_hhi, n + 1)
                nc.vector.tensor_tensor(hp[1][:, f, m * 512:(m + 1) * 512], ps[n % R][:, :],
                                        hp[0][:, f, m * 512:(m + 1) * 512].bitcast(F32),
                                        ALU.subtract).then_inc(s_hlo, 1)

            def z_stats(n):
                r, k = rows[n], n % 2
                dve.wait_ge(s_mm, n + 1)
                nc.vector.tensor_tensor(z0[0:r, k, :], zps[k][0:r, :], vec["b_in"][0:r, :], ALU.add).then_inc(s_z0, 1)
                dve.wait_ge(s_z0, n + 1)
                nc.vector.bn_stats(stats[0:r, k, :], z0[0:r, k, :]).then_inc(s_zstat, 1)
                dve.wait_ge(s_zstat, n + 1)
                nc.vector.bn_aggr(mv[0:r, k, :], stats[0:r, k, :]).then_inc(s_mv, 1)

            def z_normalise(n):
                r, k = rows[n], n % 2
                if n >= RZ:
                    dve.wait_ge(s_zst[n % RZ], 32 * (n // RZ))
                dve.wait_ge(s_rstd, n + 1)
                nc.vector.tensor_scalar(z1[0:r, n % RZ, :], z0[0:r, k, :], mv[0:r, k, 0:1], rstd[0:r, k:k + 1],
                                        ALU.subtract, ALU.mult).then_inc(s_n, 1)

            def z_lo(n):
                r = rows[n]
                dve.wait_ge(s_zhi, n + 1)
                nc.vector.tensor_tensor(zl[0:r, n % RZ, :], z1[0:r, n % RZ, :], zh[0:r, n % RZ, :].bitcast(F32),
                                        ALU.subtract).then_inc(s_zlo, 1)

            def row_bias(m):
                dve.wait_ge(s_row, m + 1)
                if m >= RW:
                    dve.wait_ge(s_st[m % RW], 16 * (m // RW))
                nc.vector.tensor_tensor(wh[:, m % RW, :], ps[m % R][:, :], bp2[:, :], ALU.add)\
                  .then_inc(s_bias, 1)

            for n in range(4):
                hidden_lo(n)
            for k in range(KC):
                m_win.split_lo(dve, k)
                m_ct.split_lo(dve, k)
            for n in range(4, NH):
                hidden_lo(n)
            dve.wait_ge(s_vec, 48)
            for n in range(ZT + 2):
                if n < ZT:
                    if n >= 2:
                        dve.wait_ge(s_n, n - 1)
                    z_stats(n)
                if 1 <= n <= ZT:
                    z_normalise(n - 1)
                if n >= 2:
                    z_lo(n - 2)
                if n < KH:
                    m_wp2.split_lo(dve, n)
                elif n < KH + 3:
                    (m_dft, m_fz, m_inv)[n - KH].split_lo(dve, 0)
                if n == KH + 3:
                    dve.wait_ge(s_x0, 16)
                    ln0.dve(dve, X0, 0)
                    dve.wait_ge(s_bp2, 16)
                if n >= ZT:
                    row_bias(2 * (n - ZT))
                    row_bias(2 * (n - ZT) + 1)
            for m in range(4, LT):
                row_bias(m)

            def copy_bias(c, banks):
                dve.wait_ge(s_b, KC * c + KC)
                if c == 0:
                    dve.wait_ge(s_n, ZT)
                else:
                    dve.wait_ge(s_gb, 2 * ZT)
                for h in range(2):
                    nc.vector.tensor_copy(bias_row[c][h], banks[h][0:1, :]).then_inc(s_brow, 1)

            for n in range(2 * NP):
                dve.wait_ge(s_ghi, n + 1)
                nc.vector.tensor_tensor(gl[:, n % RG, :], gin[:, n % RG, :], gh[:, n % RG, :].bitcast(F32),
                                        ALU.subtract).then_inc(s_glo, 1)
                if n >= 2 * NP - NF:
                    m_w2.split_lo(dve, n - (2 * NP - NF))
                if n == 5:
                    copy_bias(0, bps)
                if n == 11:
                    copy_bias(1, zps)
                if n in range(2, 2 + KC):
                    dve.wait_ge(s_b, n - 1)
                    m_w1.split_lo(dve, n - 2)
            dve.wait_ge(s_bcol, 16)
            nc.vector.tensor_tensor(b1[:, :], bias_col[:, :], b1c[:, :], ALU.add).then_inc(s_bout, 1)

        @block.tensor
        def _(pe):
            def hidden(n):
                f, m = HID[n]
                if n >= R:
                    pe.wait_ge(s_hlo, n - R + 1)
                cut = slice(m * 512, (m + 1) * 512)
                product(pe, ps[n % R][:, :], [(wp1[0][:, 0, f * P:(f + 1) * P], wp1[1][:, 0, f * P:(f + 1) * P],
                                               pet[0][:, 0, cut], pet[1][:, 0, cut])]).then_inc(s_hid, 1)

            pe.wait_ge(m_wp1.s_lo, 1)
            pe.wait_ge(m_pet.s_lo, 1)
            for n in range(NH):
                hidden(n)
            pe.wait_ge(m_win.s_lo, KC)
            pe.wait_ge(m_ct.s_lo, KC)
            for n in range(ZT):
                if n >= 2:
                    pe.wait_ge(s_z0, n - 1)
                r, at = rows[n], n * P
                product(pe, zps[n % 2][0:r, :], [(ct[0][:, k, at:at + r], ct[1][:, k, at:at + r],
                                                  win[0][:, k, :], win[1][:, k, :]) for k in range(KC)])\
                    .then_inc(s_mm, 1)
            pe.wait_ge(s_hlo, NH)
            pe.wait_ge(m_wp2.s_lo, KH)
            for m in range(LT):
                if m >= R:
                    pe.wait_ge(s_bias, m - R + 1)
                product(pe, ps[m % R][:, :], [(hp[0][:, f, m * P:(m + 1) * P], hp[1][:, f, m * P:(m + 1) * P],
                                               wp2[0][:, f, :], wp2[1][:, f, :]) for f in range(KH)])\
                    .then_inc(s_row, 1)
            pe.wait_ge(s_bias, LT)
            pe.wait_ge(m_dft.s_lo, 1)
            pe.wait_ge(s_cols, 48)
            pe.wait_ge(s_bcols, 48)
            pe.wait_ge(s_z0, ZT)

            def bias(c):
                k = c % KC
                if c < KC:
                    m_w1.loaded(pe, k)
                    bias_chunk(pe, bps, m_w1.raw[:, k], be1c, k).then_inc(s_b, 1)
                else:
                    pe.wait_ge(s_w2a[k], 16)
                    bias_chunk(pe, zps, w2a[k], b_cols[1], k).then_inc(s_b, 1)

            for c in range(KC):
                bias(c)
            for n in range(2 * NP):
                pe.wait_ge(s_glo, n + 1)
                if n >= R:
                    pe.wait_ge(s_g1, n - R + 1)
                product(pe, ps[n % R][:, :], [(dft[0][:, 0, :], dft[1][:, 0, :], gh[:, n % RG, :], gl[:, n % RG, :])])\
                    .then_inc(s_spec, 1)
                if n in (4, 6, 8, 9):
                    bias(KC + (4, 6, 8, 9).index(n))


class Ffn:

    def __init__(self, nc, ctx, name, nf, func, w1, w2, b1):
        def sb(n, shape, dt=F32):
            return ctx.enter_context(nc.sbuf_tensor(f"{name}_{n}", shape, dt))

        def sem(n):
            return nc.alloc_semaphore(name=f"{name}_{n}")

        self.nc, self.nf, self.func, self.w1, self.w2, self.b1 = nc, nf, func, w1, w2, b1
        self.xT = [sb(f"xT{h}", [P, KC, 512], F32R) for h in "hl"]
        self.hid = [sb(f"hid{h}", [P, 2, 512], F32R) for h in "hl"]
        self.acc = [ctx.enter_context(nc.psum_tensor(f"{name}_acc{t}", [P, D], F32)) for t in range(NT)]
        self.up = [ctx.enter_context(nc.psum_tensor(f"{name}_up{t}", [P, 512], F32)) for t in range(2)]
        self.side = [ctx.enter_context(nc.psum_tensor(f"{name}_side{t}", [P, 512], F32)) for t in range(2)]
        self.s_up = sem("hidden_product_done")
        self.s_act = sem("hidden_act_done")
        self.s_hi = sem("hidden_hi_done")
        self.s_hid = sem("hidden_split_primed")
        self.s_down = sem("hidden_used_primed")
        self.s_acc = sem("outputs_free_primed")
        self.s_sum = sem("output_tile_summed")
        self.s_t = sem("transposed")
        self.s_thi = sem("transposed_hi_done")
        self.s_xT = sem("input_ready")

    def prime(self, eng):
        eng.sem_inc(self.s_hid, 2)
        eng.sem_inc(self.s_down, 2)
        eng.sem_inc(self.s_acc, 1)

    def up_product(self, pe, u, f):
        if f == 0:
            pe.wait_ge(self.s_xT, NT * u + NT)
        pe.wait_ge(self.s_hid, self.nf * u + f + 1)
        cut = slice(f * P, (f + 1) * P)
        product(pe, self.up[f % 2][:, :], [(self.w1[0][:, k, cut], self.w1[1][:, k, cut],
                                            self.xT[0][:, k, :], self.xT[1][:, k, :]) for k in range(KC)])\
            .then_inc(self.s_up, 1)

    def down_product(self, pe, u, f):
        if f == 0:
            pe.wait_ge(self.s_acc, u + 1)
        pe.wait_ge(self.s_hid, self.nf * u + f + 3)
        for t in range(NT):
            cut = slice(t * P, (t + 1) * P)
            pairs = passes(self.hid[0][:, f % 2, cut], self.hid[1][:, f % 2, cut],
                           self.w2[0][:, f, :], self.w2[1][:, f, :])
            for n, (a, b) in enumerate(pairs):
                last = pe.matmul(self.acc[t][:, :], a, b, start=(f == 0 and n == 0),
                                 stop=(f == self.nf - 1 and n == 2), skip_group_check=True)
            if f == self.nf - 1 and t < NT - 1:
                last.then_inc(self.s_sum, 1)
        last.then_inc(self.s_down, 1)

    def transpose(self, pe, src, ident, t):
        for k in range(KC):
            last = pe.transpose(self.side[t % 2][:, k * P:(k + 1) * P], src[:, k * P:(k + 1) * P], ident)
        last.then_inc(self.s_t, 1)

    def activate(self, act, u, f):
        act.wait_ge(self.s_up, self.nf * u + f + 1)
        self.nc.scalar.activation(self.up[f % 2][:, :], self.up[f % 2][:, :], self.func,
                                  bias=self.b1[:, f:f + 1]).then_inc(self.s_act, 1)
        act.wait_ge(self.s_act, self.nf * u + f + 1)
        act.wait_ge(self.s_down, self.nf * u + f + 1)
        self.nc.scalar.activation(self.hid[0][:, f % 2, :], self.up[f % 2][:, :], ACT.Copy)\
            .then_inc(self.s_hi, 1)

    def input_hi(self, act, u, t):
        act.wait_ge(self.s_t, NT * u + t + 1)
        side = self.side[t % 2][:, :].rearrange("p (k n) -> p k n", k=KC)
        self.nc.scalar.activation(self.xT[0][:, :, t * P:(t + 1) * P], side, ACT.Copy).then_inc(self.s_thi, 1)

    def hidden_lo(self, dve, u, f):
        dve.wait_ge(self.s_hi, self.nf * u + f + 1)
        self.nc.vector.tensor_tensor(self.hid[1][:, f % 2, :], self.up[f % 2][:, :],
                                     self.hid[0][:, f % 2, :].bitcast(F32), ALU.subtract)\
            .then_inc(self.s_hid, 1)

    def output_summed(self, dve, u, t):
        if t < NT - 1:
            dve.wait_ge(self.s_sum, (NT - 1) * u + t + 1)
        else:
            dve.wait_ge(self.s_down, self.nf * u + self.nf + 2)

    def input_lo(self, dve, u, t):
        dve.wait_ge(self.s_thi, NT * u + t + 1)
        side = self.side[t % 2][:, :].rearrange("p (k n) -> p k n", k=KC)
        cut = slice(t * P, (t + 1) * P)
        self.nc.vector.tensor_tensor(self.xT[1][:, :, cut], side, self.xT[0][:, :, cut].bitcast(F32),
                                     ALU.subtract).then_inc(self.s_xT, 1)


def pairs_loop(eng, body, n):
    with eng.Fori(0, n - 1) as i:
        for par in range(2):
            body(2 * i + par, i, par, False)
    for par in range(2):
        body(2 * (n - 1) + par, n - 1, par, par == 1)


def ffn_weights(weights):
    return weights.halves(0, KC, F), weights.halves(2 * KC * F, NF, D)


def stage_a_tables(tables):
    return tables.halves(0, 1, 4 * P), tables.halves(8 * P, 1, 4 * P)


def stage_a(nc, T, weights, spectra, tables, b1, s_g2, X0, s_x0, X1, s_ys, zhi, zlo, y_dram, ident,
            next_w1, s_y0, ln0, ln1, s_xn, bias_dram, s_bst, b_bias, s_bias_b):
    with ExitStack() as ctx:
        ctx.enter_context(nc.cleanup_on_exit())
        def sb(n, shape, dt=F32):
            return ctx.enter_context(nc.sbuf_tensor(f"a_{n}", shape, dt))

        def sem(n):
            return nc.alloc_semaphore(name=f"a_{n}")

        w1, w2 = ffn_weights(weights)
        fz, inv = stage_a_tables(tables)
        G = [spectra.raw[:, n * 2 * NP * D:(n + 1) * 2 * NP * D]
             .rearrange("p (q a h d) -> p q a h d", q=NP // 2, a=2, h=2) for n in range(2)]
        ffn = Ffn(nc, ctx, "af", NF, ACT.Silu, w1, w2, b1)
        X = [X0, X1]
        hat = sb("hat", [P, 2, D])
        b2 = sb("b2", [P, D])
        zn = [sb(f"zn{h}", [CTX, D], F32R) for h in "hl"]
        zs = sb("zs", [P, 4, DH])
        pr = [sb(f"pr{h}", [P, NP, D], F32R) for h in "hl"]
        ta = [sb(f"ta{n}", [P, 2, DH]) for n in range(2)]
        tb = [sb(f"tb{n}", [P, 2, DH]) for n in range(2)]
        NG = 6
        GROUP_STEP = [0, 1, 3, 4, 5, 6]
        s_vec = sem("vectors_loaded")
        s_x = [s_x0, sem("x_loaded1")]
        s_zn = sem("zn_loaded")
        s_hat = sem("x_hat_done")
        s_xb = sem("x_bias_added")
        s_z = sem("z_spectrum_done")
        s_zc = sem("z_spectrum_copied")
        s_zu = sem("z_spectrum_used_primed")
        s_pc = sem("product_steps_primed")
        s_phi = sem("product_hi_done")
        s_p = sem("product_split_primed")
        s_i = sem("convolution_done_primed")
        s_r = sem("ffn_output_done")
        s_y = sem("y_done_primed")
        assert nc.sbuf_base <= nc.sbuf_top - 2 * NT * D * 4
        block = ctx.enter_context(nc.Block())
        y_rows = y_dram.rearrange("b (t p) d -> b p t d", p=P)
        x_rows = T["x"].rearrange("b (t p) d -> b p t d", p=P)

        def conv_bank(t):
            return (ffn.up[t] if t < 2 else ffn.side[t - 2])[:, :]

        def next_count(i, par):
            return i + par

        @block.sync
        def _(sp):
            for p in range(2):
                sp.sem_inc(s_ys[p], 16)
            sp.dma_start(b2[:, :], bcast(T["b1b"])).then_inc(s_vec, 16)
            sp.dma_start(zn[0][:, :].bitcast(F32), zhi[0:CTX, :]).then_inc(s_zn, 16)
            sp.dma_start(zn[1][:, :].bitcast(F32), zlo[0:CTX, :]).then_inc(s_zn, 16)
            sp.wait_ge(s_bst[1], 32)
            sp.dma_start(b_bias[:, :], bias_dram[1].rearrange("(f p) -> p f", p=P),
                         allow_slow_non_contiguous=True).then_inc(s_bias_b, 16)

            def body(b, i, par, last):
                if not last:
                    n = next_count(i, par)
                    sp.wait_ge(s_ys[1 - par], 16 * n + 16)
                    sp.dma_start(X[1 - par][:, :, :], x_rows[bass.ds(b + 1, 1)].rearrange("o p t d -> (o p) t d"))\
                      .then_inc(s_x[1 - par], 16)
                    sp.wait_ge(s_z, 2 * b + 2)
                    for h, src in ((0, zhi), (1, zlo)):
                        sp.dma_start(zn[h][:, :].bitcast(F32), src[bass.ds((b + 1) * CTX, CTX), :]).then_inc(s_zn, 16)
                if last:
                    sp.wait_ge(s_pc, 7 * NG * NB + 7)
                    next_w1.load(sp)
                    sp.wait_ge(s_ys[0], 16 * (NB // 2) + 16)
                    sp.dma_start(X[0][:, :, :], y_rows[0]).then_inc(s_y0, 16)
                sp.wait_ge(s_y, NT * b + 2 * NT)
                sp.dma_start(y_rows[bass.ds(b, 1)].rearrange("o p t d -> (o p) t d"), X[par][:, :, :])\
                  .then_inc(s_ys[par], 16)

            pairs_loop(sp, body, NB // 2)

        @block.gpsimd
        def _(pool):
            def add_bias(n, par):
                for t in range(NT):
                    pool.wait_ge(s_hat, NT * n + t + 1)
                    nc.gpsimd.tensor_tensor(X[par][:, t, :], X[par][:, t, :], b2[:, :], ALU.add).then_inc(s_xb, 1)

            pool.wait_ge(s_vec, 16)
            add_bias(0, 0)

            def product_lo(b, g):
                pool.wait_ge(s_phi, NG * b + g + 1)
                half, q = g // 3, g % 3
                dst = (slice(None), slice(2 * q, 2 * q + 2), slice(half * DH, (half + 1) * DH))
                nc.gpsimd.tensor_tensor(pr[1][dst], ta[g % 2][:, :, :], pr[0][dst].bitcast(F32), ALU.subtract)\
                  .then_inc(s_p, 1)

            def body(b, i, par, last):
                product_lo(b, 0)
                if not last:
                    ln0.pool(pool, b + 1, shift=True)
                product_lo(b, 1)
                if not last:
                    ln1.pool_mean(pool, b + 1, s_xn)
                product_lo(b, 2)
                product_lo(b, 3)
                if not last:
                    ln1.pool_rstd(pool, b + 1)
                product_lo(b, 4)
                product_lo(b, 5)
                if not last:
                    add_bias(b + 1, 1 - par)

            pairs_loop(pool, body, NB // 2)

        @block.scalar
        def _(act):
            def squares(n, par, t):
                if t == 0:
                    act.wait_ge(ln1.s_mean, n + 1)
                    act.wait_ge(ffn.s_t, NT * n)
                if t >= 2:
                    act.wait_ge(ln1.s_sq, NT * n + t - 1)
                square(nc, X[par], t, hat[:, t % 2, :], ln1)

            def hat_tile(n, par, t):
                if t == 0:
                    act.wait_ge(ln1.s_rstd, n + 1)
                if t >= 2:
                    act.wait_ge(ffn.s_t, NT * n + t - 1)
                nc.scalar.activation(hat[:, t % 2, :], X[par][:, t, :], ACT.Identity, bias=ln1.shift[:, t:t + 1],
                                     scale=ln1.rstd[:, t:t + 1]).then_inc(s_hat, 1)

            hat_tile(0, 0, 0)
            hat_tile(0, 0, 1)
            ffn.input_hi(act, 0, 0)
            ffn.input_hi(act, 0, 1)
            hat_tile(0, 0, 2)
            hat_tile(0, 0, 3)
            ffn.input_hi(act, 0, 2)
            ffn.input_hi(act, 0, 3)

            def product_hi(b, g):
                act.wait_ge(s_pc, 7 * NG * b + 7 * g + 14)
                if g == 0:
                    act.wait_ge(s_i, NT * b + NT)
                half, q = g // 3, g % 3
                nc.scalar.activation(pr[0][:, 2 * q:2 * q + 2, half * DH:(half + 1) * DH], ta[g % 2][:, :, :],
                                     ACT.Copy).then_inc(s_phi, 1)

            def z_copy(b, half):
                act.wait_ge(s_z, 2 * b + half + 1)
                act.wait_ge(s_zu, 2 * b + half + 1)
                for n in range(2):
                    done = nc.scalar.activation(zs[:, 2 * n:2 * n + 2, :],
                                                ffn.side[n][:, :].rearrange("p (a n) -> p a n", a=2), ACT.Copy)
                done.then_inc(s_zc, 1)

            def body(b, i, par, last):
                for f in range(NF):
                    ffn.activate(act, b, f)
                    if f == 0:
                        z_copy(b, 0)
                    if f == 4:
                        z_copy(b, 1)
                    if f in GROUP_STEP[1:]:
                        product_hi(b, GROUP_STEP.index(f) - 1)
                    if f == 7:
                        product_hi(b, NG - 1)
                    if not last:
                        if f == 3:
                            act.wait_ge(ln0.s_shift, b + 2)
                            for t in range(NT):
                                normalise(nc, X[1 - par], t, ln0, ln1, s_xn)
                        if f == 4:
                            act.wait_ge(s_xn, NT * b + 2 * NT)
                            for t in range(NT):
                                squares(b + 1, 1 - par, t)
                        if f == 6:
                            hat_tile(b + 1, 1 - par, 0)
                            hat_tile(b + 1, 1 - par, 1)
                if not last:
                    ffn.input_hi(act, b + 1, 0)
                    ffn.input_hi(act, b + 1, 1)
                    hat_tile(b + 1, 1 - par, 2)
                    hat_tile(b + 1, 1 - par, 3)
                    ffn.input_hi(act, b + 1, 2)
                    ffn.input_hi(act, b + 1, 3)

            pairs_loop(act, body, NB // 2)

        @block.vector
        def _(dve):
            def norm_a(n, par, count):
                dve.wait_ge(s_x[par], 16 * count)
                ln0.dve(dve, X[par], n)

            def group(b, g):
                half, q = g // 3, g % 3
                c = 7 * NG * b + 7 * g + 7
                if q == 0:
                    dve.wait_ge(s_zc, 2 * b + half + 1)
                dve.wait_ge(s_p, NG * b + g + 1)
                acc = ta[g % 2][:, :, :]

                def multiply(n, out):
                    nc.vector.tensor_tensor(out, G[n % 2][:, q, :, n // 2, half * DH:(half + 1) * DH],
                                            zs[:, n:n + 1, :].broadcast_to([P, 2, DH]), ALU.mult).then_inc(s_pc, 1)

                def add(term):
                    nc.vector.tensor_tensor(acc, acc, term, ALU.add).then_inc(s_pc, 1)

                t0, t1 = tb[g % 2][:, :, :], tb[1 - g % 2][:, :, :]
                multiply(0, acc)
                dve.wait_ge(s_pc, c - 1)
                multiply(1, t0)
                dve.wait_ge(s_pc, c)
                multiply(2, t1)
                dve.wait_ge(s_pc, c + 2)
                add(t0)
                dve.wait_ge(s_pc, c + 4)
                multiply(3, t0)
                add(t1)
                dve.wait_ge(s_pc, c + 6)
                add(t0)
                if q == 2:
                    dve.wait_ge(s_pc, c + 7)
                    dve.sem_inc(s_zu, 1)

            def output(b, par, t):
                dve.wait_ge(s_xb, NT * b + t + 1)
                ffn.output_summed(dve, b, t)
                r = nc.vector.tensor_tensor(X[par][:, t, :], ffn.acc[t][:, :], X[par][:, t, :], ALU.add)
                r.then_inc(s_r, 1)
                dve.wait_ge(s_r, NT * b + t + 1)
                dve.wait_ge(s_i, NT * b + NT + t + 1)
                nc.vector.tensor_tensor(X[par][:, t, :], conv_bank(t), X[par][:, t, :], ALU.mult)\
                  .then_inc(s_y, 1)

            ffn.prime(dve)
            dve.sem_inc(s_zu, 1)
            dve.sem_inc(s_p, 2)
            dve.sem_inc(s_pc, 7)
            dve.sem_inc(s_i, NT)
            dve.sem_inc(s_y, NT)
            dve.wait_ge(s_g2, 96)
            for t in range(NT):
                ffn.input_lo(dve, 0, t)

            def body(b, i, par, last):
                for f in range(NF):
                    ffn.hidden_lo(dve, b, f)
                    if f in GROUP_STEP:
                        group(b, GROUP_STEP.index(f))
                    if not last and f == 2:
                        norm_a(b + 1, 1 - par, next_count(i, par) + 1)
                if not last:
                    for t in range(NT):
                        ffn.input_lo(dve, b + 1, t)
                for t in range(NT):
                    output(b, par, t)
                dve.wait_ge(s_r, NT * b + NT)
                dve.sem_inc(ffn.s_acc, 1)

            pairs_loop(dve, body, NB // 2)

        @block.tensor
        def _(pe):
            def z_spectrum(b, half):
                if half == 0:
                    pe.wait_ge(s_zn, 32 * b + 32)
                    pe.wait_ge(s_y, NT * b + NT)
                else:
                    pe.wait_ge(s_zc, 2 * b + 1)
                cut = slice(half * DH, (half + 1) * DH)
                for n in range(4):
                    m = slice(n * P, (n + 1) * P)
                    last = product(pe, ffn.side[n // 2][:, (n % 2) * DH:(n % 2 + 1) * DH],
                                   [(fz[0][0:CTX, 0, m], fz[1][0:CTX, 0, m], zn[0][:, cut], zn[1][:, cut])])
                last.then_inc(s_z, 1)

            def inverse(b, t):
                if t == 0:
                    pe.wait_ge(s_p, NG * b + NG + 2)
                terms = []
                for n, p in enumerate(PIECES[t]):
                    m = slice((2 * (t % 2) + n) * P, (2 * (t % 2) + n + 1) * P)
                    terms.append((inv[0][:, 0, m], inv[1][:, 0, m], pr[0][:, p, :], pr[1][:, p, :]))
                product(pe, conv_bank(t), terms).then_inc(s_i, 1)

            def transpose(n, t):
                pe.wait_ge(s_hat, NT * n + t + 1)
                ffn.transpose(pe, hat[:, t % 2, :], ident, t)

            for t in range(NT):
                if t >= 2:
                    pe.wait_ge(ffn.s_xT, t - 1)
                transpose(0, t)

            def body(b, i, par, last):
                for f in range(NF):
                    if f < 2:
                        pe.wait_ge(s_y, NT * b + f + 1)
                    ffn.up_product(pe, b, f)
                    if f == 0:
                        z_spectrum(b, 0)
                    if f == 1:
                        z_spectrum(b, 1)
                    if f >= 2:
                        ffn.down_product(pe, b, f - 2)
                pe.wait_ge(s_zc, 2 * b + 2)
                if not last:
                    transpose(b + 1, 0)
                    transpose(b + 1, 1)
                ffn.down_product(pe, b, NF - 2)
                for t in (0, 1):
                    pe.wait_ge(ffn.s_hid, NF * b + NF + 1 + t)
                    inverse(b, t)
                if not last:
                    for t in (2, 3):
                        pe.wait_ge(ffn.s_xT, NT * b + NT + t - 1)
                        transpose(b + 1, t)
                ffn.down_product(pe, b, NF - 1)
                for t in (2, 3):
                    if not last:
                        pe.wait_ge(ffn.s_xT, NT * b + NT + 1 + t)
                    inverse(b, t)

            pairs_loop(pe, body, NB // 2)


class Ranking:

    def __init__(self, nc, sb, sem, scratch, const, rank, score, ident):
        self.nc, self.rank, self.score, self.ident = nc, rank, score, ident
        self.x1, self.xm, self.us = (sb(n, [P, NT, D]) for n in ("x1", "xm", "u"))
        self.base = sb("base", [P, NB * NT])
        self.sc, self.rk = sb("scores", [P, NT]), sb("ranks", [P, NT])
        self.cnt = sb("counts", [P, 2, NT])
        self.row = sb("rows", [P, NT], U32)
        self.ln = LayerNorm(nc, sb, sem, "ln_x1", const)
        self.junk, self.wr = scratch[:, 0:D], scratch[:, D:2 * D]
        self.scb = cut3(scratch, 2 * D, NT, P)
        self.ones = scratch[:, 3 * D:3 * D + P]
        self.tri = scratch[:, 3 * D + P:4 * D + NT * P]
        self.s_x1 = sem("x1_done")
        self.s_xm = sem("x1_normalised")
        self.s_sc = sem("scores_done")
        self.s_scb = sem("scores_spread")
        self.s_st = sem("scores_transposed")
        self.s_cnt = sem("ranks_counted")
        self.s_rk = sem("rank_done")
        self.s_row = sem("row_done")
        self.s_keep = sem("rank_kept")
        self.s_u = sem("u_done")
        self.s_us = sem("u_stored")
        self.s_sct = sem("rows_scattered")
        self.s_go = sem("scatter_started")

    def normalise(self, act, n, first=False):
        act.wait_ge(self.ln.s_shift, n + 1)
        if not first:
            act.wait_ge(self.s_sct, 16 * NT * n)
        for t in range(NT):
            self.nc.scalar.activation(self.xm[:, t, :], self.x1[:, t, :], ACT.Identity,
                                      bias=self.ln.shift[:, t:t + 1], scale=self.ln.rstd[:, t:t + 1])\
                .then_inc(self.s_xm, 1)

    def x1_stats(self, dve, n):
        dve.wait_ge(self.s_x1, NT * n + NT)
        self.ln.dve(dve, self.x1, n)

    def scores(self, dve, n, tiles):
        for t in tiles:
            dve.wait_ge(self.s_xm, NT * n + t + 1)
            self.nc.vector.tensor_tensor_reduce(self.junk, self.xm[:, t, :], self.wr, 1.0, 0.0, ALU.mult, ALU.add,
                                                self.sc[:, t:t + 1]).then_inc(self.s_sc, 1)
            dve.wait_ge(self.s_sc, NT * n + t + 1)
            self.nc.vector.tensor_scalar(self.scb[:, t, :], self.ones, self.sc[:, t:t + 1], None, ALU.mult)\
                .then_inc(self.s_scb, 1)

    def count(self, dve, n, t, spread):
        if t == 0:
            dve.wait_ge(self.s_st, n + 1)
        self.nc.vector.tensor_scalar(self.junk, spread, self.sc[:, t:t + 1], None, ALU.is_gt, ALU.add,
                                     accum_out=self.cnt[:, 0, t:t + 1]).then_inc(self.s_cnt, 1)
        dve.wait_ge(self.s_cnt, 2 * NT * n + 2 * t + 1)
        self.nc.vector.scalar_tensor_tensor(self.junk, spread, self.sc[:, t:t + 1],
                                            self.tri[:, (NT - 1 - t) * P:(NT - 1 - t) * P + S],
                                            ALU.is_equal, ALU.mult, accum_out=self.cnt[:, 1, t:t + 1])\
            .then_inc(self.s_cnt, 1)
        dve.wait_ge(self.s_cnt, 2 * NT * n + 2 * t + 2)

    def ranks(self, dve, n):
        v, at = self.nc.vector, bass.ds(n * NT, NT)
        v.tensor_tensor(self.rk[:, :], self.cnt[:, 0, :], self.cnt[:, 1, :], ALU.add).then_inc(self.s_rk, 1)
        dve.wait_ge(self.s_rk, n + 1)
        v.tensor_tensor(self.row[:, :], self.rk[:, :], self.base[:, at], ALU.add).then_inc(self.s_row, 1)
        v.tensor_copy(self.rank[:, at], self.rk[:, :]).then_inc(self.s_keep, 1)
        v.tensor_copy(self.score[:, at], self.sc[:, :]).then_inc(self.s_keep, 1)
        dve.wait_ge(self.s_keep, 2 * n + 2)

    def post(self, pool, n, first=False):
        if not first:
            pool.wait_ge(self.s_us, 16 * n)
        for t in range(NT):
            pool.wait_ge(self.s_xm, NT * n + t + 1)
            self.nc.gpsimd.tensor_tensor(self.us[:, t, :], self.x1[:, t, :], self.xm[:, t, :], ALU.add)\
                .then_inc(self.s_u, 1)

    def scatter(self, pool, n, xs_dram):
        pool.wait_ge(self.s_row, n + 1)
        pool.sem_inc(self.s_go, 1)
        for t in range(NT):
            pool.indirect_dma_start(xs_dram[:, :], bass.IndirectOffsetOnAxis(ap=self.row[:, t:t + 1], axis=0),
                                    self.xm[:, t, :], None).then_inc(self.s_sct, 16)

    def spread_scores(self, pe, n, side):
        pe.wait_ge(self.s_scb, NT * n + NT)
        for t in range(NT):
            last = pe.transpose(side[:, t * P:(t + 1) * P], self.scb[:, t, :], self.ident)
        last.then_inc(self.s_st, 1)


def stage_b(nc, T, weights, m_w1, b1, cols, s_cols, bias, s_bias, next_w1, Y, s_ys, s_y0, s_sel,
            y_dram, u_dram, xs_dram, ident, const, rk):
    with ExitStack() as ctx:
        ctx.enter_context(nc.cleanup_on_exit())
        def sb(n, shape, dt=F32):
            return ctx.enter_context(nc.sbuf_tensor(f"b_{n}", shape, dt))

        def sem(n):
            return nc.alloc_semaphore(name=f"b_{n}")

        m_w2 = Halves(nc, sem, "w2b", T["W2b"], *weights.halves(0, NF, D), parts=4)
        ffn = Ffn(nc, ctx, "bf", NF, ACT.Silu, (m_w1.hi, m_w1.lo), (m_w2.hi, m_w2.lo), b1)
        X = sb("x", [P, NT, D])
        hat = sb("hat", [P, 2, D])
        b2 = sb("b2", [P, D])
        ln0 = LayerNorm(nc, sb, sem, "bln0", const)
        s_vec = sem("vectors_loaded")
        s_yl = [s_y0, sem("y_loaded1")]
        s_x = sem("x_loaded")
        s_hat = sem("y_hat_done")
        s_yb = sem("y_bias_added")
        s_r = sem("ffn_output_done")
        s_one, s_b1 = sem("ones_done"), sem("bias_done")
        assert nc.sbuf_base <= nc.sbuf_top - 2 * NT * D * 4
        block = ctx.enter_context(nc.Block())
        rows = lambda d: d.rearrange("b (t p) d -> b p t d", p=P)
        one = lambda d, b: rows(d)[bass.ds(b, 1)].rearrange("o p t d -> (o p) t d")

        def loop(eng, body):
            n = NB // 2
            for par in range(2):
                body(par, 0, par, par == 0, False)
            with eng.Fori(1, n - 1) as i:
                for par in range(2):
                    body(2 * i + par, i, par, False, False)
            for par in range(2):
                body(2 * (n - 1) + par, n - 1, par, False, par == 1)

        @block.sync
        def _(sp):
            sp.dma_start(b2[:, :], bcast(T["b2b"])).then_inc(s_vec, 16)
            sp.dma_start(rk.wr, bcast(T["w_router"])).then_inc(s_vec, 16)
            sp.dma_start(rk.tri, T["tri"]).then_inc(s_vec, 16)
            sp.dma_start(rk.base[:, :], T["base_all"]).then_inc(s_vec, 16)
            m_w2.load(sp)
            next_w1.load(sp)

            def body(b, i, par, first, last):
                if not first:
                    sp.wait_ge(rk.s_x1, NT * b)
                sp.dma_start(X[:, :, :], one(T["x"], b)).then_inc(s_x, 16)
                if not last:
                    if not first:
                        sp.wait_ge(s_r, NT * b)
                    if first:
                        sp.wait_ge(s_ys[1], 16 * (NB // 2) + 16)
                    sp.dma_start(Y[1 - par][:, :, :], one(y_dram, b + 1)).then_inc(s_yl[1 - par], 16)
                else:
                    sp.wait_ge(s_r, NT * b)
                    sp.wait_ge(rk.s_sct, 16 * NT * 2)
                    load_routed(sp, xs_dram, Y[0], 0, s_sel)
                if not first:
                    sp.wait_ge(rk.s_u, NT * b)
                    sp.dma_start(one(u_dram, b - 1), rk.us[:, :, :]).then_inc(rk.s_us, 16)

            loop(sp, body)

        @block.gpsimd
        def _(pool):
            def add_bias(n, par):
                for t in range(NT):
                    pool.wait_ge(s_hat, NT * n + t + 1)
                    nc.gpsimd.tensor_tensor(Y[par][:, t, :], Y[par][:, t, :], b2[:, :], ALU.add).then_inc(s_yb, 1)

            ln0.pool(pool, 0, shift=True)
            pool.wait_ge(s_vec, 64)
            add_bias(0, 0)

            def body(b, i, par, first, last):
                if not first:
                    rk.ln.pool(pool, b - 1, shift=True)
                if not last:
                    ln0.pool(pool, b + 1, shift=True)
                if not first:
                    rk.post(pool, b - 1, isinstance(b, int) and b == 1)
                    rk.scatter(pool, b - 1, xs_dram)
                if not last:
                    add_bias(b + 1, 1 - par)

            loop(pool, body)

        @block.scalar
        def _(act):
            def hat_tile(n, par, t):
                if t == 0:
                    act.wait_ge(ln0.s_shift, n + 1)
                    act.wait_ge(s_yl[par], 16)
                if t >= 2:
                    act.wait_ge(ffn.s_t, NT * n + t - 1)
                nc.scalar.activation(hat[:, t % 2, :], Y[par][:, t, :], ACT.Identity, bias=ln0.shift[:, t:t + 1],
                                     scale=ln0.rstd[:, t:t + 1]).then_inc(s_hat, 1)

            act.wait_ge(s_cols, 48)
            for k in range(KC):
                m_w1.split_hi(act, k)
            hat_tile(0, 0, 0)
            hat_tile(0, 0, 1)
            ffn.input_hi(act, 0, 0)
            ffn.input_hi(act, 0, 1)
            hat_tile(0, 0, 2)
            hat_tile(0, 0, 3)
            ffn.input_hi(act, 0, 2)
            ffn.input_hi(act, 0, 3)

            def body(b, i, par, first, last):
                for f in range(NF):
                    if first and f == 0:
                        act.wait_ge(s_b1, 1)
                    ffn.activate(act, b, f)
                    if first:
                        m_w2.split_hi(act, f)
                    if f == 2 and not first:
                        rk.normalise(act, b - 1, isinstance(b, int) and b == 1)
                    if f in (5, 6) and not last:
                        hat_tile(b + 1, 1 - par, f - 5)
                if not last:
                    ffn.input_hi(act, b + 1, 0)
                    ffn.input_hi(act, b + 1, 1)
                    hat_tile(b + 1, 1 - par, 2)
                    hat_tile(b + 1, 1 - par, 3)
                    ffn.input_hi(act, b + 1, 2)
                    ffn.input_hi(act, b + 1, 3)

            loop(act, body)

        @block.vector
        def _(dve):
            def output(b, par, t, first):
                dve.wait_ge(s_yb, NT * b + t + 1)
                if t == 0 and not first:
                    dve.wait_ge(rk.s_u, NT * b)
                ffn.output_summed(dve, b, t)
                nc.vector.tensor_tensor(rk.x1[:, t, :], ffn.acc[t][:, :], Y[par][:, t, :], ALU.add).then_inc(s_r, 1)

            def residual(n):
                dve.wait_ge(s_x, 16 * n + 16)
                dve.wait_ge(s_r, NT * n + NT)
                for t in range(NT):
                    nc.vector.tensor_tensor(rk.x1[:, t, :], rk.x1[:, t, :], X[:, t, :], ALU.add).then_inc(rk.s_x1, 1)

            nc.vector.memset(rk.ones, 1.0).then_inc(s_one, 1)
            dve.wait_ge(s_one, 1)
            dve.wait_ge(s_yl[0], 16)
            ln0.dve(dve, Y[0], 0)
            dve.wait_ge(s_cols, 48)
            dve.wait_ge(s_bias, 16)
            nc.vector.tensor_tensor(b1[:, :], bias[:, :], cols[2][:, :], ALU.add).then_inc(s_b1, 1)
            for k in range(KC):
                m_w1.split_lo(dve, k)
            ffn.prime(dve)
            for t in range(NT):
                ffn.input_lo(dve, 0, t)
            dve.wait_ge(s_vec, 64)

            def body(b, i, par, first, last):
                for f in range(NF):
                    ffn.hidden_lo(dve, b, f)
                    if first:
                        m_w2.split_lo(dve, f)
                    if not first:
                        if f == 0:
                            residual(b - 1)
                        if f == 1:
                            rk.x1_stats(dve, b - 1)
                        if f == 3:
                            rk.scores(dve, b - 1, (0, 1, 2))
                        if f == 4:
                            rk.scores(dve, b - 1, (3,))
                        if f in (5, 6):
                            rk.count(dve, b - 1, 2 * f - 10, ffn.side[0][:, :])
                            rk.count(dve, b - 1, 2 * f - 9, ffn.side[0][:, :])
                        if f == 6:
                            rk.ranks(dve, b - 1)
                    if not last and f == 2:
                        dve.wait_ge(s_yl[1 - par], 16 * (i + par) + 16)
                        ln0.dve(dve, Y[1 - par], b + 1)
                if not last:
                    for t in range(NT):
                        ffn.input_lo(dve, b + 1, t)
                for t in range(NT):
                    output(b, par, t, first)
                dve.wait_ge(s_r, NT * b + NT)
                dve.sem_inc(ffn.s_acc, 1)

            loop(dve, body)
            residual(NB - 1)
            dve.wait_ge(rk.s_x1, NT * NB)

        @block.tensor
        def _(pe):
            def transpose(n, t):
                pe.wait_ge(s_hat, NT * n + t + 1)
                ffn.transpose(pe, hat[:, t % 2, :], ident, t)

            for t in range(NT):
                if t >= 2:
                    pe.wait_ge(ffn.s_xT, t - 1)
                transpose(0, t)
            pe.wait_ge(m_w1.s_lo, KC)

            def body(b, i, par, first, last):
                for f in range(NF):
                    ffn.up_product(pe, b, f)
                    if f == 5 and not first:
                        pe.wait_ge(ffn.s_xT, NT * b + NT)
                        rk.spread_scores(pe, b - 1, ffn.side[0])
                    if f >= 2:
                        if first:
                            pe.wait_ge(m_w2.s_lo, f - 1)
                        ffn.down_product(pe, b, f - 2)
                if not last:
                    if not first:
                        pe.wait_ge(rk.s_cnt, 2 * NT * b)
                    transpose(b + 1, 0)
                    transpose(b + 1, 1)
                if first:
                    pe.wait_ge(m_w2.s_lo, NF)
                ffn.down_product(pe, b, NF - 2)
                if not last:
                    for t in (2, 3):
                        pe.wait_ge(ffn.s_xT, NT * b + NT + t - 1)
                        transpose(b + 1, t)
                ffn.down_product(pe, b, NF - 1)

            loop(pe, body)


def load_routed(sp, xs_dram, sel, q, s_sel):
    rows = xs_dram.rearrange("(b r) d -> b r d", b=NB)[:, 0:TOP, :].rearrange("(q e) (h p) d -> q p e h d", e=2, p=P)
    for e in range(2):
        src = rows[bass.ds(q, 1), :, e].rearrange("o p h d -> (o p) h d")
        sp.dma_start(sel[:, 2 * e:2 * e + 2, :], src).then_inc(s_sel, 16)


def stage_c(nc, T, weights, spectra, m_w1, sel, s_sel, u_dram, xs_dram, upd_dram, out, ident, rk):
    with ExitStack() as ctx:
        ctx.enter_context(nc.cleanup_on_exit())
        def sb(n, shape, dt=F32):
            return ctx.enter_context(nc.sbuf_tensor(f"c_{n}", shape, dt))

        def sem(n):
            return nc.alloc_semaphore(name=f"c_{n}")

        w1 = [cut3(spectra.split, 0, KC, FM), cut3(weights.split, KC * FM, KC, FM)]
        w2 = [sb("w2h", [P, NFM, D], F32R), cut3(weights.split, 0, NFM, D)]
        m_w2 = Halves(nc, sem, "w2", T["W2"], *w2, cut3(weights.raw, 0, NFM, D), parts=8)
        b1 = sb("b1", [P, NFM])
        ffn = Ffn(nc, ctx, "cf", NFM, ACT.Gelu_apprx_tanh, w1, w2, b1)
        upd = rk.xm
        gat = [rk.x1, cut3(spectra.raw, KC * FM, NT, D)]
        us = [rk.us, cut3(spectra.raw, KC * FM + NT * D, NT, D)]
        b2 = sb("b2", [P, D])
        NC = NB * NT
        weight = sb("weight", [P, NC])
        cbase = sb("cbase", [P, NC])
        issel = sb("issel", [P, NC])
        t1 = sb("t1", [P, NC])
        t2 = sb("t2", [P, NC])
        idx = sb("idx", [P, NC], U32)
        idxb = sb("idxb", [P, 2 * NT], U32)
        wtb = sb("wtb", [P, 2 * NT])
        zrow = sb("zrow", [1, D])
        NPAIR = NB // 2
        s_vec, s_idx, s_wt, s_zr, s_zs = (sem("vectors_loaded"), sem("index_steps"), sem("weights_done"),
                                          sem("zero_row_done"), sem("zero_row_stored"))
        s_u = sem("update_done")
        s_us = sem("update_stored")
        s_ul = [sem(f"u_loaded{e}") for e in range(2)]
        s_gat = [sem(f"update_gathered{e}") for e in range(2)]
        s_go = sem("gather_started")
        s_ix = sem("indices_picked")
        s_o = sem("output_done")
        s_os = [sem(f"output_stored{e}") for e in range(2)]
        assert nc.sbuf_base <= nc.sbuf_top - 1 * NT * D * 4
        block = ctx.enter_context(nc.Block())
        rows = lambda d: d.rearrange("b (t p) d -> b p t d", p=P)
        one = lambda d, b: rows(d)[bass.ds(b, 1)].rearrange("o p t d -> (o p) t d")
        upd_rows = upd_dram[0:2 * TOP, :].rearrange("(t p) d -> p t d", p=P)

        def loop(eng, body):
            body(0, True, False)
            with eng.Fori(1, NPAIR - 1) as q:
                body(q, False, False)
            body(NPAIR - 1, False, True)

        @block.sync
        def _(sp):
            sp.dma_start(b1[:, :], T["b1"]).then_inc(s_vec, 16)
            sp.dma_start(b2[:, :], bcast(T["b2"])).then_inc(s_vec, 16)
            sp.dma_start(cbase[:, :], T["base_sel"]).then_inc(s_vec, 16)
            sp.wait_ge(s_zr, 1)
            sp.dma_start(upd_dram[2 * TOP:2 * TOP + 1, :], zrow[:, :]).then_inc(s_zs, 16)

            def load_u(p, e, first):
                if not first:
                    sp.wait_ge(s_os[e], 16 * p)
                sp.dma_start(us[e][:, :, :], one(u_dram, 2 * p + e)).then_inc(s_ul[e], 16)

            def store(p, e):
                sp.wait_ge(s_o, 2 * NT * p + NT * (e + 1))
                sp.dma_start(one(out, 2 * p + e), us[e][:, :, :]).then_inc(s_os[e], 16)

            sp.wait_ge(rk.s_sct, 16 * NT * (NB - 1))
            m_w2.load(sp)

            def body(q, first, last):
                if not last:
                    sp.wait_ge(ffn.s_t, NT * q + NT)
                    load_routed(sp, xs_dram, sel, q + 1, s_sel)
                if first:
                    sp.wait_ge(rk.s_u, NT * NB)
                    sp.dma_start(one(u_dram, NB - 1), rk.us[:, :, :]).then_inc(rk.s_us, 16)
                else:
                    for e in range(2):
                        load_u(q - 1, e, isinstance(q, int) and q == 1)
                    for e in range(2):
                        store(q - 1, e)
                if last:
                    for e in range(2):
                        load_u(q, e, False)
                    for t in range(NT):
                        sp.wait_ge(s_u, NT * q + t + 1)
                        sp.dma_start(upd_rows[:, t, :], upd[:, t, :]).then_inc(s_us, 16)
                else:
                    sp.wait_ge(s_u, NT * q + NT)
                    sp.dma_start(upd_rows, upd[:, :, :]).then_inc(s_us, 16)
                if first:
                    sp.wait_ge(rk.s_us, 16 * NB)
                    sp.wait_ge(rk.s_sct, 16 * NT * NB)
                    sp.wait_ge(rk.s_row, NB)

            loop(sp, body)
            for e in range(2):
                b = NB - 2 + e
                for h in range(2):
                    sp.wait_ge(s_o, NT * b + 2 * h + 2)
                    cut = slice(2 * h, 2 * h + 2)
                    sp.dma_start(rows(out)[b, :, cut, :], us[e][:, cut, :]).then_inc(s_os[e], 16)
            for e in range(2):
                sp.wait_ge(s_os[e], 16 * (NPAIR + 1))

        @block.gpsimd
        def _(pool):
            rk.ln.pool(pool, NB - 1, shift=True)
            rk.post(pool, NB - 1)
            rk.scatter(pool, NB - 1, xs_dram)
            pool.wait_ge(rk.s_u, NT * NB)
            pool.wait_ge(s_zs, 16)

            def gather(p, first, last):
                pool.wait_ge(s_us, 16 * p + (16 * NT if last else 16))
                pool.wait_ge(s_ix, 2 * p + 2)
                if not first:
                    pool.wait_ge(s_o, 2 * NT * p)
                pool.sem_inc(s_go, 1)
                for e in range(2):
                    for t in range(NT):
                        at = e * NT + t
                        pool.indirect_dma_start(gat[e][:, t, :], None, upd_dram[:, :],
                                                bass.IndirectOffsetOnAxis(ap=idxb[:, at:at + 1], axis=0))\
                            .then_inc(s_gat[e], 16)

            def body(q, first, last):
                if not first:
                    gather(q - 1, isinstance(q, int) and q == 1, False)

            loop(pool, body)
            gather(NPAIR - 1, False, True)

        @block.scalar
        def _(act):
            m_w1.split_hi(act, 0)
            for t in range(NT):
                ffn.input_hi(act, 0, t)
            act.wait_ge(s_vec, 48)

            def body(q, first, last):
                for f in range(NFM):
                    if first and f + 1 < m_w1.K:
                        m_w1.split_hi(act, f + 1)
                    ffn.activate(act, q, f)
                    if first:
                        m_w2.split_hi(act, f)
                        if f == 6:
                            rk.normalise(act, NB - 1)
                        if f == 13:
                            act.wait_ge(rk.s_keep, 2 * NB)
                            nc.scalar.activation(weight[:, :], rk.score[:, :], ACT.Sigmoid).then_inc(s_wt, 1)
                if not last:
                    for t in range(NT):
                        ffn.input_hi(act, q + 1, t)

            loop(act, body)

        @block.vector
        def _(dve):
            ffn.prime(dve)
            nc.vector.memset(zrow[:, :], 0.0).then_inc(s_zr, 1)
            m_w1.split_lo(dve, 0)
            dve.wait_ge(s_vec, 48)
            for t in range(NT):
                ffn.input_lo(dve, 0, t)

            def indices():
                nc.vector.tensor_scalar(issel[:, :], rk.rank[:, :], float(TOP), None, ALU.is_lt).then_inc(s_idx, 1)
                nc.vector.tensor_tensor(t1[:, :], rk.rank[:, :], cbase[:, :], ALU.add).then_inc(s_idx, 1)
                dve.wait_ge(s_idx, 2)
                nc.vector.tensor_tensor(t2[:, :], t1[:, :], issel[:, :], ALU.mult).then_inc(s_idx, 1)
                dve.wait_ge(s_idx, 3)
                nc.vector.tensor_scalar(idx[:, :], t2[:, :], float(2 * TOP), None, ALU.add).then_inc(s_idx, 1)

            def pick(p, first):
                if first:
                    dve.wait_ge(s_idx, 4)
                    dve.wait_ge(s_wt, 1)
                else:
                    dve.wait_ge(s_gat[1], 16 * NT * p)
                    dve.wait_ge(s_o, 2 * NT * p)
                at = bass.ds(2 * NT * p, 2 * NT)
                nc.vector.tensor_copy(idxb[:, :], idx[:, at]).then_inc(s_ix, 1)
                nc.vector.tensor_copy(wtb[:, :], weight[:, at]).then_inc(s_ix, 1)

            def finish(p, e):
                dve.wait_ge(s_ix, 2 * p + 2)
                dve.wait_ge(s_gat[e], 16 * NT * p + 16 * NT)
                dve.wait_ge(s_ul[e], 16 * p + 16)
                for t in range(NT):
                    at = e * NT + t
                    nc.vector.scalar_tensor_tensor(us[e][:, t, :], gat[e][:, t, :], wtb[:, at:at + 1],
                                                   us[e][:, t, :], ALU.mult, ALU.add).then_inc(s_o, 1)

            def body(q, first, last):
                for f in range(NFM):
                    if not first:
                        if f == 0:
                            pick(q - 1, isinstance(q, int) and q == 1)
                        if f in (5, 8):
                            finish(q - 1, int(f == 8))
                    if first and f + 1 < m_w1.K:
                        m_w1.split_lo(dve, f + 1)
                    ffn.hidden_lo(dve, q, f)
                    if first:
                        m_w2.split_lo(dve, f)
                        if f == 4:
                            rk.x1_stats(dve, NB - 1)
                        if f in (7, 8):
                            rk.scores(dve, NB - 1, (2 * f - 14, 2 * f - 13))
                        if f in (10, 11):
                            rk.count(dve, NB - 1, 2 * f - 20, ffn.side[0][:, :])
                            rk.count(dve, NB - 1, 2 * f - 19, ffn.side[0][:, :])
                        if f == 11:
                            rk.ranks(dve, NB - 1)
                            indices()
                if not last:
                    for t in range(NT):
                        ffn.input_lo(dve, q + 1, t)
                if first:
                    dve.wait_ge(rk.s_u, NT * NB)
                    dve.wait_ge(rk.s_sct, 16 * NT * NB)
                else:
                    dve.wait_ge(s_us, 16 * q)
                for t in range(NT):
                    ffn.output_summed(dve, q, t)
                    nc.vector.tensor_tensor(upd[:, t, :], ffn.acc[t][:, :], b2[:, :], ALU.add).then_inc(s_u, 1)
                dve.wait_ge(s_u, NT * q + NT)
                dve.sem_inc(ffn.s_acc, 1)

            loop(dve, body)
            pick(NPAIR - 1, False)
            for e in range(2):
                finish(NPAIR - 1, e)

        @block.tensor
        def _(pe):
            def transpose(n, t):
                if t == 0:
                    pe.wait_ge(s_sel, 32 * n + 32)
                ffn.transpose(pe, sel[:, t, :], ident, t)

            for t in range(NT):
                if t >= 2:
                    pe.wait_ge(ffn.s_xT, t - 1)
                transpose(0, t)

            def body(q, first, last):
                for f in range(NFM):
                    if first and f % 4 == 0:
                        pe.wait_ge(m_w1.s_lo, f // 4 + 1)
                    ffn.up_product(pe, q, f)
                    if first and f == 9:
                        pe.wait_ge(ffn.s_xT, NT)
                        rk.spread_scores(pe, NB - 1, ffn.side[0])
                    if f >= 2:
                        if first:
                            pe.wait_ge(m_w2.s_lo, f - 1)
                        ffn.down_product(pe, q, f - 2)
                if first:
                    pe.wait_ge(rk.s_cnt, 2 * NT * NB)
                if not last:
                    transpose(q + 1, 0)
                    transpose(q + 1, 1)
                if first:
                    pe.wait_ge(m_w2.s_lo, NFM)
                ffn.down_product(pe, q, NFM - 2)
                if not last:
                    for t in (2, 3):
                        pe.wait_ge(ffn.s_xT, NT * q + NT + t - 1)
                        transpose(q + 1, t)
                ffn.down_product(pe, q, NFM - 1)

            loop(pe, body)


def program(nc, T, out):
    gpad = nc.dram_tensor("gpad", [GROWS, D], F32, kind="Internal").ap()
    zhi = nc.dram_tensor("zhi", [ZROWS, D], F32, kind="Internal").ap()
    zlo = nc.dram_tensor("zlo", [ZROWS, D], F32, kind="Internal").ap()
    y_dram = nc.dram_tensor("y_mid", [NB, S, D], F32, kind="Internal").ap()
    u_dram = nc.dram_tensor("u_mid", [NB, S, D], F32, kind="Internal").ap()
    xs_dram = nc.dram_tensor("rows_by_rank", [NB * S, D], F32, kind="Internal").ap()
    bias_dram = nc.dram_tensor("biases", [2, F], F32, kind="Internal").ap()
    upd_dram = nc.dram_tensor("updates", [2 * TOP + 1, D], F32, kind="Internal").ap()
    with ExitStack() as ctx:
        def sb(n, shape, dt=F32):
            return ctx.enter_context(nc.sbuf_tensor(n, shape, dt))

        ident = sb("ident", [P, P])
        values = (-0.5, EPS, 0.0, -1.0 / D, 1.0 / D)
        const = sb("constants", [P, len(values), NT])
        with nc.semaphore("ident_loaded") as s_id, nc.semaphore("const_done") as s_c, nc.Block() as block:
            @block.sync
            def _(sp):
                sp.dma_start(ident[:, :], T["ident"]).then_inc(s_id, 16)
                sp.wait_ge(s_id, 16)

            @block.vector
            def _(dve):
                for k, v in enumerate(values):
                    nc.vector.memset(const[:, k, :], v).then_inc(s_c, 1)
                dve.wait_ge(s_c, len(values))
        def sem(n):
            return ctx.enter_context(nc.semaphore(n))

        half = 2 * KC * F
        weights = Place(nc, ctx, "weights", 2 * half)
        spectra = Place(nc, ctx, "spectra", 2 * 2 * NP * D)
        b_cols = [sb(f"b_{n}", [P, w]) for n, w in (("g2", KC), ("be2", KC), ("b2a", NF))]
        b_b1, b_bias = sb("b_b1", [P, NF]), sb("b_bias", [P, NF])
        s_bst, s_bias_b = [sem(f"bias_stored{c}") for c in range(2)], sem("b_bias_loaded")
        s_cols = sem("b_columns_loaded")
        top = nc.sbuf_top
        X = [nc.alloc_sbuf_tensor_at(f"tokens{p}", [P, NT, D], F32, offset=top - (p + 1) * NT * D * 4)
             for p in range(2)]
        s_ys = [sem(f"y_stored_primed{p}") for p in range(2)]
        s_y0, s_sel = sem("first_y_loaded"), sem("routed_rows_loaded")
        b_w1 = Halves(nc, sem, "w2a", T["W2a"], *spectra.halves(0, KC, F), scale=b_cols[0])
        by_columns = [cut3(t, at, KC, FM).rearrange("p k (c n) -> p c k n", c=4)
                      for t, at in ((spectra.split, 0), (weights.split, half), (weights.raw, half))]
        c_w1 = Halves(nc, sem, "w1", T["W1"].rearrange("(k p) (c n) -> p c k n", p=P, c=4), *by_columns, parts=4)
        with ExitStack() as actx:
            def asb(n, shape, dt=F32):
                return actx.enter_context(nc.sbuf_tensor(n, shape, dt))

            tables = Place(nc, actx, "tables", 4 * 4 * P)
            b1 = asb("a_b1", [P, NF])
            s_x0, s_g2 = sem("first_x_loaded"), sem("g2_done")
            ln0 = LayerNorm(nc, asb, sem, "ln0", const)
            ln1 = SecondLayerNorm(nc, asb, sem, "ln1", const)
            s_xn = sem("x_normalised")
            setup(nc, T, weights, spectra, tables, b1, zhi, zlo, gpad, const, s_g2, X[0], s_x0,
                  b_cols, s_cols, ln0, ln1, s_xn, bias_dram, s_bst)
            stage_a(nc, T, weights, spectra, tables, b1, s_g2, X[0], s_x0, X[1], s_ys, zhi, zlo, y_dram,
                    ident[:, :], b_w1, s_y0, ln0, ln1, s_xn, bias_dram, s_bst, b_bias, s_bias_b)
        rank = sb("rank", [P, NB * NT])
        score = sb("score", [P, NB * NT])
        scratch = spectra.raw[:, KC * FM:]
        rk = Ranking(nc, lambda n, shape, dt=F32: sb(f"rk_{n}", shape, dt), lambda n: sem(f"rk_{n}"), scratch, const,
                     rank, score, ident[:, :])
        stage_b(nc, T, weights, b_w1, b_b1, b_cols, s_cols, b_bias, s_bias_b, c_w1, X, s_ys, s_y0, s_sel,
                y_dram, u_dram, xs_dram, ident[:, :], const, rk)
        stage_c(nc, T, weights, spectra, c_w1, X[0], s_sel, u_dram, xs_dram, upd_dram, out, ident[:, :], rk)


_INS = {'x': 'x', 'ctx_1024': 'ctxT', 'L0_xattn_pe': 'peT', 'L0_xattn_W_in': 'W_in', 'L0_xattn_b_in': 'b_in',
        'L0_xattn_g_ln': 'g_ln', 'L0_xattn_beta_ln': 'beta_ln', 'L0_xattn_Wp1': 'Wp1', 'L0_xattn_bp1': 'bp1',
        'L0_xattn_Wp2': 'Wp2', 'L0_xattn_bp2': 'bp2', 'L0_xattn_a': 'a', 'L0_xattn_g1': 'g1',
        'L0_xattn_be1': 'be1', 'L0_xattn_W1a': 'W1a', 'L0_xattn_b1a': 'b1a', 'L0_xattn_W1b': 'W1b',
        'L0_xattn_b1b': 'b1b', 'L0_xattn_g2': 'g2', 'L0_xattn_be2': 'be2', 'L0_xattn_W2a': 'W2a',
        'L0_xattn_b2a': 'b2a', 'L0_xattn_W2b': 'W2b', 'L0_xattn_b2b': 'b2b', 'L0_ffn_w_router': 'w_router',
        'L0_ffn_W1': 'W1', 'L0_ffn_b1': 'b1', 'L0_ffn_W2': 'W2', 'L0_ffn_b2': 'b2'}


_COLUMNS = ("bp1", "g1", "be1", "b1a", "g2", "be2", "b2a", "b1")


def _constants(np):
    k, n = np.arange(64), np.arange(P)
    angle = np.pi * np.outer(n, 2 * k + 1) / P
    cos, sin = np.cos(angle), np.sin(angle)
    c = {"dft_g": np.concatenate([cos, -sin], 1)}
    fz = np.zeros((P, 4, P))
    for ph in range(2):
        rows = np.arange(ph, CTX, 2)
        j = np.arange(len(rows))
        fz[rows, 2 * ph] = np.concatenate([cos[j], cos[j]], 1)
        fz[rows, 2 * ph + 1] = np.concatenate([sin[j], -sin[j]], 1)
    c["dft_z"] = fz.reshape(P, 4 * P)
    inv = np.zeros((P, 4, P))
    for t in range(2):
        for m, p in enumerate(PIECES[t]):
            end = EDGES[p + 1]
            for col in range(P):
                u = t * P + col
                if EDGES[p] <= u < end:
                    at = u - EDGES[p] + HALO
                    inv[:64, 2 * t + m, col] = cos[at] / 64
                    inv[64:, 2 * t + m, col] = -sin[at] / 64
    c["dft_inv"] = inv.reshape(P, 4 * P)
    c["negl"] = -(np.arange(L // P)[None, :] * P + n[:, None])
    c["ident"] = np.eye(P)
    c["tri"] = (np.arange((NT - 1) * P + S)[None, :] < (NT - 1) * P + n[:, None])
    b = np.repeat(np.arange(NB), NT)[None, :]
    c["base_all"] = np.repeat(b * S, P, 0)
    c["base_sel"] = np.repeat((b % 2) * TOP - 2 * TOP, P, 0)
    return {name: np.ascontiguousarray(v, dtype=np.float32) for name, v in c.items()}


def kernel(**inputs):
    import numpy as _np
    import concourse.bacc as _bacc
    from concourse import mybir as _mybir
    from concourse.bass_utils import run_bass_kernel_spmd as _run

    nc = _bacc.Bacc("TRN2", target_bir_lowering=False, num_devices=1)
    arrays, T = {}, {}
    for name, short in _INS.items():
        a = _np.asarray(inputs[name])
        if short == "ctxT":
            a = a.reshape(ZROWS, D).T
        if short == "peT":
            a = a.T
        if short in _COLUMNS:
            a = a.reshape(-1, P).T
        arrays[f"in_{short}"] = _np.ascontiguousarray(a)
    for short, a in _constants(_np).items():
        arrays[f"in_{short}"] = a
    for full, a in arrays.items():
        T[full[3:]] = nc.dram_tensor(full, a.shape, _mybir.dt.from_np(a.dtype), kind="ExternalInput").ap()
    out = nc.dram_tensor("out_0", (NB, S, D), _mybir.dt.float32, kind="ExternalOutput").ap()
    program(nc, T, out)
    r = _run(nc, [arrays], core_ids=[0])
    return r.results[0]["out_0"]
```
